# Optimizing a Trainium2 kernel written in Bass

```python
import numpy as np
import jax
import jax.numpy as jnp

def _softmax(x, axis=-1):
    return jax.nn.softmax(x, axis=axis)

def _gelu(x):
    return jax.nn.gelu(x, approximate=True)

def _silu(x):
    return jax.nn.silu(x)

def _sigmoid(x):
    return jax.nn.sigmoid(x)

def _layernorm(x, axis=-1, eps=1e-05):
    m = jnp.mean(x, axis=axis, keepdims=True)
    v = jnp.var(x, axis=axis, keepdims=True)
    return (x - m) / jnp.sqrt(v + eps)

def _scatter_add(tgt, idx, src, axis=0):
    return tgt.at[idx].add(src)

def _segment_sum(src, seg, n):
    return jax.ops.segment_sum(src, seg, n)
kernel_name = 'mk_gnn_resnorm_d4_gnn_r8_95ef42'

def setup_inputs(seed: int=0):
    np.random.seed(seed)
    _w = jnp.asarray

    def _rec_inputs():
        import jax
        import jax.numpy as jnp
        _gk = jax.random.key(seed)
        x = -1.857e-05 + 0.05 * jax.random.normal(jax.random.fold_in(_gk, 1), (12500, 128), jnp.float32)
        src = jax.random.randint(jax.random.fold_in(_gk, 2), (200000,), 0, 12500, jnp.int32)
        dst = jnp.minimum((12500 * jax.random.uniform(jax.random.fold_in(_gk, 3), (200000,)) ** 2.0).astype(jnp.int32), 99999)
        _o = jnp.argsort(dst, stable=True)
        src = src[_o]
        dst = dst[_o]
        edge_weight = jax.random.uniform(jax.random.fold_in(_gk, 13), (200000,), jnp.float32, 0.0, 0.999999)
        return (x, src, dst, edge_weight)
    x, src, dst, edge_weight = _rec_inputs()

    def _L0_gnn_setup():
        import jax, jax.numpy as jnp
        import numpy as np
        C = 1.0
        N_NODES = 12500
        N_EDGES = 75000
        D = 128
        EPS = 1e-15
        DEN_EPS = 1e-10

        def _artanh(x):
            return jnp.arctanh(jnp.clip(x, -1.0 + 1e-07, 1.0 - 1e-07))

        def _safe_norm(v):
            return jnp.clip(jnp.linalg.norm(v, axis=-1, keepdims=True), EPS)

        def expmap0(u, c):
            sc = jnp.sqrt(c)
            un = _safe_norm(u)
            return jnp.tanh(sc * un) * u / (sc * un)

        def logmap0(p, c):
            sc = jnp.sqrt(c)
            pn = _safe_norm(p)
            return _artanh(sc * pn) * p / (sc * pn)

        def mobius_scalar_mul(r, v, c):
            sc = jnp.sqrt(c)
            vn = _safe_norm(v)
            return jnp.tanh(r * _artanh(sc * vn)) * v / (sc * vn)

        def weighted_midpoint_spmm(x_hyp, c, rows, cols, vals):
            gamma = 2.0 / jnp.clip(1.0 - c * jnp.sum(x_hyp * x_hyp, axis=-1, keepdims=True), EPS)
            gx = gamma * x_hyp
            num = jax.ops.segment_sum(vals[:, None] * gx[cols], rows, num_segments=N_NODES)
            den = jax.ops.segment_sum(vals * (gamma[:, 0] - 1.0)[cols], rows, num_segments=N_NODES)[:, None]
            sign = jnp.where(den >= 0, 1.0, -1.0)
            den = sign * jnp.clip(jnp.abs(den), DEN_EPS)
            two_mean = num / den
            return mobius_scalar_mul(0.5, two_mean, c)
        key = jax.random.key(seed)
        k1, k2, k3, k4 = jax.random.split(key, 4)
        x = jax.random.normal(k1, (N_NODES, D), dtype=jnp.float32) * 0.05
        rows = jnp.sort(jax.random.randint(k2, (N_EDGES,), 0, N_NODES, dtype=jnp.int32))
        cols = jax.random.randint(k3, (N_EDGES,), 0, N_NODES, dtype=jnp.int32)
        vals = jax.random.uniform(k4, (N_EDGES,), dtype=jnp.float32)
        return {'x': x, 'rows': rows, 'cols': cols, 'vals': vals}
    _L0_gnn_all = _L0_gnn_setup()
    _L0_gnn_in = {k: v for k, v in _L0_gnn_all.items() if k in ()}
    del _L0_gnn_all

    def _L1_gnn_setup():
        import jax, jax.numpy as jnp
        import numpy as np
        N_NODES = 6250
        N_EDGES = 62500
        D_MODEL = 128
        D_INNER = 256
        N_EXPERT = 64
        TOP_K = 2
        CAP_FACTOR = 2
        BN_EPS = 1e-05

        def _gcn_conv(feats, edge_src, edge_dst, W_conv, b_conv):
            n = feats.shape[0]
            ones = jnp.ones_like(edge_dst, dtype=feats.dtype)
            deg = jax.ops.segment_sum(ones, edge_dst, num_segments=n)
            deg = jnp.maximum(deg, 1.0)
            inv_sqrt = jax.lax.rsqrt(deg)
            norm = inv_sqrt[edge_src] * inv_sqrt[edge_dst]
            msgs = feats[edge_src] * norm[:, None]
            agg = jax.ops.segment_sum(msgs, edge_dst, num_segments=n)
            return agg @ W_conv + b_conv

        def _moe_ffn(x, gate_W, gate_b, W1, b1, W2, b2):
            T, d = x.shape
            E, h = (W1.shape[0], W1.shape[2])
            scores = x @ gate_W + gate_b
            topv, topi = jax.lax.top_k(scores, TOP_K)
            gw = jax.nn.softmax(topv, axis=-1)
            P = T * TOP_K
            eid = topi.reshape(P)
            x_rep = jnp.repeat(x, TOP_K, axis=0)
            onehot = jax.nn.one_hot(eid, E, dtype=jnp.int32)
            pos = jnp.sum(jnp.cumsum(onehot, axis=0) * onehot, axis=-1) - 1
            C = CAP_FACTOR * int(np.ceil(P / E))
            valid = pos < C
            slot = eid * C + jnp.where(valid, pos, 0)
            buf = jnp.zeros((E * C, d), x.dtype).at[slot].add(jnp.where(valid[:, None], x_rep, 0.0))
            buf = buf.reshape(E, C, d)
            hact = jax.nn.gelu(jnp.einsum('ecd,edh->ech', buf, W1) + b1[:, None, :], approximate=False)
            y = jnp.einsum('ech,ehd->ecd', hact, W2) + b2[:, None, :]
            y_pairs = y.reshape(E * C, d)[slot] * valid[:, None].astype(x.dtype)
            y_pairs = y_pairs.reshape(T, TOP_K, d)
            return jnp.einsum('tk,tkd->td', gw, y_pairs)

        def _batchnorm(x, gamma, beta):
            mean = jnp.mean(x, axis=0)
            var = jnp.mean(jnp.square(x - mean), axis=0)
            return (x - mean) * jax.lax.rsqrt(var + BN_EPS) * gamma + beta
        key = jax.random.key(seed)
        ks = jax.random.split(key, 12)
        d, h, E = (D_MODEL, D_INNER, N_EXPERT)
        return {'feats': jax.random.normal(ks[0], (N_NODES, d), jnp.float32), 'edge_src': jax.random.randint(ks[1], (N_EDGES,), 0, N_NODES), 'edge_dst': jax.random.randint(ks[2], (N_EDGES,), 0, N_NODES), 'W_conv': jax.random.normal(ks[3], (d, d), jnp.float32) / np.sqrt(d), 'b_conv': jnp.zeros((d,), jnp.float32), 'gate_W': jax.random.normal(ks[4], (d, E), jnp.float32) / np.sqrt(d), 'gate_b': jnp.zeros((E,), jnp.float32), 'W1': jax.random.normal(ks[5], (E, d, h), jnp.float32) / np.sqrt(d), 'b1': jnp.zeros((E, h), jnp.float32), 'W2': jax.random.normal(ks[6], (E, h, d), jnp.float32) / np.sqrt(h), 'b2': jnp.zeros((E, d), jnp.float32), 'bn_gamma': jnp.ones((d,), jnp.float32), 'bn_beta': jnp.zeros((d,), jnp.float32)}
    _L1_gnn_all = _L1_gnn_setup()
    _L1_gnn_in = {k: v for k, v in _L1_gnn_all.items() if k in ('W_conv', 'b_conv', 'gate_W', 'gate_b', 'W1', 'b1', 'W2', 'b2', 'bn_gamma', 'bn_beta')}
    del _L1_gnn_all

    def _L2_gnn_setup():
        import jax, jax.numpy as jnp
        import numpy as np
        key = jax.random.key(seed)
        k1, k2, k3 = jax.random.split(key, 3)
        N, E, D = (6250, 75000, 128)
        x = jax.random.normal(k1, (N, D), dtype=jnp.float32)
        src = jax.random.randint(k2, (E,), 0, N, dtype=jnp.int64)
        dst = jax.random.randint(k3, (E,), 0, N, dtype=jnp.int64)
        return {'x': x, 'src': src, 'dst': dst}
    _L2_gnn_all = _L2_gnn_setup()
    _L2_gnn_in = {k: v for k, v in _L2_gnn_all.items() if k in ()}
    del _L2_gnn_all

    def _L3_gnn_setup():
        import jax, jax.numpy as jnp
        import numpy as np
        N_NODES = 6250
        N_EDGES = 100000
        D_IN = 128
        D_OUT = 128
        key = jax.random.key(seed)
        ks = jax.random.split(key, 8)
        x = jax.random.normal(ks[0], (N_NODES, D_IN), dtype=jnp.float32)
        edge_index = jax.random.randint(ks[1], (2, N_EDGES), 0, N_NODES, dtype=jnp.int64)
        s = 1.0 / np.sqrt(D_IN)
        so = 1.0 / np.sqrt(D_OUT)
        W1 = jax.random.uniform(ks[2], (D_IN, D_OUT), jnp.float32, -s, s)
        b1 = jax.random.uniform(ks[3], (D_OUT,), jnp.float32, -s, s)
        W2 = jax.random.uniform(ks[4], (D_OUT, D_OUT), jnp.float32, -so, so)
        b2 = jax.random.uniform(ks[5], (D_OUT,), jnp.float32, -so, so)
        Wres = jax.random.uniform(ks[6], (D_IN, D_OUT), jnp.float32, -s, s)
        bres = jax.random.uniform(ks[7], (D_OUT,), jnp.float32, -s, s)
        return {'x': x, 'edge_index': edge_index, 'W1': W1, 'b1': b1, 'W2': W2, 'b2': b2, 'Wres': Wres, 'bres': bres}
    _L3_gnn_all = _L3_gnn_setup()
    _L3_gnn_in = {k: v for k, v in _L3_gnn_all.items() if k in ('W1', 'b1', 'W2', 'b2', 'Wres', 'bres')}
    del _L3_gnn_all
    return {'x': x, 'src': src, 'dst': dst, 'edge_weight': edge_weight, 'L1_gnn_W_conv': _L1_gnn_in['W_conv'], 'L1_gnn_b_conv': _L1_gnn_in['b_conv'], 'L1_gnn_gate_W': _L1_gnn_in['gate_W'], 'L1_gnn_gate_b': _L1_gnn_in['gate_b'], 'L1_gnn_W1': _L1_gnn_in['W1'], 'L1_gnn_b1': _L1_gnn_in['b1'], 'L1_gnn_W2': _L1_gnn_in['W2'], 'L1_gnn_b2': _L1_gnn_in['b2'], 'L1_gnn_bn_gamma': _L1_gnn_in['bn_gamma'], 'L1_gnn_bn_beta': _L1_gnn_in['bn_beta'], 'L3_gnn_W1': _L3_gnn_in['W1'], 'L3_gnn_b1': _L3_gnn_in['b1'], 'L3_gnn_W2': _L3_gnn_in['W2'], 'L3_gnn_b2': _L3_gnn_in['b2'], 'L3_gnn_Wres': _L3_gnn_in['Wres'], 'L3_gnn_bres': _L3_gnn_in['bres']}

def reference(x, src, dst, edge_weight, L1_gnn_W_conv, L1_gnn_b_conv, L1_gnn_gate_W, L1_gnn_gate_b, L1_gnn_W1, L1_gnn_b1, L1_gnn_W2, L1_gnn_b2, L1_gnn_bn_gamma, L1_gnn_bn_beta, L3_gnn_W1, L3_gnn_b1, L3_gnn_W2, L3_gnn_b2, L3_gnn_Wres, L3_gnn_bres):
    import jax
    import jax.numpy as jnp

    def _L0_gnn_ref(x, rows, cols, vals):
        import jax, jax.numpy as jnp
        import numpy as np
        C = 1.0
        N_NODES = 12500
        N_EDGES = 75000
        D = 128
        EPS = 1e-15
        DEN_EPS = 1e-10

        def _artanh(x):
            return jnp.arctanh(jnp.clip(x, -1.0 + 1e-07, 1.0 - 1e-07))

        def _safe_norm(v):
            return jnp.clip(jnp.linalg.norm(v, axis=-1, keepdims=True), EPS)

        def expmap0(u, c):
            sc = jnp.sqrt(c)
            un = _safe_norm(u)
            return jnp.tanh(sc * un) * u / (sc * un)

        def logmap0(p, c):
            sc = jnp.sqrt(c)
            pn = _safe_norm(p)
            return _artanh(sc * pn) * p / (sc * pn)

        def mobius_scalar_mul(r, v, c):
            sc = jnp.sqrt(c)
            vn = _safe_norm(v)
            return jnp.tanh(r * _artanh(sc * vn)) * v / (sc * vn)

        def weighted_midpoint_spmm(x_hyp, c, rows, cols, vals):
            gamma = 2.0 / jnp.clip(1.0 - c * jnp.sum(x_hyp * x_hyp, axis=-1, keepdims=True), EPS)
            gx = gamma * x_hyp
            num = jax.ops.segment_sum(vals[:, None] * gx[cols], rows, num_segments=N_NODES)
            den = jax.ops.segment_sum(vals * (gamma[:, 0] - 1.0)[cols], rows, num_segments=N_NODES)[:, None]
            sign = jnp.where(den >= 0, 1.0, -1.0)
            den = sign * jnp.clip(jnp.abs(den), DEN_EPS)
            two_mean = num / den
            return mobius_scalar_mul(0.5, two_mean, c)
        x_hyp = expmap0(x, C)
        x_hyp_agg = weighted_midpoint_spmm(x_hyp, C, rows, cols, vals)
        x_euc_agg = logmap0(x_hyp_agg, C)
        return x_euc_agg

    def _L1_gnn_ref(feats, edge_src, edge_dst, W_conv, b_conv, gate_W, gate_b, W1, b1, W2, b2, bn_gamma, bn_beta):
        import jax, jax.numpy as jnp
        import numpy as np
        N_NODES = 6250
        N_EDGES = 62500
        D_MODEL = 128
        D_INNER = 256
        N_EXPERT = 64
        TOP_K = 2
        CAP_FACTOR = 2
        BN_EPS = 1e-05

        def _gcn_conv(feats, edge_src, edge_dst, W_conv, b_conv):
            n = feats.shape[0]
            ones = jnp.ones_like(edge_dst, dtype=feats.dtype)
            deg = jax.ops.segment_sum(ones, edge_dst, num_segments=n)
            deg = jnp.maximum(deg, 1.0)
            inv_sqrt = jax.lax.rsqrt(deg)
            norm = inv_sqrt[edge_src] * inv_sqrt[edge_dst]
            msgs = feats[edge_src] * norm[:, None]
            agg = jax.ops.segment_sum(msgs, edge_dst, num_segments=n)
            return agg @ W_conv + b_conv

        def _moe_ffn(x, gate_W, gate_b, W1, b1, W2, b2):
            T, d = x.shape
            E, h = (W1.shape[0], W1.shape[2])
            scores = x @ gate_W + gate_b
            topv, topi = jax.lax.top_k(scores, TOP_K)
            gw = jax.nn.softmax(topv, axis=-1)
            P = T * TOP_K
            eid = topi.reshape(P)
            x_rep = jnp.repeat(x, TOP_K, axis=0)
            onehot = jax.nn.one_hot(eid, E, dtype=jnp.int32)
            pos = jnp.sum(jnp.cumsum(onehot, axis=0) * onehot, axis=-1) - 1
            C = CAP_FACTOR * int(np.ceil(P / E))
            valid = pos < C
            slot = eid * C + jnp.where(valid, pos, 0)
            buf = jnp.zeros((E * C, d), x.dtype).at[slot].add(jnp.where(valid[:, None], x_rep, 0.0))
            buf = buf.reshape(E, C, d)
            hact = jax.nn.gelu(jnp.einsum('ecd,edh->ech', buf, W1) + b1[:, None, :], approximate=False)
            y = jnp.einsum('ech,ehd->ecd', hact, W2) + b2[:, None, :]
            y_pairs = y.reshape(E * C, d)[slot] * valid[:, None].astype(x.dtype)
            y_pairs = y_pairs.reshape(T, TOP_K, d)
            return jnp.einsum('tk,tkd->td', gw, y_pairs)

        def _batchnorm(x, gamma, beta):
            mean = jnp.mean(x, axis=0)
            var = jnp.mean(jnp.square(x - mean), axis=0)
            return (x - mean) * jax.lax.rsqrt(var + BN_EPS) * gamma + beta
        new_feats = _gcn_conv(feats, edge_src, edge_dst, W_conv, b_conv)
        core = _moe_ffn(new_feats, gate_W, gate_b, W1, b1, W2, b2)
        return _batchnorm(new_feats + core, bn_gamma, bn_beta)

    def _L2_gnn_ref(x, src, dst):
        import jax, jax.numpy as jnp
        import numpy as np
        N = x.shape[0]
        loop = jnp.arange(N, dtype=src.dtype)
        s = jnp.concatenate([src, loop])
        d = jnp.concatenate([dst, loop])
        ones = jnp.ones(s.shape[0], dtype=x.dtype)
        in_deg = jax.ops.segment_sum(ones, d, num_segments=N)
        out_deg = jax.ops.segment_sum(ones, s, num_segments=N)
        norm_in = jnp.clip(in_deg, 1.0) ** (-0.5)
        norm_out = jnp.clip(out_deg, 1.0) ** (-0.5)
        xs = x * norm_in[:, None]
        h = jax.ops.segment_sum(xs[s], d, num_segments=N)
        return h * norm_out[:, None]

    def _L3_gnn_ref(x, edge_index, W1, b1, W2, b2, Wres, bres):
        import jax, jax.numpy as jnp
        import numpy as np
        N_NODES = 6250
        N_EDGES = 100000
        D_IN = 128
        D_OUT = 128
        src = edge_index[0]
        dst = edge_index[1]
        agg = jax.ops.segment_sum(x[src], dst, num_segments=x.shape[0])
        h = x + agg
        h = jnp.maximum(h @ W1 + b1, 0.0) @ W2 + b2
        res = x @ Wres + bres
        return res + h
    edge_index = jnp.stack([src, dst])
    x = _layernorm(x + _L0_gnn_ref(x, src, dst, edge_weight), axis=-1)
    x = _layernorm(x + _L1_gnn_ref(x, src, dst, L1_gnn_W_conv, L1_gnn_b_conv, L1_gnn_gate_W, L1_gnn_gate_b, L1_gnn_W1, L1_gnn_b1, L1_gnn_W2, L1_gnn_b2, L1_gnn_bn_gamma, L1_gnn_bn_beta), axis=-1)
    x = _layernorm(x + _L2_gnn_ref(x, src, dst), axis=-1)
    x = _layernorm(x + _L3_gnn_ref(x, edge_index, L3_gnn_W1, L3_gnn_b1, L3_gnn_W2, L3_gnn_b2, L3_gnn_Wres, L3_gnn_bres), axis=-1)
    return x

_drawn_inputs = setup_inputs


def setup_inputs(seed=0):
    import zlib

    import numpy as np

    out = dict(_drawn_inputs(seed))
    spreads = {'L1_gnn_b_conv': (0.0, 0.1),
     'L1_gnn_gate_b': (0.0, 0.1),
     'L1_gnn_b1': (0.0, 0.1),
     'L1_gnn_b2': (0.0, 0.1),
     'L1_gnn_bn_gamma': (1.0, 0.2),
     'L1_gnn_bn_beta': (0.0, 0.1)}
    factors = {'L3_gnn_b1': 4.387}
    for name, (base, spread) in spreads.items():
        noise = np.random.default_rng([zlib.crc32(name.encode()), seed]).standard_normal(out[name].shape)
        drawn = base * np.exp(spread * noise) if base else spread * noise
        out[name] = jnp.asarray(drawn.astype(out[name].dtype))
    for name, factor in factors.items():
        out[name] = (out[name] * factor).astype(out[name].dtype)
    return out
```

```python
from contextlib import ExitStack

import concourse.bass as bass
from concourse import mybir

N, D, E = 12500, 128, 200000
P = 128
NT = -(-N // P)
NPAD = NT * P
TB = 7
NB = NT // TB
BW = TB * P
LASTN = N - (NB - 1) * BW
KC = 4
GE = KC * P
NG = -(-E // GE)
NCOL = NG * KC
EREST = E - (NG - 1) * GE
KLAST = -(-EREST // P)
NQ = -(-NG // P)
GREST = NG - (NQ - 1) * P
SLOTS = 6
TURNS = (NG - 1) // SLOTS
WIN = P
ACCW = NPAD + WIN
T0W = D + 2
NE, DH = 64, 256
CAP = 2 * (-(-2 * N // NE))
ET = 7
EP = -(-CAP // ET)
CROWS = ET * EP
FAR = 1 << 20
EPS_NORM, EPS_DEN, CLIP = 1e-15, 1e-10, 1.0 - 1e-07
LN_EPS = BN_EPS = 1e-05
assert NB * TB == NT and TURNS * SLOTS + 1 == NG and EREST % 64 == 0


def program(nc, x, src, dst, edge_weight, W_conv, b_conv, gate_W, gate_b, W1e, b1e, W2e, b2e,
            bn_gamma, bn_beta, W1, b1, W2, b2, Wres, bres, out):
    f32, bf16, i32, u32 = mybir.dt.float32, mybir.dt.bfloat16, mybir.dt.int32, mybir.dt.uint32
    ALU, ACT, AX = mybir.AluOpType, mybir.ActivationFunctionType, mybir.AxisListType
    ds = bass.ds
    ctx = ExitStack()
    with ctx:
        def sb(name, shape, dt=f32):
            return ctx.enter_context(nc.sbuf_tensor(name, shape, dt))

        def sem(name):
            return ctx.enter_context(nc.semaphore(name))

        table0 = nc.dram_tensor("table0", [NPAD + WIN, T0W], f32).ap()
        tables = [table0] + [nc.dram_tensor(f"table{n}", [NPAD, D], f32).ap() for n in (1, 2, 3)]
        sums0 = [nc.dram_tensor(f"sums0_{k}", [NPAD + P, T0W], f32).ap() for k in range(KC)]
        expert_in = nc.dram_tensor("expert_in", [NE * CROWS, D], f32).ap()
        expert_out = nc.dram_tensor("expert_out", [NE * CROWS, D], f32).ap()
        group_numbers = nc.dram_tensor("group_numbers", [2, NQ * P], i32).ap()

        X = sb("X", [P, NT, D])
        acc = sb("acc", [P, ACCW])
        shared = sb("shared", [P, ACCW])
        work = sb("work", [P, 6272])
        src_t = sb("src_t", [P, NCOL], i32)
        rel_t = sb("rel_t", [P, NCOL])
        w_t = sb("w_t", [P, NCOL])
        base_row = sb("base_row", [1, NG], i32)
        extra_row = sb("extra_row", [1, NG], i32)
        any_extra = sb("any_extra", [1, 1], i32)
        idx = sb("idx", [P, SLOTS, KC], i32)
        ident = sb("ident", [P, P])
        iota = sb("iota", [P, P])
        iota_b = sb("iota_b", [P, P], bf16)
        before = sb("before", [P, P])
        ones = sb("ones", [P, P])
        zeros = sb("zeros", [P, T0W])
        small = sb("small", [P, 18, NT])
        w_gcn = sb("w_gcn", [P, D + NE])
        col = sb("col", [P, 8])
        bconv_bc = sb("bconv_bc", [P, D])
        gateb_bc = sb("gateb_bc", [P, NE])
        b1_t = sb("b1_t", [P, 2, NE])
        bn_mv = sb("bn_mv", [P, 4])
        bn_wide = sb("bn_wide", [P, 2, P])
        run = sb("run", [P, 2, NE])
        mv = sb("mv", [P, 2, TB, 2])
        sd = sb("sd", [P, 2, TB])

        def part(t, at, shape, dt=None):
            n = 1
            for m in shape:
                n *= m
            v = t[:, at:at + (n // 2 if dt is bf16 else n)]
            if dt is not None:
                v = v.bitcast(dt)
            names = "abcd"[:len(shape)]
            if len(shape) == 1:
                return v
            sizes = {c: m for c, m in zip(names[1:], shape[1:])}
            return v.rearrange(f"p ({' '.join(names)}) -> p {' '.join(names)}", **sizes)

        deg = part(w_t, 0, (NT, 2))
        gate = part(w_t, 2 * NT, (NT, 2))
        pair_row = part(w_t, 4 * NT, (NT, 2), i32)
        self_scale = part(w_t, 6 * NT, (NT,))
        in_scale = part(w_t, 7 * NT, (3, NT))
        bn_bc = part(w_t, 10 * NT, (2, D))
        bn_stat = part(w_t, 10 * NT + 2 * D, (2 * NB, 6))
        send_row = part(w_t, 10 * NT + 2 * D + 12 * NB, (2, 2 * TB), i32)
        fetch_row = part(w_t, 10 * NT + 2 * D + 12 * NB + 4 * TB, (2, 2 * TB), i32)
        stat = part(w_t, 10 * NT + 2 * D + 12 * NB + 8 * TB, (2, TB, 6))
        dst_i = part(shared, 0, (NQ, GE), i32)
        src_i = part(shared, 2048, (NQ, GE), i32)
        w_g = part(shared, 4096, (NQ, GE))
        dst_f = part(shared, 6144, (NQ, GE))
        src_f = part(shared, 8192, (NQ, GE))
        g_min = part(shared, 10240, (NQ,))
        g_max = part(shared, 10240 + NQ, (NQ,))
        g_base = part(shared, 10240 + 2 * NQ, (NQ,), i32)
        g_span = part(shared, 10240 + 3 * NQ, (NQ,), i32)
        g_extra = part(shared, 10240 + 4 * NQ, (NQ,), i32)
        less_dump = part(shared, 0, (NCOL,))
        dst_n, bits_hi, bits_lo = (part(shared, 2048 + n * NCOL, (NCOL,), i32) for n in range(3))
        parts0 = part(shared, 0, (2, KC, TB * T0W)).rearrange("p s k (t d) -> p s k t d", d=T0W)
        dst_hi = part(acc, 0, (NCOL,))
        dst_lo = part(acc, NCOL, (NCOL,))
        edge_cols = part(acc, 2 * NCOL, (3, NCOL), bf16)
        at0 = 2 * NCOL + 3 * NCOL // 2
        ident_b = part(acc, at0, (P,), bf16)
        cols = part(acc, at0 + P // 2, (2, 3, KC), bf16)
        at0 += P // 2 + 3 * KC
        hot0 = part(acc, at0, (2, KC, P))
        same = part(acc, at0 + 2 * GE, (3, KC, P))
        window0 = part(acc, at0 + 5 * GE, (3, T0W))
        wrow = part(acc, at0 + 5 * GE + 3 * T0W, (2, KC, T0W))
        at0 += 5 * GE + 3 * T0W + 2 * KC * T0W
        later = part(acc, at0, (2, KC))
        keep = part(acc, at0 + 2 * KC, (KC,))
        unread = part(acc, at0 + 3 * KC, (KC, P))
        base_bc = part(acc, at0 + 3 * KC + GE, (NG,), i32)
        assert at0 + 3 * KC + GE + NG <= NPAD
        e_rows = part(shared, 0, (2, ET, D))
        e_rows_t = part(shared, 1792, (2, CROWS))
        e_hid = part(shared, 3360, (2, 2, CROWS))
        e_y = part(shared, 6496, (2, ET, D))
        e_w1 = part(shared, 8288, (2, DH))
        e_w2 = part(shared, 8800, (2, 2, D))
        e_b2 = part(shared, 9312, (2, D))
        e_bias = part(shared, 9568, (2, 2))
        msg = part(work, 0, (SLOTS, KC, D))
        rows0 = part(work, 0, (3, KC, T0W))
        hot = part(work, 4656, (3, KC, WIN))
        rel_x = part(work, 6192, (KC,))
        idx_x = part(work, 6196, (KC,), i32)
        b1_rows = work[0:NE, 5376:5376 + DH]
        w_conv_t = part(work, 5376 + DH, (D,))
        gate_w = part(work, 5376 + DH + D, (NE,))
        extra_f = work[0:1, 4656:4656 + NG]
        hot_lo = part(work, 3096, (2, KC, P), bf16)
        hot_hi = part(work, 3096 + KC * P, (2, KC, NT), bf16)
        slot = part(work, 0, (7, TB, D))
        slot_w = part(work, 0, (7, BW))
        tab0 = part(work, 0, (2, TB, T0W))

        c_score = part(shared, 0, (2, TB, NE))
        c_one = part(shared, 896, (2, 2, TB * NE)).rearrange("p s k (j e) -> p s k j e", j=TB)
        c_pick = part(shared, 2688, (2, TB, NE))
        c_prod = part(shared, 3584, (2, 2, TB * NE)).rearrange("p s k (j e) -> p s k j e", j=TB)
        c_top = part(shared, 5376, (2, TB, 8))
        c_at = part(shared, 5488, (2, TB, 8), u32)
        c_small = part(shared, 5632, (2, 10, 2 * TB))
        c_sum = part(shared, 6016, (NE,))
        w1_sb, w2_sb, wres_sb, bias_bc, bres_bc = (part(shared, 10752 + n * D, (D,)) for n in range(5))
        r_xt_sb = part(shared, 0, (2, BW))
        r_h_sb = part(shared, 2 * BW, (2, BW))
        r_z_sb = part(shared, 4 * BW, (2, BW))

        pp = [ctx.enter_context(nc.psum_tensor(f"pp{n}", [P, 1024], f32)) for n in range(4)]
        win = [pp[0][:, 0:512], pp[0][:, 512:1024], pp[1][:, 0:512]]
        hist = pp[1][:, 512:512 + NT]
        node_ps = [pp[2], pp[3]]
        chunk_at = lambda t, k: t[:, k // 2 * 512 + k % 2 * T0W:k // 2 * 512 + (k % 2 + 1) * T0W]
        by_bank = lambda t: t[:, :].rearrange("p (a n) -> p a n", a=2)[:, :, 0:2 * T0W]\
            .rearrange("p a (k d) -> p a k d", k=2)
        picked_ps, combined_ps = pp[0], pp[2]
        rel_ps = pp[1][:, 0:512]
        src_ps = [pp[3][:, 0:512], pp[3][:, 512:1024]]

        consts_made = sem("consts_made")
        pool_const = sem("pool_const")
        acc_zero = sem("acc_zero")
        edges_in = sem("edges_in")
        x_in = sem("x_in")
        x_pad = sem("x_pad")
        weights_in, weights3_in = sem("weights_in"), sem("weights3_in")
        bias_ready = sem("bias_ready")
        prep = sem("prep")
        rel_ready, srcf_ready = sem("rel_ready"), sem("srcf_ready")
        rel_up, src_up, w_up = sem("rel_up"), sem("src_up"), sem("w_up")
        rel_down, src_down, w_down = sem("rel_down"), sem("src_down"), sem("w_down")
        numbers_out, numbers_in = sem("numbers_out"), sem("numbers_in")
        edges_ready = sem("edges_ready")
        sq_made, sq_summed = sem("sq_made"), sem("sq_summed")
        a_dve, a_act = sem("a_dve"), sem("a_act")
        row_made, table_stored0 = sem("row_made"), [sem("table_stored0_0"), sem("table_stored0_1")]
        idx_ready = sem("idx_ready")
        msg_in = [sem(f"msg_in{s}") for s in range(SLOTS)]
        sums_zero, pad_zero, bases_in = sem("sums_zero"), sem("pad_zero"), sem("bases_in")
        cols_ready, spread, hot0_ready, route0 = sem("cols_ready"), sem("spread"), sem("hot0_ready"), sem("route0")
        window_in = [sem(f"window_in{s}") for s in range(3)]
        taken, weighted, combined, rows_ready = sem("taken"), sem("weighted"), sem("combined"), sem("rows_ready")
        scattered = [sem(f"scattered{k}") for k in range(KC)]
        sum_in = [sem("sum_in0"), sem("sum_in1")]
        z_go, z_cols, z_spread, z_win, z_hot, z_taken, z_weighted, z_combined, z_rows, z_sent, z_done, z_step = (
            sem(f"extra0_{n}") for n in ("go", "cols", "spread", "win", "hot", "taken", "weighted", "combined", "rows",
                                         "sent", "done", "step"))
        hot_ready, hist_ready, route_step = sem("hot_ready"), sem("hist_ready"), sem("route_step")
        summed, hist_summed = sem("summed"), sem("hist_summed")
        added = sem("added")
        layer_done = sem("layer_done")
        bits_ready = sem("bits_ready")
        degree, degree_sqrt = sem("degree"), sem("degree_sqrt")
        x_idx, x_msg, x_hot, x_sum, x_step = (sem(f"extra_{n}") for n in ("idx", "msg", "hot", "sum", "step"))
        half_staged, staged, evacuated, reduced = sem("half_staged"), sem("staged"), sem("evacuated"), sem("reduced")
        b_dve, b_act = sem("b_dve"), sem("b_act")
        y_ready, mv_ready, sd_ready, x_ready = sem("y_ready"), sem("mv_ready"), sem("sd_ready"), sem("x_ready")
        rstd_ready, stat_ready = sem("rstd_ready"), sem("stat_ready")
        tab_ready = sem("tab_ready")
        tab_stored = [sem("tab_stored0"), sem("tab_stored1")]
        out_stored = sem("out_stored")
        cleared = sem("cleared")
        w_dve, w_pe, w_act = sem("w_dve"), sem("w_pe"), sem("w_act")
        buffers_zero = sem("buffers_zero")
        c_staged, c_up, c_new, c_kept = sem("c_staged"), sem("c_up"), sem("c_new"), sem("c_kept")
        c_scores, c_step, c_exp = sem("c_scores"), sem("c_step"), sem("c_exp")
        c_hot, c_cum, c_route = sem("c_hot"), sem("c_cum"), sem("c_route")
        sent = [sem("sent0"), sem("sent1")]
        e_in = [sem("e_in0"), sem("e_in1")]
        e_up, e_down, e_mm1, e_act, e_mm2, e_yup = (sem(f"e_{n}") for n in ("up", "down", "mm1", "act", "mm2", "yup"))
        e_out = [sem("e_out0"), sem("e_out1")]
        k_idx, k_half, k_sum, k_kept, k_up, k_stat = (sem(f"k_{n}") for n in ("idx", "half", "sum", "kept", "up", "stat"))
        k_in = [sem("k_in0"), sem("k_in1")]
        bn_step, bn_sd, bn_up, bn_done = sem("bn_step"), sem("bn_sd"), sem("bn_up"), sem("bn_done")
        c_late = sem("c_late")
        n_prod, n_shift = sem("n_prod"), sem("n_shift")
        d_staged, d_up, d_self = sem("d_staged"), sem("d_up"), sem("d_self")
        r_in = [sem("r_in0"), sem("r_in1")]
        r_up, r_xt, r_h, r_z, r_zt, r_y, r_xb = (sem(f"r_{n}") for n in ("up", "xt", "h", "z", "zt", "y", "xb"))

        noted = {name: sem(f"noted_{name}") for name in ("Pool", "DVE")}
        e_bias_in = sem("e_bias_in")

        block = ctx.enter_context(nc.Block())

        def after(eng, s, n):
            if not isinstance(n, int) or n > 0:
                eng.wait_ge(s, n)

        def apart(eng, s, n):
            eng.wait_ge(s, n)
            eng.sem_inc(noted[eng.engine.name], 1)

        def batches(eng, *stages):
            lag = len(stages) - 1
            peeled = 4 if lag else 2

            def fixed(t):
                for k, stage in enumerate(stages):
                    if 0 <= t - k < NB:
                        stage(t - k, (t - k) % 2, (t - k) // 2)

            for t in range(peeled):
                fixed(t)
            with eng.Fori(peeled // 2, NB // 2) as i:
                for half in range(2):
                    for k, stage in enumerate(stages):
                        stage(2 * i + (half - k), (half - k) % 2, i + (half - k) // 2)
            for t in range(NB, NB + lag):
                fixed(t)

        def tiles(b, n=TB):
            return ds(b * TB, n)

        def groups(eng, body, turns=TURNS, begin=None):
            if begin:
                begin(0)
            for s in range(SLOTS):
                body(s, s, 0)
            with eng.Fori(1, turns) as turn:
                if begin:
                    begin(turn)
                for s in range(SLOTS):
                    body(turn * SLOTS + s, s, turn)

        def rounds(eng, body, begin=None):
            groups(eng, body, TURNS - 1, begin)
            for turn in (TURNS - 1, TURNS):
                todo = range(SLOTS) if turn < TURNS else range(1)
                if begin:
                    begin(turn)
                for s in todo:
                    body(turn * SLOTS + s, s, turn)

        def there(g):
            return not isinstance(g, int) or g < NG

        def extra_windows(eng, body, begin=None):
            for k in range(KC):
                eng.wait_ge(scattered[k], 16 * NG)
            flag = eng.value_load(any_extra[0:1, 0:1], min_val=0, max_val=NT)
            with eng.If(flag > 0):
                with eng.Fori(0, NG) as g:
                    n = eng.value_load(extra_row[0:1, ds(g, 1)], min_val=0, max_val=NT)
                    with eng.If(n > 0):
                        if begin:
                            begin(g)
                        with eng.Fori(0, n) as j:
                            body(g, j)

        def take(eng, s):
            n = {z_win: 16, z_sent: 16 * KC}.get(s, 1)
            eng.wait_ge(s, n)
            eng.sem_clear(s)

        LAST = NG - 1
        PREP_STEPS = 5
        B_STEPS = (7, 11)
        BN_STEPS = 6
        USES = [TURNS * KC * 16 + (KLAST * 16 if s == 0 else 0) for s in range(SLOTS)]
        msg_at = lambda layer, s, turn: (layer - 1) * USES[s] + (turn + 1) * (KC * 16)
        STORES = NB // 2

        @block.sync
        def _(sp):
            full = (NQ - 1) * P * GE
            most = (NG - 1) * GE
            for src_ap, dst_ap, fill in ((dst, dst_i, E - (GE - EREST)), (src, src_i, 0), (edge_weight, w_g, 0)):
                sp.dma_start(dst_ap[:, 0:NQ - 1, :],
                             src_ap[0:full].rearrange("(q p j) -> p q j", p=P, j=GE)).then_inc(edges_in, 16)
                sp.dma_start(dst_ap[0:GREST - 1, NQ - 1, :],
                             src_ap[full:most].rearrange("(p j) -> p j", j=GE)).then_inc(edges_in, 16)
                sp.dma_start(dst_ap[GREST - 1:GREST, NQ - 1, 0:EREST],
                             src_ap[most:E].rearrange("(p j) -> p j", p=1)).then_inc(edges_in, 16)
                sp.dma_start(dst_ap[GREST - 1:GREST, NQ - 1, EREST:GE],
                             src_ap[fill:fill + GE - EREST].rearrange("(p j) -> p j", p=1)).then_inc(edges_in, 16)
            sp.wait_ge(x_pad, 1)
            for c in range(NB):
                m = TB if c < NB - 1 else TB - 1
                sp.dma_start(X[:, c * TB:c * TB + m, :],
                             x[c * BW:c * BW + m * P, :].rearrange("(t p) d -> p t d", p=P)).then_inc(x_in, 16)
            sp.dma_start(X[0:N - (NT - 1) * P, NT - 1, :], x[(NT - 1) * P:N, :]).then_inc(x_in, 16)
            column = lambda v: v.rearrange("(p a) -> p a", a=1)
            for to, of in ((w_gcn[:, 0:D], W_conv), (gate_w[:, :], gate_W), (b1_rows[:, :], b1e), (col[:, 0:1], column(b_conv)),
                           (col[:, 1:2], column(bn_gamma)), (col[:, 2:3], column(bn_beta)), (col[:, 3:4], column(b1)),
                           (bconv_bc[:, :], b_conv.partition_broadcast(P)),
                           (gateb_bc[:, :], gate_b.partition_broadcast(P))):
                sp.dma_start(to, of).then_inc(weights_in, 16)
            sp.wait_ge(prep, PREP_STEPS)
            for n, g in enumerate((g_base, g_extra)):
                sp.dma_start(group_numbers[n, 0:(NQ - 1) * P].rearrange("(q p) -> p q", p=P),
                             g[:, 0:NQ - 1], allow_slow_non_contiguous=True).then_inc(numbers_out, 16)
                sp.dma_start(group_numbers[n, (NQ - 1) * P:NG].rearrange("(p a) -> p a", a=1),
                             g[0:GREST, NQ - 1:NQ], allow_slow_non_contiguous=True).then_inc(numbers_out, 16)
            sp.wait_ge(numbers_out, 64)
            sp.dma_start(base_row[:, :], group_numbers[0:1, 0:NG]).then_inc(numbers_in, 16)
            sp.dma_start(extra_row[:, :], group_numbers[1:2, 0:NG]).then_inc(numbers_in, 16)
            sp.dma_start(base_bc, group_numbers[0:1, 0:NG].rearrange("a g -> (a g)").partition_broadcast(P)).then_inc(bases_in, 16)

            def store0(b, s, turn):
                sp.wait_ge(row_made, b + 1)
                sp.dma_start(table0.rearrange("(t p) d -> p t d", p=P)[:, tiles(b), :],
                             tab0[:, s, :, :]).then_inc(table_stored0[s], 16)
            sp.wait_ge(pool_const, 1)
            sp.dma_start(table0[NPAD:NPAD + WIN, :], zeros[:, :]).then_inc(pad_zero, 16)
            batches(sp, store0)

            bases = {}

            def load_bases(turn):
                for s in range(SLOTS if not isinstance(turn, int) or turn < TURNS else 1):
                    bases[s] = sp.value_load(base_row[0:1, ds(turn * SLOTS + s, 1)], min_val=0, max_val=N - 1)

            def load_window(g, s, turn):
                after(sp, taken, g - 2)
                sp.dma_start(window0[:, s % 3, :], table0[ds(bases[s], WIN), :]).then_inc(window_in[s % 3], 16)

            def load_extra(g, j):
                first = sp.value_load(base_row[0:1, ds(g, 1)], min_val=0, max_val=N - 1)
                take(sp, z_go)
                at = nc.s_assert_within(first + WIN * (j + 1), WIN, N - 1,
                                        skip_runtime_bounds_check_because="no window begins beyond the group's last node")
                sp.dma_start(window0[:, 0, :], table0[ds(at, WIN), :]).then_inc(z_win, 16)

            sp.wait_ge(numbers_in, 32)
            sp.wait_ge(pad_zero, 16)
            for n in range(2):
                sp.wait_ge(table_stored0[n], 16 * (NB // 2))
            rounds(sp, load_window, load_bases)
            extra_windows(sp, load_extra)

            def load_sums(b, s, turn):
                after(sp, reduced, b - 1)
                for k in range(KC):
                    sp.dma_start(parts0[:, s, k, :, :], sums0[k].rearrange("(t p) d -> p t d", p=P)[:, tiles(b), :])\
                        .then_inc(sum_in[s], 16)
            sp.wait_ge(layer_done, 1)
            batches(sp, load_sums)

            def store_table(layer):
                view = tables[layer].rearrange("(t p) d -> p t d", p=P)

                def body(b, s, turn):
                    sp.wait_ge(tab_ready, (layer - 1) * NB + b + 1)
                    sp.dma_start(view[:, tiles(b), :], slot[:, 2 + s, :, :]).then_inc(tab_stored[s], 16)
                batches(sp, body)

            store_table(1)
            for to, of in ((w1_sb, W1), (w2_sb, W2), (wres_sb, Wres), (bias_bc, b2.partition_broadcast(P)),
                           (bres_bc, bres.partition_broadcast(P))):
                sp.dma_start(to, of).then_inc(weights3_in, 16)

            def expert_load(e, s):
                after(sp, e_mm2, e - 1)
                after(sp, e_yup, e - 1)
                sp.dma_start(e_rows[0:EP, s, :, :],
                             expert_in[ds(e * CROWS, CROWS), :].rearrange("(t p) d -> p t d", p=EP)).then_inc(e_in[s], 16)
                sp.dma_start(e_w1[:, s, :], W1e.rearrange("e p h -> p e h")[:, ds(e, 1), :]
                             .rearrange("p e h -> p (e h)")).then_inc(e_in[s], 16)
                sp.dma_start(e_w2[:, s, :, :], W2e.rearrange("e (h p) d -> p (e h) d", p=P)[:, ds(e * 2, 2), :])\
                    .then_inc(e_in[s], 16)
                sp.dma_start(e_b2[0:EP, s, :], b2e[ds(e, 1), :].rearrange("e d -> (e d)").partition_broadcast(EP))\
                    .then_inc(e_in[s], 16)

            def expert_store(e, s):
                sp.wait_ge(e_yup, e + 1)
                sp.dma_start(expert_out[ds(e * CROWS, CROWS), :].rearrange("(t p) d -> p t d", p=EP),
                             e_y[0:EP, s, :, :]).then_inc(e_out[s], 16)

            for s in range(2):
                sp.wait_ge(sent[s], 16 * 2 * TB * (NB // 2))
            expert_load(0, 0)
            expert_load(1, 1)
            expert_store(0, 0)
            with sp.Fori(1, NE // 2) as i:
                expert_load(2 * i, 0)
                expert_store(2 * i - 1, 1)
                expert_load(2 * i + 1, 1)
                expert_store(2 * i, 0)
            expert_store(NE - 1, 1)

            store_table(2)

            def store3(b, s, turn):
                sp.wait_ge(x_ready, 2 * NB + b + 1)
                sp.dma_start(tables[3].rearrange("(t p) d -> p t d", p=P)[:, tiles(b), :],
                             X[:, tiles(b), :]).then_inc(tab_stored[s], 16)
            batches(sp, store3)

            def load_rows(b, s):
                after(sp, r_up, b - 1)
                sp.dma_start(slot[:, s, :, :],
                             tables[3].rearrange("(t p) d -> p t d", p=P)[:, tiles(b), :]).then_inc(r_in[s], 16)

            def store_out(b, s):
                sp.wait_ge(x_ready, 3 * NB + b + 1)
                sp.dma_start(out[ds(b * BW, BW), :].rearrange("(t p) d -> p t d", p=P),
                             X[:, tiles(b), :]).then_inc(out_stored, 16)

            for s in range(2):
                sp.wait_ge(tab_stored[s], 16 * 3 * STORES)
            sp.wait_ge(layer_done, 4)
            load_rows(0, 0)
            load_rows(1, 1)
            with sp.Fori(1, NB // 2) as i:
                load_rows(2 * i, 0)
                store_out(2 * i - 2, 0)
                load_rows(2 * i + 1, 1)
                store_out(2 * i - 1, 1)
            store_out(NB - 2, 0)
            b = NB - 1
            sp.wait_ge(x_ready, 4 * NB)
            sp.dma_start(out[b * BW:b * BW + (TB - 1) * P, :].rearrange("(t p) d -> p t d", p=P),
                         X[:, b * TB:NT - 1, :]).then_inc(out_stored, 16)
            sp.dma_start(out[(NT - 1) * P:N, :], X[0:N - (NT - 1) * P, NT - 1, :]).then_inc(out_stored, 16)
            sp.wait_ge(out_stored, 16 * (NB + 1))

        @block.gpsimd
        def _(pool):
            pool.memset(X[:, NT - 1, :], 0.0).then_inc(x_pad, 1)
            pool.memset(zeros[:, :], 0.0).then_inc(pool_const, 1)
            pool.memset(ident[:, :], 0.0).then_inc(consts_made, 1)
            pool.memset(ones[:, :], 1.0).then_inc(consts_made, 1)
            pool.iota(iota[:, :], [[1, P]], base=0, channel_multiplier=0,
                      allow_small_or_imprecise_dtypes=True).then_inc(consts_made, 1)
            pool.iota(iota_b[:, :], [[1, P]], base=0, channel_multiplier=0,
                      allow_small_or_imprecise_dtypes=True).then_inc(consts_made, 1)
            pool.wait_ge(consts_made, 4)
            pool.affine_select(out=ident[:, :], in_=ident[:, :], compare_op=ALU.not_equal, fill=1.0,
                               base=0, pattern=[[-1, P]], channel_multiplier=1).then_inc(consts_made, 1)
            pool.affine_select(out=before[:, :], in_=ones[:, :], compare_op=ALU.is_gt, fill=0.0,
                               base=0, pattern=[[1, P]], channel_multiplier=-1).then_inc(consts_made, 1)
            pool.memset(run[:, 0, :], 0.0).then_inc(consts_made, 1)
            pool.affine_select(out=ident_b, in_=ones[:, :], compare_op=ALU.is_equal, fill=0.0,
                               base=0, pattern=[[-1, P]], channel_multiplier=1).then_inc(consts_made, 1)
            pool.iota(col[:, 5:6], [[1, 1]], base=0, channel_multiplier=1,
                      allow_small_or_imprecise_dtypes=True).then_inc(consts_made, 1)
            pool.iota(col[:, 6:7], [[1, 1]], base=NPAD, channel_multiplier=1,
                      allow_small_or_imprecise_dtypes=True).then_inc(consts_made, 1)
            pool.memset(acc[:, NPAD:ACCW], 0.0).then_inc(acc_zero, 1)

            blank = zeros[:, 0:D].unsqueeze(1).to_broadcast([P, TB, D])

            def gather(layer):
                table = tables[layer]

                def table_complete():
                    pool.wait_ge(tab_stored[0], 16 * layer * STORES)
                    pool.wait_ge(tab_stored[1], 16 * layer * STORES)

                def rows(s, chunks):
                    for k in range(chunks):
                        pool.indirect_dma_start(
                            out=msg[:, s, k, :], out_offset=None, in_=table,
                            in_offset=bass.IndirectOffsetOnAxis(ap=idx[:, s, k:k + 1], axis=0),
                            bounds_check=NPAD - 1, oob_is_err=False).then_inc(msg_in[s], 16)

                def body(g, s, turn):
                    apart(pool, idx_ready, (layer - 1) * NG + g + 1)
                    rows(s, KC)
                table_complete()
                groups(pool, body)
                pool.wait_ge(idx_ready, layer * NG)
                rows(0, KLAST)

                pool.wait_ge(added, layer * NG)
                flag = pool.value_load(any_extra[0:1, 0:1], min_val=0, max_val=NT)
                with pool.If(flag > 0):
                    with pool.Fori(0, NG) as g:
                        n = pool.value_load(extra_row[0:1, ds(g, 1)], min_val=0, max_val=NT)
                        with pool.If(n > 0):
                            pool.wait_ge(x_idx, 1)
                            pool.sem_clear(x_idx)
                            for k in range(KC):
                                pool.indirect_dma_start(
                                    out=msg[:, 0, k, :], out_offset=None, in_=table,
                                    in_offset=bass.IndirectOffsetOnAxis(ap=idx_x[:, k:k + 1], axis=0),
                                    bounds_check=NPAD - 1, oob_is_err=False).then_inc(x_msg, 16)

            def clear_sums(layer):
                def body(b, s, turn):
                    pool.wait_ge(y_ready, layer * NB + b + 1)
                    pool.tensor_copy(acc[:, ds(b * BW, BW)].rearrange("p (t d) -> p t d", d=D), blank).then_inc(cleared, 1)
                batches(pool, body)

            def add_rows(rows, picked, k, done):
                pool.indirect_dma_start(
                    out=sums0[k], out_offset=bass.IndirectOffsetOnAxis(ap=picked, axis=0), in_=rows, in_offset=None,
                    bounds_check=NPAD + P - 1, oob_is_err=True, compute_op=ALU.add).then_inc(done, 16)

            def scatter(g, s, turn):
                if isinstance(g, int):
                    pool.wait_ge(route0, g + 1)
                    pool.wait_ge(rows_ready, g + 1)
                else:
                    apart(pool, route0, g + 1)
                    apart(pool, rows_ready, g + 1)
                for k in range(KC):
                    if not isinstance(g, int):
                        apart(pool, scattered[k], 16 * g)
                    elif g:
                        pool.wait_ge(scattered[k], 16 * g)
                    add_rows(rows0[:, s % 3, k, :], idx[:, s, k:k + 1], k, scattered[k])

            def scatter_extra(g, j):
                take(pool, z_rows)
                for k in range(KC):
                    add_rows(rows0[:, 0, k, :], idx[:, 0, k:k + 1], k, z_sent)
                take(pool, z_sent)
                pool.sem_inc(z_done, 1)
            pool.wait_ge(sums_zero, 16 * KC)
            rounds(pool, scatter)
            extra_windows(pool, scatter_extra)
            clear_sums(0)
            gather(1)

            pool.wait_ge(buffers_zero, 64)

            def send(b, s, turn):
                apart(pool, c_route, b + 1)
                for j in range(TB):
                    for k in range(2):
                        pool.indirect_dma_start(
                            out=expert_in, out_offset=bass.IndirectOffsetOnAxis(ap=send_row[:, s, 2 * j + k:2 * j + k + 1], axis=0),
                            in_=slot[:, 2 + s, j, :], in_offset=None,
                            bounds_check=NE * CROWS - 1, oob_is_err=False).then_inc(sent[s], 16)
            batches(pool, send)

            def fetch(b, s, turn):
                apart(pool, k_idx, b + 1)
                for j in range(TB):
                    for k in range(2):
                        pool.indirect_dma_start(
                            out=slot[:, 2 * s + k, j, :], out_offset=None, in_=expert_out,
                            in_offset=bass.IndirectOffsetOnAxis(ap=fetch_row[:, s, 2 * j + k:2 * j + k + 1], axis=0),
                            bounds_check=NE * CROWS - 1, oob_is_err=False).then_inc(k_in[s], 16)
            for s in range(2):
                pool.wait_ge(e_out[s], 16 * (NE // 2))
            batches(pool, fetch)

            pool.wait_ge(bn_done, 1)

            def shift(b, s, turn):
                pool.wait_ge(y_ready, NB + b - 1)
                pool.tensor_tensor(slot[:, 4 + s, :, :], X[:, tiles(b), :],
                                   bn_bc[:, 1, :].unsqueeze(1).to_broadcast([P, TB, D]), ALU.add).then_inc(n_shift, 1)

            def clear(b, s, turn):
                pool.wait_ge(y_ready, NB + b + 1)
                pool.tensor_copy(acc[:, ds(b * BW, BW)].rearrange("p (t d) -> p t d", d=D), blank).then_inc(cleared, 1)
            batches(pool, shift, clear)

            gather(2)
            clear_sums(2)
            gather(3)

            pool.wait_ge(bias_ready, 1)

            pool.wait_ge(layer_done, 4)

            def residual(b, s, turn):
                pool.wait_ge(y_ready, 3 * NB + b - 1)
                pool.tensor_tensor(slot[:, 5 + s, :, :], X[:, tiles(b), :],
                                   bias_bc[:, :].unsqueeze(1).to_broadcast([P, TB, D]), ALU.add).then_inc(r_xb, 1)
            batches(pool, residual)

        @block.scalar
        def _(act):
            act.wait_ge(pool_const, 1)
            for k in range(KC):
                act.dma_start(sums0[k].rearrange("(t p) d -> p t d", p=P),
                              zeros[:, :].unsqueeze(1).to_broadcast([P, NT + 1, T0W])).then_inc(sums_zero, 16)

            act.wait_ge(edges_in, 12 * 16)
            act.activation(src_f[:, 0:NQ - 1, :], src_i[:, 0:NQ - 1, :], ACT.Copy).then_inc(srcf_ready, 1)
            act.activation(src_f[0:GREST, NQ - 1, :], src_i[0:GREST, NQ - 1, :], ACT.Copy).then_inc(srcf_ready, 1)
            for q in range(NQ):
                m = P if q < NQ - 1 else GREST
                cols = slice(q * GE, q * GE + KC * m)
                act.wait_ge(src_up, q + 1)
                act.activation(src_t[:, cols].rearrange("p (g k) -> p k g", k=KC),
                               pp[3][:, 0:512].rearrange("p (k g) -> p k g", k=KC)[:, :, 0:m], ACT.Copy).then_inc(src_down, 1)
                act.wait_ge(w_up, q + 1)
                act.activation(w_t[:, cols].rearrange("p (g k) -> p k g", k=KC),
                               pp[3][:, 512:1024].rearrange("p (k g) -> p k g", k=KC)[:, :, 0:m], ACT.Copy).then_inc(w_down, 1)

            act.wait_ge(w_pe, 1)
            act.activation(w_conv_t[:, :], pp[1][:, 512:640], ACT.Copy).then_inc(w_act, 1)
            act.activation(b1_t[:, :, :], pp[1][:, 640:768].rearrange("p (h e) -> p h e", h=2), ACT.Copy).then_inc(w_act, 1)

            act.wait_ge(x_in, 16 * (NB + 1))
            act.wait_ge(x_pad, 1)

            def squares(b, s, turn):
                after(act, sq_summed, b - 1)
                act.activation(slot[:, 4 + s, :, :], X[:, tiles(b), :], ACT.Square).then_inc(sq_made, 1)
            batches(act, squares)
            act.wait_ge(sq_summed, NB)
            act.activation(small[:, 1, :], small[:, 0, :], ACT.Sqrt).then_inc(a_act, 1)
            act.wait_ge(a_dve, 1)
            act.activation(small[:, 2, :], small[:, 1, :], ACT.Tanh).then_inc(a_act, 1)

            def source_rows(g, s):
                act.copy(idx[:, s, :], src_t[:, ds(g * KC, KC)]).then_inc(idx_ready, 1)

            quarter = NE * ET // 4
            for n in range(4):
                rows = expert_in[n * quarter * EP:(n + 1) * quarter * EP, :].rearrange("(t p) d -> p t d", p=EP)
                act.dma_start(rows, zeros[0:EP, 0:D].unsqueeze(1).to_broadcast([EP, quarter, D])).then_inc(buffers_zero, 16)

            def weigh_rows(g, ws):
                act.copy(wrow[:, ws, :, T0W - 1].rearrange("p (a k) -> p a k", a=2), by_bank(picked_ps)[:, :, :, T0W - 1])
                for k in range(KC):
                    i = act.activation(wrow[:, ws, k, 0:T0W - 1], chunk_at(picked_ps, k)[:, 0:T0W - 1], ACT.Copy,
                                       scale=w_t[:, ds(g * KC + k, 1)])
                return i

            def keep_rows(rs):
                return act.activation(rows0[:, rs, :, :].rearrange("p (a k) d -> p a k d", a=2), by_bank(combined_ps), ACT.Copy)

            def weigh(g, s):
                act.wait_ge(taken, g + 1)
                after(act, combined, g - 1)
                weigh_rows(g, s % 2).then_inc(weighted, 1)

            def rows_by_source(g, s, turn):
                if there(g + 1):
                    weigh(g + 1, (s + 1) % SLOTS)
                for k in range(KC):
                    after(act, scattered[k], 16 * (g - 2))
                act.wait_ge(combined, g + 1)
                keep_rows(s % 3).then_inc(rows_ready, 1)

            def rows_extra(g, j):
                take(act, z_taken)
                weigh_rows(g, 0).then_inc(z_weighted, 1)
                take(act, z_combined)
                keep_rows(0).then_inc(z_rows, 1)

            def layer0_rows():
                act.wait_ge(w_down, NQ)
                weigh(0, 0)
                rounds(act, rows_by_source)
                extra_windows(act, rows_extra)

            def gather(layer):
                act.wait_ge(layer_done, layer)
                for s in range(SLOTS):
                    source_rows(s, s)

                def body(g, s, turn):
                    act.wait_ge(summed, (layer - 1) * NG + g + 1)
                    source_rows(g + SLOTS, s)
                groups(act, body, TURNS - 1)
                act.wait_ge(summed, (layer - 1) * NG + LAST - SLOTS + 1)
                source_rows(LAST, 0)

            def deviation(layer):
                def body(b, s, turn):
                    act.wait_ge(mv_ready, layer * NB + b + 1)
                    act.activation(sd[:, s, :], mv[:, s, :, 1], ACT.Sqrt, bias=col[:, 4:5]).then_inc(sd_ready, 1)
                return body

            def table_rows(layer, scale):
                def late(b, s, turn):
                    act.wait_ge(x_ready, layer * NB + b + 1)
                    after(act, tab_stored[s], 16 * (layer * STORES + turn))
                    for j in range(TB):
                        i = act.activation(slot[:, 2 + s, j, :], X[:, b * TB + j, :], ACT.Copy,
                                           scale=in_scale[:, scale, ds(b * TB + j, 1)])
                    i.then_inc(tab_ready, 1)
                return late

            layer0_rows()

            def down(b, s, turn):
                act.wait_ge(staged, b + 1)
                after(act, reduced, b - 1)
                act.activation(acc[:, ds(b * BW, BW)].rearrange("p (t d) -> p t d", d=D), parts0[:, s, 0, :, 0:D], ACT.Copy)
                act.activation(slot[:, 4 + s, :, :], parts0[:, s, 0, :, 0:D], ACT.Square).then_inc(evacuated, 1)
            batches(act, down)
            act.wait_ge(reduced, NB)
            act.activation(small[:, 1, :], small[:, 0, :], ACT.Sqrt).then_inc(b_act, 1)
            act.wait_ge(b_dve, B_STEPS[0])
            act.activation(small[:, 8, :], small[:, 7, :], ACT.Sqrt).then_inc(b_act, 1)
            act.activation(small[:, 10, :], small[:, 9, :], ACT.Sqrt).then_inc(b_act, 1)
            act.wait_ge(b_dve, B_STEPS[1])
            act.activation(small[:, 12, :], small[:, 11, :], ACT.Ln).then_inc(b_act, 1)
            batches(act, deviation(0), table_rows(0, 0))
            gather(1)

            act.wait_ge(degree, 1)
            act.activation(small[:, 1, :], small[:, 0, :], ACT.Sqrt).then_inc(degree_sqrt, 1)

            def keep_new(b, s, turn):
                act.wait_ge(c_new, b + 1)
                act.activation(acc[:, ds(b * BW, BW)], slot_w[:, 2 + s, :], ACT.Copy).then_inc(c_kept, 1)
                act.wait_ge(c_scores, b + 1)
                act.activation(c_small[:, s, 1, 0:TB], c_small[:, s, 0, 0:TB], ACT.Exp).then_inc(c_exp, 1)
            batches(act, keep_new)

            def hidden(e, s):
                act.copy(e_bias[:, s, :], b1_t[:, :, ds(e, 1)].rearrange("p h e -> p (h e)")).then_inc(e_bias_in, 1)
                act.wait_ge(e_bias_in, e + 1)
                for h in range(2):
                    for n in range(2):
                        act.wait_ge(e_mm1, 4 * e + 2 * h + n + 1)
                        if h == n == 0:
                            after(act, e_mm2, e - 1)
                        half = slice(n * CROWS // 2, (n + 1) * CROWS // 2)
                        act.activation(e_hid[:, s, h, half], pp[1 + h][:, n * 512:n * 512 + CROWS // 2], ACT.Gelu,
                                       bias=e_bias[:, s, h:h + 1]).then_inc(e_act, 1)
            hidden(0, 0)
            hidden(1, 1)
            with act.Fori(1, NE // 2) as i:
                hidden(2 * i, 0)
                hidden(2 * i + 1, 1)

            def keep_sum(b, s, turn):
                act.wait_ge(k_sum, b + 1)
                act.activation(acc[:, ds(b * BW, BW)], slot_w[:, 4 + s, :], ACT.Copy).then_inc(k_kept, 1)
            batches(act, keep_sum)
            act.wait_ge(bn_step, 1)
            act.activation(bn_mv[:, 2:3], bn_mv[:, 1:2], ACT.Sqrt, bias=col[:, 4:5]).then_inc(bn_sd, 1)
            batches(act, deviation(1), table_rows(1, 1))
            gather(2)

            def own(b, s, turn):
                after(act, y_ready, 2 * NB + b - 1)
                for j in range(TB):
                    i = act.activation(slot[:, 4 + s, j, :], X[:, b * TB + j, :], ACT.Copy,
                                       scale=self_scale[:, ds(b * TB + j, 1)])
                i.then_inc(d_self, 1)
                deviation(2)(b, s, turn)
            act.wait_ge(layer_done, 3)
            batches(act, own)
            gather(3)

            def hidden3(b, s, turn):
                act.wait_ge(r_up, b + 1)
                after(act, r_y, b - 1)
                act.activation(r_xt_sb[:, s, :], pp[0][:, 0:BW], ACT.Copy).then_inc(r_xt, 1)
                act.wait_ge(r_z, b + 1)
                act.activation(r_z_sb[:, s, :].rearrange("p (a n) -> p a n", a=2),
                               pp[1][:, :].rearrange("p (a n) -> p a n", a=2)[:, :, 0:BW // 2], ACT.Relu,
                               bias=col[:, 3:4]).then_inc(r_zt, 1)
            batches(act, hidden3, deviation(3))

        @block.tensor
        def _(pe):
            pe.wait_ge(consts_made, 7)
            pe.wait_ge(edges_in, 12 * 16)
            pe.wait_ge(srcf_ready, 2)
            for q in range(NQ):
                m = P if q < NQ - 1 else GREST
                pe.wait_ge(rel_ready, q + 1)
                for of, to, up, free in ((dst_f, pp[2][:, q % 2 * 512:q % 2 * 512 + 512], rel_up, (rel_down, q - 1)),
                                         (src_f, pp[3][:, 0:512], src_up, (src_down, q)),
                                         (w_g, pp[3][:, 512:1024], w_up, (w_down, q))):
                    after(pe, *free)
                    for k in range(KC):
                        i = pe.transpose(to[:, k * P:k * P + m], of[0:m, q, k * P:(k + 1) * P], ident[0:m, 0:m])
                    i.then_inc(up, 1)

            pe.wait_ge(weights_in, 9 * 16)
            pe.transpose(pp[1][:, 512:640], w_gcn[:, 0:D], ident[:, :])
            for h in range(2):
                i = pe.transpose(pp[1][:, 640 + h * NE:640 + (h + 1) * NE], b1_rows[:, h * P:(h + 1) * P], ident[0:NE, 0:NE])
            i.then_inc(w_pe, 1)
            pe.wait_ge(w_act, 2)
            pe.wait_ge(w_dve, 1)
            pe.matmul(pp[1][:, 512:512 + NE], w_conv_t[:, :], gate_w[:, :], start=True, stop=True)
            pe.matmul(pp[1][:, 512 + NE:512 + 2 * NE], bn_wide[:, 0, :], gate_w[:, :], start=True, stop=True).then_inc(w_pe, 1)

            def spread_columns(cs, ss):
                for k in range(KC):
                    to = slice(k * P, (k + 1) * P)
                    along = lambda n: cols[:, cs, n, k:k + 1].to_broadcast([P, P])
                    pe.matmul(src_ps[ss][:, to], along(0), ident_b, start=True, stop=False)
                    pe.matmul(src_ps[ss][:, to], along(1), ident_b, start=False, stop=True)
                    i = pe.matmul(rel_ps[:, to], along(2), ident_b, start=True, stop=True)
                return i

            def take_rows(ws, hs):
                for k in range(KC):
                    i = pe.matmul(chunk_at(picked_ps, k), hot0[:, hs, k, :], window0[:, ws, :], start=True, stop=True)
                return i

            def combine_rows(es, rs):
                for k in range(KC):
                    i = pe.matmul(chunk_at(combined_ps, k), same[:, es, k, :], wrow[:, rs, k, :], start=True, stop=True)
                return i

            def spread_group(g, s):
                pe.wait_ge(cols_ready, g + 1)
                after(pe, hot0_ready, g)
                spread_columns(s % 2, s % 2).then_inc(spread, 1)

            def take_group(g, s, turn):
                pe.wait_ge(hot0_ready, g + 1)
                pe.wait_ge(window_in[s % 3], 16 * (2 * turn + s // 3 + 1))
                after(pe, weighted, g)
                take_rows(s % 3, s % 2).then_inc(taken, 1)

            def count_in(g, s):
                pe.wait_ge(hist_ready, g + 1)
                for k in range(KC):
                    i = pe.matmul(hist, hot_lo[:, s % 2, k, :], hot_hi[:, s % 2, k, :],
                                  start=(isinstance(g, int) and g == k == 0),
                                  stop=(isinstance(g, int) and g == LAST and k == KC - 1))
                i.then_inc(hist_summed, 1)

            def products0(g, s, turn):
                next_of = lambda n: ((s + n) % SLOTS, turn + (s + n) // SLOTS)
                if there(g + 2):
                    spread_group(g + 2, next_of(2)[0])
                if there(g + 1):
                    take_group(g + 1, *next_of(1))
                    count_in(g + 1, next_of(1)[0])
                pe.wait_ge(weighted, g + 1)
                after(pe, rows_ready, g)
                combine_rows(s % 3, s % 2).then_inc(combined, 1)

            def products_extra(g, j):
                take(pe, z_cols)
                spread_columns(0, 0).then_inc(z_spread, 1)
                take(pe, z_hot)
                take(pe, z_win)
                take_rows(0, 0).then_inc(z_taken, 1)
                take(pe, z_weighted)
                combine_rows(0, 0).then_inc(z_combined, 1)

            pe.wait_ge(consts_made, 10)
            pe.wait_ge(w_dve, 2)
            for s, n in ((rel_down, NQ), (src_down, NQ), (w_down, NQ)):
                pe.wait_ge(s, n)
            spread_group(0, 0)
            take_group(0, 0, 0)
            count_in(0, 0)
            spread_group(1, 1)
            rounds(pe, products0)
            extra_windows(pe, products_extra)

            def sums(layer):
                def window(at, rs, hs, chunks):
                    for k in range(chunks):
                        i = pe.matmul(win[at][:, 0:WIN], msg[:, rs, k, :], hot[:, hs, k, :],
                                      start=(k == 0), stop=(k == chunks - 1))
                    return i

                def body(g, s, turn, chunks=KC):
                    pe.wait_ge(msg_in[s], msg_at(layer, s, turn) if chunks == KC else layer * USES[s])
                    after(pe, added, (layer - 1) * NG + g - 2)
                    pe.wait_ge(hot_ready, (layer - 1) * NG + g + 1)
                    window(s % 3, s, s % 3, chunks).then_inc(summed, 1)
                groups(pe, body)
                body(LAST, 0, TURNS, KLAST)

                pe.wait_ge(added, layer * NG)
                flag = pe.value_load(any_extra[0:1, 0:1], min_val=0, max_val=NT)
                with pe.If(flag > 0):
                    with pe.Fori(0, NG) as g:
                        n = pe.value_load(extra_row[0:1, ds(g, 1)], min_val=0, max_val=NT)
                        with pe.If(n > 0):
                            with pe.Fori(0, n):
                                pe.wait_ge(x_hot, 1)
                                pe.sem_clear(x_hot)
                                window(0, 0, 0, KC).then_inc(x_sum, 1)

            sums(1)

            def product1(b, s, turn):
                pe.wait_ge(c_staged, b + 1)
                after(pe, c_scores, b - 1)
                for j in range(TB):
                    pe.matmul(node_ps[s][:, j * P:(j + 1) * P], slot[:, s, j, :], w_gcn[:, 0:D], start=True, stop=True)
                for j in range(TB):
                    i = pe.matmul(pp[0][:, s * 512 + j * NE:s * 512 + (j + 1) * NE], slot[:, s, j, :], w_gcn[:, D:D + NE],
                                  start=True, stop=True)
                i.then_inc(c_up, 1)

            def counts(b, s, turn):
                pe.wait_ge(c_hot, b + 1)
                after(pe, c_route, b - 1)
                for j in range(TB):
                    to = pp[1][:, s * 512 + j * NE:s * 512 + (j + 1) * NE]
                    pe.matmul(to, before[:, :], c_pick[:, s, j, :], start=True, stop=False)
                    for i in range(j):
                        pe.matmul(to, ones[:, :], c_pick[:, s, i, :], start=False, stop=False)
                    i = pe.matmul(to, ones[:, :], run[:, s, :], start=False, stop=True)
                i.then_inc(c_cum, 1)
            batches(pe, product1, counts)

            def turn_rows(e, s):
                pe.wait_ge(e_in[s], 64 * (e // 2 + 1) if isinstance(e, int) else 32 * (e - s) + 64)
                after(pe, e_down, e)
                for j in range(ET):
                    at = j // 4 * 512 + j % 4 * EP
                    i = pe.transpose(pp[0][:, at:at + EP], e_rows[0:EP, s, j, :], ident[0:EP, 0:EP])
                i.then_inc(e_up, 1)

            def first_product(e, s):
                pe.wait_ge(e_down, e + 1)
                for h in range(2):
                    for n in range(2):
                        after(pe, e_act, 4 * (e - 1) + 2 * h + n + 1)
                        pe.matmul(pp[1 + h][:, n * 512:n * 512 + CROWS // 2], e_w1[:, s, h * P:(h + 1) * P],
                                  e_rows_t[:, s, n * CROWS // 2:(n + 1) * CROWS // 2], start=True, stop=True)\
                            .then_inc(e_mm1, 1)

            def second_product(e, s):
                pe.wait_ge(e_act, 4 * e + 4)
                after(pe, e_yup, e)
                for j in range(ET):
                    for h in range(2):
                        i = pe.matmul(pp[3][0:EP, j * D:(j + 1) * D], e_hid[:, s, h, j * EP:(j + 1) * EP],
                                      e_w2[:, s, h, :], start=(h == 0), stop=(h == 1))
                i.then_inc(e_mm2, 1)

            turn_rows(0, 0)
            first_product(0, 0)
            turn_rows(1, 1)
            second_product(0, 0)
            with pe.Fori(1, NE // 2) as i:
                first_product(2 * i - 1, 1)
                turn_rows(2 * i, 0)
                second_product(2 * i - 1, 1)
                first_product(2 * i, 0)
                turn_rows(2 * i + 1, 1)
                second_product(2 * i, 0)
            first_product(NE - 1, 1)
            second_product(NE - 1, 1)

            def turn1(b, s, turn):
                pe.wait_ge(k_sum, b + 1)
                after(pe, k_stat, b - 1)
                for j in range(TB):
                    i = pe.transpose(node_ps[s][:, j * P:(j + 1) * P], slot[:, 4 + s, j, :], ident[:, :])
                i.then_inc(k_up, 1)
            batches(pe, turn1)
            pe.wait_ge(bn_step, BN_STEPS)
            for n in range(2):
                i = pe.matmul(pp[0][:, n * P:(n + 1) * P], bn_wide[:, n, :], ident[:, :], start=True, stop=True)
            i.then_inc(bn_up, 1)
            sums(2)

            def turn2(b, s, turn):
                pe.wait_ge(d_staged, b + 1)
                after(pe, y_ready, 2 * NB + b - 1)
                for j in range(TB):
                    i = pe.transpose(node_ps[s][:, j * P:(j + 1) * P], slot[:, 2 + s, j, :], ident[:, :])
                i.then_inc(d_up, 1)
            batches(pe, turn2)
            sums(3)

            pe.wait_ge(layer_done, 4)
            pe.wait_ge(weights3_in, 5 * 16)

            def rows3(b, s, turn):
                pe.wait_ge(r_in[s], 16 * (turn + 1))
                after(pe, r_h, b)
                after(pe, r_xt, b)
                for j in range(TB):
                    i = pe.transpose(pp[0][:, j * P:(j + 1) * P], slot[:, s, j, :], ident[:, :])
                i.then_inc(r_up, 1)
                pe.wait_ge(r_h, b + 1)
                after(pe, r_zt, b)
                for a in range(2):
                    i = pe.matmul(pp[1][:, a * 512:a * 512 + BW // 2], w1_sb[:, :],
                                  r_h_sb[:, s, a * BW // 2:(a + 1) * BW // 2], start=True, stop=True)
                i.then_inc(r_z, 1)
                pe.wait_ge(r_xt, b + 1)
                pe.wait_ge(r_zt, b + 1)
                after(pe, y_ready, 3 * NB + b - 1)
                for j in range(TB):
                    to = node_ps[s][:, j * P:(j + 1) * P]
                    pe.matmul(to, r_z_sb[:, s, j * P:(j + 1) * P], w2_sb[:, :], start=True, stop=False)
                    i = pe.matmul(to, r_xt_sb[:, s, j * P:(j + 1) * P], wres_sb[:, :], start=False, stop=True)
                i.then_inc(r_y, 1)
            batches(pe, rows3)

        @block.vector
        def _(dve):
            dve.memset(col[:, 4:5], LN_EPS)
            dve.wait_ge(edges_in, 12 * 16)
            dve.tensor_copy(dst_f[:, 0:NQ - 1, :], dst_i[:, 0:NQ - 1, :])
            dve.tensor_copy(dst_f[0:GREST, NQ - 1, :], dst_i[0:GREST, NQ - 1, :]).then_inc(prep, 1)
            dve.wait_ge(prep, 1)
            for m, q in ((P, slice(0, NQ - 1)), (GREST, slice(NQ - 1, NQ))):
                dve.tensor_reduce(g_min[0:m, q], dst_f[0:m, q, :], AX.X, ALU.min)
                i = dve.tensor_reduce(g_max[0:m, q], dst_f[0:m, q, :], AX.X, ALU.max)
            i.then_inc(prep, 1)
            dve.wait_ge(prep, 2)
            for q in range(NQ):
                m = P if q < NQ - 1 else GREST
                dve.tensor_scalar(dst_f[0:m, q, :], dst_f[0:m, q, :], g_min[0:m, q:q + 1], None, ALU.subtract)\
                    .then_inc(rel_ready, 1)
            for m, q in ((P, slice(0, NQ - 1)), (GREST, slice(NQ - 1, NQ))):
                dve.tensor_copy(g_base[0:m, q], g_min[0:m, q])
                i = dve.tensor_tensor(g_max[0:m, q], g_max[0:m, q], g_min[0:m, q], ALU.subtract)
            i.then_inc(prep, 1)
            dve.wait_ge(prep, 3)
            for m, q in ((P, slice(0, NQ - 1)), (GREST, slice(NQ - 1, NQ))):
                i = dve.tensor_copy(g_span[0:m, q], g_max[0:m, q])
            i.then_inc(prep, 1)
            dve.wait_ge(prep, 4)
            for m, q in ((P, slice(0, NQ - 1)), (GREST, slice(NQ - 1, NQ))):
                i = dve.tensor_scalar(g_extra[0:m, q], g_span[0:m, q], WIN.bit_length() - 1, None, ALU.arith_shift_right)
            i.then_inc(prep, 1)
            for q in range(NQ):
                m = P if q < NQ - 1 else GREST
                dve.wait_ge(rel_up, q + 1)
                dve.tensor_copy(rel_t[:, q * GE:q * GE + KC * m].rearrange("p (g k) -> p k g", k=KC),
                                pp[2][:, q % 2 * 512:q % 2 * 512 + 512].rearrange("p (k g) -> p k g", k=KC)[:, :, 0:m])\
                    .then_inc(rel_down, 1)
            dve.wait_ge(rel_down, NQ)
            dve.memset(rel_t[:, LAST * KC + KLAST:NCOL], -1.0)
            dve.memset(rel_t[EREST % P:P, LAST * KC + KLAST - 1:LAST * KC + KLAST], -1.0).then_inc(rel_down, 1)

            def square_sums(b, s, turn):
                dve.wait_ge(sq_made, b + 1)
                dve.tensor_reduce(small[:, 0, tiles(b)], slot[:, 4 + s, :, :], AX.X, ALU.add).then_inc(sq_summed, 1)
            batches(dve, square_sums)
            dve.wait_ge(a_act, 1)
            dve.tensor_scalar(small[:, 1, :], small[:, 1, :], EPS_NORM, None, ALU.max).then_inc(a_dve, 1)
            dve.wait_ge(a_dve, 1)
            dve.reciprocal(small[:, 3, :], small[:, 1, :]).then_inc(a_dve, 1)
            dve.wait_ge(a_act, 2)
            dve.wait_ge(a_dve, 2)
            dve.tensor_tensor(small[:, 4, :], small[:, 2, :], small[:, 3, :], ALU.mult).then_inc(a_dve, 1)
            dve.wait_ge(a_dve, 3)
            dve.tensor_tensor(small[:, 5, :], small[:, 4, :], small[:, 4, :], ALU.mult).then_inc(a_dve, 1)
            dve.wait_ge(a_dve, 4)
            dve.tensor_tensor(small[:, 5, :], small[:, 5, :], small[:, 0, :], ALU.mult).then_inc(a_dve, 1)
            dve.wait_ge(a_dve, 5)
            dve.tensor_scalar(small[:, 5, :], small[:, 5, :], -1.0, 1.0, ALU.mult, ALU.add).then_inc(a_dve, 1)
            dve.wait_ge(a_dve, 6)
            dve.tensor_scalar(small[:, 5, :], small[:, 5, :], EPS_NORM, None, ALU.max).then_inc(a_dve, 1)
            dve.wait_ge(a_dve, 7)
            dve.reciprocal(small[:, 6, :], small[:, 5, :]).then_inc(a_dve, 1)
            dve.wait_ge(a_dve, 8)
            dve.scalar_tensor_tensor(small[:, 7, :], small[:, 6, :], 2.0, small[:, 4, :], ALU.mult, ALU.mult)
            dve.tensor_scalar(small[:, 8, :], small[:, 6, :], 2.0, -1.0, ALU.mult, ALU.add).then_inc(a_dve, 1)
            dve.wait_ge(a_dve, 9)

            def table0_rows(b, s, turn):
                after(dve, table_stored0[s], 16 * turn)
                for j in range(TB):
                    dve.tensor_scalar(tab0[:, s, j, 0:D], X[:, b * TB + j, :], small[:, 7, ds(b * TB + j, 1)], None, ALU.mult)
                dve.memset(tab0[:, s, :, D + 1], 1.0)
                dve.tensor_copy(tab0[:, s, :, D], small[:, 8, tiles(b)]).then_inc(row_made, 1)
            batches(dve, table0_rows)

            dve.wait_ge(weights_in, 9 * 16)
            dve.tensor_copy(bn_wide[:, 0, :], col[:, 0:1].to_broadcast([P, P])).then_inc(w_dve, 1)
            dve.wait_ge(w_pe, 2)
            dve.tensor_copy(w_gcn[:, D:D + NE], pp[1][:, 512:512 + NE])
            dve.tensor_tensor(gateb_bc[:, :], gateb_bc[:, :], pp[1][:, 512 + NE:512 + 2 * NE], ALU.add).then_inc(w_dve, 1)

            dve.wait_ge(numbers_in, 32)
            dve.tensor_copy(extra_f[:, :], extra_row[:, :]).then_inc(prep, 1)
            dve.wait_ge(prep, PREP_STEPS + 1)
            dve.tensor_reduce(extra_f[:, 0:1], extra_f[:, :], AX.X, ALU.max).then_inc(prep, 1)
            dve.wait_ge(prep, PREP_STEPS + 2)
            dve.tensor_copy(any_extra[:, :], extra_f[:, 0:1]).then_inc(prep, 1)

            dve.wait_ge(consts_made, 10)
            dve.wait_ge(bases_in, 16)
            dve.wait_ge(numbers_out, 64)
            dve.wait_ge(src_up, NQ)
            dve.wait_ge(w_up, NQ)
            dve.wait_ge(src_down, NQ)
            dve.wait_ge(rel_down, NQ + 1)
            dve.tensor_tensor(dst_n.rearrange("p (g k) -> p g k", k=KC), rel_t[:, :].rearrange("p (g k) -> p g k", k=KC),
                              base_bc.unsqueeze(2).to_broadcast([P, NG, KC]), ALU.add).then_inc(bits_ready, 1)
            dve.wait_ge(bits_ready, 1)
            shift = P.bit_length() - 1
            dve.tensor_scalar(bits_hi, dst_n, shift, None, ALU.arith_shift_right)
            dve.tensor_scalar(bits_lo, dst_n, P - 1, None, ALU.bitwise_and).then_inc(bits_ready, 1)
            dve.wait_ge(bits_ready, 2)
            dve.tensor_copy(dst_hi, bits_hi)
            dve.tensor_copy(dst_lo, bits_lo).then_inc(bits_ready, 1)
            dve.wait_ge(bits_ready, 3)
            dve.memset(dst_lo[:, LAST * KC + KLAST:NCOL], -1.0)
            dve.memset(dst_lo[EREST % P:P, LAST * KC + KLAST - 1:LAST * KC + KLAST], -1.0)
            dve.tensor_scalar(bits_lo, src_t[:, :], P - 1, None, ALU.bitwise_and)
            dve.tensor_scalar(bits_hi, src_t[:, :], -P, None, ALU.bitwise_and).then_inc(bits_ready, 1)
            dve.wait_ge(bits_ready, 4)
            dve.tensor_copy(edge_cols[:, 0, :], bits_hi)
            dve.tensor_copy(edge_cols[:, 1, :], bits_lo)
            dve.tensor_copy(edge_cols[:, 2, :], rel_t[:, :])
            dve.tensor_scalar(less_dump, src_t[:, :], col[:, 6:7], None, ALU.subtract).then_inc(bits_ready, 1)
            dve.wait_ge(bits_ready, 5)

            def by_source(g, cs, es, hs):
                dve.tensor_tensor(same[:, es, :, :], src_ps[cs].rearrange("p (k e) -> p k e", k=KC),
                                  src_t[:, ds(g * KC, KC)].unsqueeze(2).to_broadcast([P, KC, P]), ALU.is_equal)
                return dve.tensor_scalar(hot0[:, hs, :, :].rearrange("p k e -> p (k e)"), rel_ps, col[:, 5:6], None, ALU.is_equal)

            def count_later(es, ls):
                for k in range(KC):
                    i = dve.tensor_tensor_reduce(unread[:, k, :], same[:, es, k, :], before[:, :], 1.0, 0.0, ALU.mult, ALU.add,
                                                 accum_out=later[:, ls, k:k + 1])
                return i

            def route_last(g, ls):
                return dve.scalar_tensor_tensor(keep, later[:, ls, :], 0.0, less_dump[:, ds(g * KC, KC)], ALU.is_equal, ALU.mult)

            def columns(g, s):
                after(dve, spread, g - 1)
                dve.tensor_copy(cols[:, s % 2, :, :], edge_cols[:, :, ds(g * KC, KC)]).then_inc(cols_ready, 1)

            ROUTE = 2

            def compare(g, s, turn):
                if there(g + 1):
                    columns(g + 1, (s + 1) % SLOTS)
                dve.wait_ge(spread, g + 1)
                after(dve, combined, g - 2)
                after(dve, taken, g - 1)
                by_source(g, s % 2, s % 3, s % 2).then_inc(hot0_ready, 1)
                dve.wait_ge(hot0_ready, g + 1)
                count_later(s % 3, s % 2).then_inc(route_step, 1)
                after(dve, hist_summed, g - 1)
                for k in range(KC):
                    dve.tensor_scalar(hot_lo[:, s % 2, k, :], iota_b[:, :], dst_lo[:, ds(g * KC + k, 1)], None, ALU.is_equal)
                    i = dve.tensor_scalar(hot_hi[:, s % 2, k, :], iota_b[:, 0:NT], dst_hi[:, ds(g * KC + k, 1)], None, ALU.is_equal)
                i.then_inc(hist_ready, 1)
                dve.wait_ge(route_step, ROUTE * g + 1)
                route_last(g, s % 2).then_inc(route_step, 1)
                after(dve, rows_ready, g - 2)
                dve.wait_ge(route_step, ROUTE * g + 2)
                dve.tensor_scalar(idx[:, s, :], keep, col[:, 6:7], None, ALU.add).then_inc(route0, 1)

            def step(i):
                i.then_inc(z_step, 1)
                take(dve, z_step)

            def begin_extra(g):
                step(dve.tensor_copy(rel_x[:, :], rel_t[:, ds(g * KC, KC)]))

            def compare_extra(g, j):
                step(dve.tensor_scalar(rel_x[:, :], rel_x[:, :], -float(WIN), None, ALU.add))
                dve.sem_inc(z_go, 1)
                dve.tensor_copy(cols[:, 0, 0:2, :], edge_cols[:, 0:2, ds(g * KC, KC)])
                dve.tensor_copy(cols[:, 0, 2, :], rel_x[:, :]).then_inc(z_cols, 1)
                take(dve, z_spread)
                step(by_source(g, 0, 0, 0))
                step(count_later(0, 0))
                step(route_last(g, 0))
                dve.tensor_scalar(idx[:, 0, :], keep, col[:, 6:7], None, ALU.add).then_inc(z_hot, 1)
                take(dve, z_done)

            columns(0, 0)
            rounds(dve, compare)
            extra_windows(dve, compare_extra, begin_extra)
            dve.sem_inc(layer_done, 1)

            def sums(layer):
                bases = {}

                def load_bases(turn):
                    for s in range(SLOTS):
                        bases[s] = dve.value_load(base_row[0:1, ds(turn * SLOTS + s, 1)], min_val=0, max_val=N - 1)

                def make_hot(g, s):
                    after(dve, summed, (layer - 1) * NG + g - 2)
                    for k in range(KC):
                        i = dve.tensor_scalar(hot[:, s % 3, k, :], iota[:, :], rel_t[:, ds(g * KC + k, 1)], None, ALU.is_equal)
                    i.then_inc(hot_ready, 1)
                def add_window(at, base):
                    return dve.tensor_tensor(acc[:, ds(base, WIN)], acc[:, ds(base, WIN)], win[at][:, 0:WIN], ALU.add)

                def body(g, s, turn):
                    make_hot(g + 1, (s + 1) % SLOTS)
                    dve.wait_ge(summed, (layer - 1) * NG + g + 1)
                    after(dve, added, (layer - 1) * NG + g)
                    add_window(s % 3, bases[s]).then_inc(added, 1)

                dve.wait_ge(acc_zero, 1)
                dve.wait_ge(cleared, layer * NB)
                for n in range(2):
                    dve.wait_ge(tab_stored[n], 16 * layer * STORES)
                make_hot(0, 0)
                groups(dve, body, begin=load_bases)
                base = dve.value_load(base_row[0:1, LAST:NG], min_val=0, max_val=N - 1)
                dve.wait_ge(summed, layer * NG)
                dve.wait_ge(added, (layer - 1) * NG + LAST)
                add_window(LAST % 3, base).then_inc(added, 1)

                dve.wait_ge(added, layer * NG)
                flag = dve.value_load(any_extra[0:1, 0:1], min_val=0, max_val=NT)
                with dve.If(flag > 0):
                    with dve.Fori(0, NG) as g:
                        n = dve.value_load(extra_row[0:1, ds(g, 1)], min_val=0, max_val=NT)
                        with dve.If(n > 0):
                            first = dve.value_load(base_row[0:1, ds(g, 1)], min_val=0, max_val=N - 1)
                            dve.tensor_copy(idx_x[:, :], src_t[:, ds(g * KC, KC)]).then_inc(x_idx, 1)
                            dve.tensor_copy(rel_x[:, :], rel_t[:, ds(g * KC, KC)]).then_inc(x_step, 1)
                            dve.wait_ge(x_msg, 16 * KC)
                            dve.sem_clear(x_msg)
                            dve.wait_ge(x_step, 1)
                            dve.sem_clear(x_step)
                            with dve.Fori(0, n) as j:
                                dve.tensor_scalar(rel_x[:, :], rel_x[:, :], -float(WIN), None, ALU.add).then_inc(x_step, 1)
                                dve.wait_ge(x_step, 1)
                                dve.sem_clear(x_step)
                                for k in range(KC):
                                    i = dve.tensor_scalar(hot[:, 0, k, :], iota[:, :], rel_x[:, k:k + 1], None, ALU.is_equal)
                                i.then_inc(x_hot, 1)
                                dve.wait_ge(x_sum, 1)
                                dve.sem_clear(x_sum)
                                at = nc.s_assert_within(first + WIN * (j + 1), WIN, N - 1,
                                                        skip_runtime_bounds_check_because="no window begins beyond the group's last node")
                                add_window(0, at).then_inc(x_step, 1)
                                dve.wait_ge(x_step, 1)
                                dve.sem_clear(x_step)
                dve.sem_inc(layer_done, 1)

            def moments(layer, y):
                def body(b, s, turn):
                    dve.wait_ge(y_ready, layer * NB + b + 1)
                    for j in range(TB):
                        i = dve.bn_stats(stat[:, s, j, :], slot[:, y + s, j, :])
                    i.then_inc(stat_ready, 1)
                    apart(dve, stat_ready, layer * NB + b + 1)
                    for j in range(TB):
                        i = dve.bn_aggr(mv[:, s, j, :], stat[:, s, j, :])
                    i.then_inc(mv_ready, 1)
                return body

            def normal(layer, y):
                def body(b, s, turn):
                    dve.wait_ge(sd_ready, layer * NB + b + 1)
                    dve.reciprocal(sd[:, s, :], sd[:, s, :]).then_inc(rstd_ready, 1)
                    dve.wait_ge(rstd_ready, layer * NB + b + 1)
                    for j in range(TB):
                        i = dve.tensor_scalar(X[:, b * TB + j, :], slot[:, y + s, j, :], mv[:, s, j, 0:1], sd[:, s, j:j + 1],
                                              ALU.subtract, ALU.mult)
                    i.then_inc(x_ready, 1)
                return body

            def stage0(b, s, turn):
                dve.wait_ge(sum_in[s], 16 * KC * (turn + 1))
                dve.tensor_tensor(parts0[:, s, 0:2, :, :], parts0[:, s, 0:2, :, :], parts0[:, s, 2:4, :, :], ALU.add)\
                    .then_inc(half_staged, 1)
                dve.wait_ge(half_staged, b + 1)
                dve.tensor_tensor(parts0[:, s, 0, :, :], parts0[:, s, 0, :, :], parts0[:, s, 1, :, :], ALU.add).then_inc(staged, 1)

            def norms0(b, s, turn):
                dve.wait_ge(evacuated, b + 1)
                dve.tensor_reduce(small[:, 0, tiles(b)], slot[:, 4 + s, :, :], AX.X, ALU.add)
                dve.tensor_copy(deg[:, tiles(b), :], parts0[:, s, 0, :, D:T0W]).then_inc(reduced, 1)
            batches(dve, stage0, norms0)
            dve.wait_ge(reduced, NB)
            dve.wait_ge(hist_summed, NG)
            den, count = deg[:, :, 0], hist
            dve.tensor_scalar(small[:, 2, :], den, 0.0, 2.0, ALU.is_ge, ALU.mult)
            dve.scalar_tensor_tensor(small[:, 3, :], den, -1.0, den, ALU.mult, ALU.max).then_inc(b_dve, 1)
            dve.wait_ge(b_dve, 1)
            dve.tensor_scalar(small[:, 3, :], small[:, 3, :], EPS_DEN, None, ALU.max).then_inc(b_dve, 1)
            dve.wait_ge(b_dve, 2)
            dve.reciprocal(small[:, 4, :], small[:, 3, :]).then_inc(b_dve, 1)
            dve.wait_ge(b_dve, 3)
            dve.scalar_tensor_tensor(small[:, 5, :], small[:, 2, :], -1.0, small[:, 4, :], ALU.add, ALU.mult).then_inc(b_dve, 1)
            dve.wait_ge(b_act, 1)
            dve.tensor_tensor(small[:, 6, :], small[:, 4, :], small[:, 1, :], ALU.mult).then_inc(b_dve, 1)
            dve.wait_ge(b_dve, 5)
            dve.tensor_scalar(small[:, 6, :], small[:, 6, :], EPS_NORM, None, ALU.max).then_inc(b_dve, 1)
            dve.tensor_scalar(small[:, 7, :], count, 1.0, None, ALU.max)
            dve.tensor_scalar(small[:, 9, :], count, 1.0, None, ALU.add).then_inc(b_dve, 1)
            dve.wait_ge(b_dve, 7)
            dve.tensor_scalar(small[:, 13, :], small[:, 6, :], CLIP, None, ALU.min).then_inc(b_dve, 1)
            dve.wait_ge(b_dve, 8)
            dve.tensor_scalar(small[:, 14, :], small[:, 13, :], -1.0, 1.0, ALU.mult, ALU.add).then_inc(b_dve, 1)
            dve.wait_ge(b_dve, 9)
            dve.reciprocal(small[:, 15, :], small[:, 14, :]).then_inc(b_dve, 1)
            dve.wait_ge(b_dve, 10)
            dve.scalar_tensor_tensor(small[:, 11, :], small[:, 13, :], 1.0, small[:, 15, :], ALU.add, ALU.mult).then_inc(b_dve, 1)
            dve.reciprocal(small[:, 16, :], small[:, 6, :]).then_inc(b_dve, 1)
            dve.wait_ge(b_dve, 12)
            dve.tensor_tensor(small[:, 16, :], small[:, 16, :], small[:, 5, :], ALU.mult).then_inc(b_dve, 1)
            dve.wait_ge(b_act, 4)
            dve.wait_ge(b_dve, 13)
            dve.scalar_tensor_tensor(small[:, 17, :], small[:, 12, :], 0.25, small[:, 16, :], ALU.mult, ALU.mult)
            dve.reciprocal(in_scale[:, 0, :], small[:, 8, :])
            dve.reciprocal(in_scale[:, 1, :], small[:, 10, :]).then_inc(b_dve, 1)
            dve.wait_ge(b_dve, 14)

            def residual0(b, s, turn):
                after(dve, x_ready, b - 1)
                for j in range(TB):
                    i = dve.scalar_tensor_tensor(slot[:, s, j, :], acc[:, ds((b * TB + j) * P, P)], small[:, 17, ds(b * TB + j, 1)],
                                                 X[:, b * TB + j, :], ALU.mult, ALU.add)
                i.then_inc(y_ready, 1)
                moments(0, 0)(b, s, turn)
            batches(dve, residual0, normal(0, 0))

            sums(1)
            dve.wait_ge(layer_done, 2)
            dve.tensor_scalar(small[:, 0, :], deg[:, :, 1], 1.0, None, ALU.add).then_inc(degree, 1)

            C_BODY, C_LATE = 7, 5

            def route(b, s, turn):
                own = lambda n: dve.wait_ge(c_step, C_BODY * b + n)
                after(dve, c_up, b - 1)
                dve.tensor_copy(slot_w[:, s, :], acc[:, ds(b * BW, BW)]).then_inc(c_staged, 1)
                after(dve, sent[s], 16 * 2 * TB * turn)
                after(dve, c_kept, b - 1)
                dve.wait_ge(c_up, b + 1)
                for j in range(TB):
                    i = dve.scalar_tensor_tensor(slot[:, 2 + s, j, :], node_ps[s][:, j * P:(j + 1) * P],
                                                 in_scale[:, 0, ds(b * TB + j, 1)], bconv_bc[:, :], ALU.mult, ALU.add)
                i.then_inc(c_new, 1)
                for j in range(TB):
                    i = dve.scalar_tensor_tensor(c_score[:, s, j, :], pp[0][:, s * 512 + j * NE:s * 512 + (j + 1) * NE],
                                                 in_scale[:, 0, ds(b * TB + j, 1)], gateb_bc[:, :], ALU.mult, ALU.add)
                i.then_inc(c_step, 1)
                apart(dve, c_step, C_BODY * b + 1)
                for j in range(TB):
                    i = dve.max(c_top[:, s, j, :], c_score[:, s, j, :])
                i.then_inc(c_step, 1)
                own(2)
                dve.tensor_tensor(c_small[:, s, 0, 0:TB], c_top[:, s, :, 1], c_top[:, s, :, 0], ALU.subtract).then_inc(c_scores, 1)
                for j in range(TB):
                    i = dve.max_index(c_at[:, s, j, :], c_top[:, s, j, :], c_score[:, s, j, :])
                i.then_inc(c_step, 1)
                own(3)
                dve.tensor_copy(c_small[:, s, 2, :].rearrange("p (k j) -> p k j", k=2),
                                c_at[:, s, :, 0:2].rearrange("p j k -> p k j")).then_inc(c_step, 1)
                own(4)
                for k in range(2):
                    i = dve.tensor_tensor(c_one[:, s, k, :, :], iota[:, 0:NE].unsqueeze(1).to_broadcast([P, TB, NE]),
                                          c_small[:, s, 2, k * TB:(k + 1) * TB].unsqueeze(2).to_broadcast([P, TB, NE]), ALU.is_equal)
                i.then_inc(c_step, 1)
                own(5)
                dve.tensor_tensor(c_pick[:, s, :, :], c_one[:, s, 0, :, :], c_one[:, s, 1, :, :], ALU.add).then_inc(c_hot, 1)
                dve.wait_ge(c_hot, b + 1)
                dve.tensor_reduce(c_sum, c_pick[:, s, :, :].rearrange("p j e -> p e j"), AX.X, ALU.add).then_inc(c_step, 1)
                own(6)
                after(dve, c_cum, b)
                dve.tensor_tensor(run[:, 1 - s, :], run[:, s, :], c_sum, ALU.add).then_inc(c_step, 1)

            def place(b, s, turn):
                own = lambda n: dve.wait_ge(c_late, C_LATE * b + n)
                top, pos, valid, kept, row, prob = (c_small[:, s, n, :] for n in (2, 3, 4, 5, 6, 7))
                by_node = lambda t: t.rearrange("p j k -> p k j")
                two = lambda t: t.rearrange("p (k j) -> p k j", k=2)
                dve.wait_ge(c_cum, b + 1)
                dve.wait_ge(c_hot, b + 1)
                for k in range(2):
                    i = dve.tensor_tensor(c_prod[:, s, k, :, :], pp[1][:, s * 512:s * 512 + TB * NE].rearrange("p (j e) -> p j e", j=TB),
                                          c_one[:, s, k, :, :], ALU.mult)
                i.then_inc(c_late, 1)
                own(1)
                for k in range(2):
                    i = dve.tensor_reduce(pos[:, k * TB:(k + 1) * TB], c_prod[:, s, k, :, :], AX.X, ALU.add)
                dve.wait_ge(c_exp, b + 1)
                dve.tensor_scalar(prob[:, 0:TB], c_small[:, s, 1, 0:TB], 1.0, None, ALU.add).then_inc(c_late, 1)
                own(2)
                dve.tensor_scalar(valid, pos, float(CAP), None, ALU.is_lt)
                dve.reciprocal(prob[:, 0:TB], prob[:, 0:TB])
                dve.scalar_tensor_tensor(row, top, float(CROWS), pos, ALU.mult, ALU.add).then_inc(c_late, 1)
                own(3)
                dve.tensor_tensor(prob[:, TB:2 * TB], prob[:, 0:TB], c_small[:, s, 1, 0:TB], ALU.mult)
                dve.tensor_scalar(c_small[:, s, 8, :], valid, -float(FAR), float(FAR), ALU.mult, ALU.add)
                dve.tensor_tensor(kept, pos, valid, ALU.mult).then_inc(c_late, 1)
                own(4)
                dve.tensor_tensor(by_node(gate[:, tiles(b), :]), two(prob), two(valid), ALU.mult)
                dve.scalar_tensor_tensor(by_node(pair_row[:, tiles(b), :]), two(top), float(CROWS), two(kept), ALU.mult, ALU.add)\
                    .then_inc(c_late, 1)
                dve.tensor_tensor(by_node(send_row[:, s, :].rearrange("p (j k) -> p j k", k=2)), two(row),
                                  two(c_small[:, s, 8, :]), ALU.add).then_inc(c_route, 1)
            batches(dve, route, place)
            dve.wait_ge(degree_sqrt, 1)
            dve.reciprocal(in_scale[:, 2, :], small[:, 1, :]).then_inc(degree, 1)
            dve.wait_ge(degree, 2)
            dve.tensor_tensor(self_scale[:, :], in_scale[:, 1, :], in_scale[:, 2, :], ALU.mult).then_inc(degree, 1)
            dve.wait_ge(degree, 3)
            dve.tensor_scalar(self_scale[:, :], self_scale[:, :], 1.0, None, ALU.add).then_inc(degree, 1)

            def expert_rows(e, s):
                dve.wait_ge(e_up, e + 1)
                after(dve, e_mm1, 4 * (e - 1))
                dve.tensor_copy(e_rows_t[:, s, 0:4 * EP], pp[0][:, 0:4 * EP])
                dve.tensor_copy(e_rows_t[:, s, 4 * EP:CROWS], pp[0][:, 512:512 + (ET - 4) * EP]).then_inc(e_down, 1)

            def expert_answer(e, s):
                dve.wait_ge(e_mm2, e + 1)
                after(dve, e_out[s], 16 * (e // 2) if isinstance(e, int) else 8 * (e - s))
                dve.tensor_tensor(e_y[0:EP, s, :, :], pp[3][0:EP, 0:ET * D].rearrange("p (t d) -> p t d", d=D),
                                  e_b2[0:EP, s, :].unsqueeze(1).to_broadcast([EP, ET, D]), ALU.add).then_inc(e_yup, 1)
            expert_rows(0, 0)
            expert_rows(1, 1)
            expert_answer(0, 0)
            expert_rows(2, 0)
            expert_answer(1, 1)
            with dve.Fori(1, NE // 2 - 1) as i:
                expert_rows(2 * i + 1, 1)
                expert_answer(2 * i, 0)
                expert_rows(2 * i + 2, 0)
                expert_answer(2 * i + 1, 1)
            expert_rows(NE - 1, 1)
            expert_answer(NE - 2, 0)
            expert_answer(NE - 1, 1)

            def rows_of(b, s, turn):
                after(dve, k_in[s], 16 * 2 * TB * turn)
                dve.wait_ge(c_late, C_LATE * NB)
                dve.tensor_copy(fetch_row[:, s, :].rearrange("p (j k) -> p j k", k=2), pair_row[:, tiles(b), :]).then_inc(k_idx, 1)

            def combine(b, s, turn):
                dve.wait_ge(k_in[s], 16 * 2 * TB * (turn + 1))
                after(dve, k_kept, b - 1)
                after(dve, k_up, b - 1)
                for j in range(TB):
                    i = dve.scalar_tensor_tensor(slot[:, 4 + s, j, :], slot[:, 2 * s, j, :], gate[:, b * TB + j, 0:1],
                                                 acc[:, ds((b * TB + j) * P, P)], ALU.mult, ALU.add)
                i.then_inc(k_half, 1)
                dve.wait_ge(k_half, b + 1)
                for j in range(TB):
                    i = dve.scalar_tensor_tensor(slot[:, 4 + s, j, :], slot[:, 2 * s + 1, j, :], gate[:, b * TB + j, 1:2],
                                                 slot[:, 4 + s, j, :], ALU.mult, ALU.add)
                i.then_inc(k_sum, 1)
                dve.wait_ge(k_up, b + 1)
                for a in range(2):
                    n = BW // 2 if not isinstance(b, int) or b < NB - 1 or a == 0 else LASTN - BW // 2
                    i = dve.bn_stats(bn_stat[:, 2 * b + a, :], node_ps[s][:, a * BW // 2:a * BW // 2 + n])
                i.then_inc(k_stat, 1)
            dve.wait_ge(c_kept, NB)
            batches(dve, rows_of, combine)
            dve.wait_ge(k_stat, NB)
            dve.bn_aggr(bn_mv[:, 0:2], bn_stat[:, :, :]).then_inc(bn_step, 1)
            dve.wait_ge(bn_sd, 1)
            dve.reciprocal(bn_mv[:, 2:3], bn_mv[:, 2:3]).then_inc(bn_step, 1)
            dve.wait_ge(bn_step, 2)
            dve.tensor_tensor(bn_mv[:, 3:4], bn_mv[:, 2:3], col[:, 1:2], ALU.mult).then_inc(bn_step, 1)
            dve.wait_ge(bn_step, 3)
            dve.tensor_tensor(bn_mv[:, 2:3], bn_mv[:, 0:1], bn_mv[:, 3:4], ALU.mult).then_inc(bn_step, 1)
            dve.wait_ge(bn_step, 4)
            dve.tensor_tensor(bn_mv[:, 2:3], col[:, 2:3], bn_mv[:, 2:3], ALU.subtract).then_inc(bn_step, 1)
            dve.wait_ge(bn_step, 5)
            dve.tensor_copy(bn_wide[:, 0, :], bn_mv[:, 3:4].to_broadcast([P, P]))
            dve.tensor_copy(bn_wide[:, 1, :], bn_mv[:, 2:3].to_broadcast([P, P])).then_inc(bn_step, 1)
            dve.wait_ge(bn_up, 1)
            dve.tensor_copy(bn_bc[:, :, :], pp[0][:, 0:2 * P].rearrange("p (n d) -> p n d", n=2)).then_inc(bn_done, 1)
            dve.wait_ge(bn_done, 1)
            dve.wait_ge(k_kept, NB)

            def residual1(b, s, turn):
                dve.wait_ge(x_ready, NB + b - 1)
                dve.tensor_tensor(slot[:, s, :, :], acc[:, ds(b * BW, BW)].rearrange("p (t d) -> p t d", d=D),
                                  bn_bc[:, 0, :].unsqueeze(1).to_broadcast([P, TB, D]), ALU.mult).then_inc(n_prod, 1)
                dve.wait_ge(n_prod, b + 1)
                dve.wait_ge(n_shift, b + 1)
                dve.tensor_tensor(slot[:, s, :, :], slot[:, s, :, :], slot[:, 4 + s, :, :], ALU.add).then_inc(y_ready, 1)
                moments(1, 0)(b, s, turn)
            batches(dve, residual1, normal(1, 0))

            sums(2)
            dve.wait_ge(layer_done, 3)

            def stage2(b, s, turn):
                after(dve, d_up, b - 1)
                dve.tensor_copy(slot_w[:, 2 + s, :], acc[:, ds(b * BW, BW)]).then_inc(d_staged, 1)

            def residual2(b, s, turn):
                dve.wait_ge(x_ready, 2 * NB + b - 1)
                dve.wait_ge(d_up, b + 1)
                dve.wait_ge(d_self, b + 1)
                for j in range(TB):
                    i = dve.scalar_tensor_tensor(slot[:, s, j, :], node_ps[s][:, j * P:(j + 1) * P], in_scale[:, 2, ds(b * TB + j, 1)],
                                                 slot[:, 4 + s, j, :], ALU.mult, ALU.add)
                i.then_inc(y_ready, 1)
                moments(2, 0)(b, s, turn)
            batches(dve, stage2, residual2, normal(2, 0))

            sums(3)
            dve.wait_ge(layer_done, 4)
            dve.wait_ge(weights3_in, 5 * 16)
            dve.tensor_tensor(bias_bc, bias_bc, bres_bc, ALU.add).then_inc(bias_ready, 1)

            def stage3(b, s, turn):
                dve.wait_ge(r_xt, b + 1)
                after(dve, r_z, b - 1)
                dve.tensor_tensor(r_h_sb[:, s, :], acc[:, ds(b * BW, BW)], pp[0][:, 0:BW], ALU.add).then_inc(r_h, 1)

            def residual3(b, s, turn):
                dve.wait_ge(x_ready, 3 * NB + b - 1)
                dve.wait_ge(r_y, b + 1)
                dve.wait_ge(r_xb, b + 1)
                dve.tensor_tensor(slot_w[:, 2 + s, :], node_ps[s][:, 0:BW], slot_w[:, 5 + s, :], ALU.add).then_inc(y_ready, 1)
                moments(3, 2)(b, s, turn)
            batches(dve, stage3, residual3, normal(3, 2))


INPUTS = ["x", "src", "dst", "edge_weight", "L1_gnn_W_conv", "L1_gnn_b_conv", "L1_gnn_gate_W", "L1_gnn_gate_b",
          "L1_gnn_W1", "L1_gnn_b1", "L1_gnn_W2", "L1_gnn_b2", "L1_gnn_bn_gamma", "L1_gnn_bn_beta",
          "L3_gnn_W1", "L3_gnn_b1", "L3_gnn_W2", "L3_gnn_b2", "L3_gnn_Wres", "L3_gnn_bres"]


def kernel(**inputs):
    import numpy as np
    import concourse.bacc as bacc
    from concourse.bass_utils import run_bass_kernel_spmd

    nc = bacc.Bacc("TRN2", target_bir_lowering=False, num_devices=1)
    arrays, args = {}, []
    for name in INPUTS:
        a = np.ascontiguousarray(inputs[name])
        arrays[f"in_{name}"] = a
        args.append(nc.dram_tensor(f"in_{name}", a.shape, mybir.dt.from_np(a.dtype), kind="ExternalInput").ap())
    out = nc.dram_tensor("out", (N, D), mybir.dt.float32, kind="ExternalOutput").ap()
    program(nc, *args, out)
    result = run_bass_kernel_spmd(nc, [arrays], core_ids=[0])
    return result.results[0]["out"]
```

```python
from contextlib import ExitStack

import concourse.bass as bass
from concourse import mybir

N, D, E = 12500, 128, 200000
P = 128
NT = -(-N // P)
NPAD = NT * P
TB = 7
NB = NT // TB
BW = TB * P
LASTN = N - (NB - 1) * BW
KC = 4
GE = KC * P
NG = -(-E // GE)
NCOL = NG * KC
EREST = E - (NG - 1) * GE
KLAST = -(-EREST // P)
NQ = -(-NG // P)
GREST = NG - (NQ - 1) * P
SLOTS = 6
TURNS = (NG - 1) // SLOTS
WIN = P
ACCW = NPAD + WIN
T0W = D + 2
NE, DH = 64, 256
CAP = 2 * (-(-2 * N // NE))
ET = 8
EP = -(-CAP // ET)
CROWS = ET * EP
UT = 4
UROWS = UT * EP
UPE = ET // UT
QUAD = 4
EROWS = NE * CROWS + QUAD * UROWS
FAR = 1 << 20
EPS_NORM, EPS_DEN, CLIP = 1e-15, 1e-10, 1.0 - 1e-07
LN_EPS = BN_EPS = 1e-05
assert NB * TB == NT and TURNS * SLOTS + 1 == NG and EREST % 64 == 0


def program(nc, x, src, dst, edge_weight, W_conv, b_conv, gate_W, gate_b, W1e, b1e, W2e, b2e,
            bn_gamma, bn_beta, W1, b1, W2, b2, Wres, bres, out):
    f32, bf16, i32, u32 = mybir.dt.float32, mybir.dt.bfloat16, mybir.dt.int32, mybir.dt.uint32
    ALU, ACT, AX = mybir.AluOpType, mybir.ActivationFunctionType, mybir.AxisListType
    ds = bass.ds
    ctx = ExitStack()
    with ctx:
        def sb(name, shape, dt=f32):
            return ctx.enter_context(nc.sbuf_tensor(name, shape, dt))

        def sem(name):
            return ctx.enter_context(nc.semaphore(name))

        table0 = nc.dram_tensor("table0", [NPAD + WIN, T0W], f32).ap()
        tables = [table0] + [nc.dram_tensor(f"table{n}", [NPAD, D], f32).ap() for n in (1, 2, 3)]
        sums0 = [nc.dram_tensor(f"sums0_{k}", [NPAD + P, T0W], f32).ap() for k in range(KC)]
        expert_rows = nc.dram_tensor("expert_rows", [EROWS, D], f32).ap()
        group_numbers = nc.dram_tensor("group_numbers", [2, NQ * P], i32).ap()

        X = sb("X", [P, NT, D])
        acc = sb("acc", [P, ACCW])
        shared = sb("shared", [P, ACCW])
        work = sb("work", [P, 6272])
        src_t = sb("src_t", [P, NCOL], i32)
        rel_t = sb("rel_t", [P, NCOL])
        w_t = sb("w_t", [P, NCOL])
        base_row = sb("base_row", [1, NG], i32)
        extra_row = sb("extra_row", [1, NG], i32)
        any_extra = sb("any_extra", [1, 1], i32)
        idx = sb("idx", [P, SLOTS, KC], i32)
        ident = sb("ident", [P, P])
        iota = sb("iota", [P, P])
        iota_b = sb("iota_b", [P, P], bf16)
        before = sb("before", [P, P])
        ones = sb("ones", [P, P])
        zeros = sb("zeros", [P, T0W])
        small = sb("small", [P, 18, NT])
        w_gcn = sb("w_gcn", [P, D + NE])
        col = sb("col", [P, 8])
        bconv_bc = sb("bconv_bc", [P, D])
        gateb_bc = sb("gateb_bc", [P, NE])
        b1_t = sb("b1_t", [P, 2, NE])
        bn_mv = sb("bn_mv", [P, 4])
        bn_wide = sb("bn_wide", [P, 2, P])
        run = sb("run", [P, 2, NE])
        mv = sb("mv", [P, 2, TB, 2])
        sd = sb("sd", [P, 2, TB])
        off = sb("off", [P, 2, TB])

        def part(t, at, shape, dt=None):
            n = 1
            for m in shape:
                n *= m
            v = t[:, at:at + (n // 2 if dt is bf16 else n)]
            if dt is not None:
                v = v.bitcast(dt)
            names = "abcd"[:len(shape)]
            if len(shape) == 1:
                return v
            sizes = {c: m for c, m in zip(names[1:], shape[1:])}
            return v.rearrange(f"p ({' '.join(names)}) -> p {' '.join(names)}", **sizes)

        deg = part(w_t, 0, (NT, 2))
        gate = part(w_t, 2 * NT, (NT, 2))
        pair_row = part(w_t, 4 * NT, (NT, 2), i32)
        self_scale = part(w_t, 6 * NT, (NT,))
        in_scale = part(w_t, 7 * NT, (3, NT))
        bn_bc = part(w_t, 10 * NT, (2, D))
        bn_stat = part(w_t, 10 * NT + 2 * D, (2 * NB, 6))
        send_row = part(w_t, 10 * NT + 2 * D + 12 * NB, (2, 2 * TB), i32)
        fetch_row = part(w_t, 10 * NT + 2 * D + 12 * NB + 4 * TB, (2, 2 * TB), i32)
        stat = part(w_t, 10 * NT + 2 * D + 12 * NB + 8 * TB, (2, TB, 6))
        dst_i = part(shared, 0, (NQ, GE), i32)
        src_i = part(shared, 2048, (NQ, GE), i32)
        w_g = part(shared, 4096, (NQ, GE))
        dst_f = part(shared, 6144, (NQ, GE))
        src_f = part(shared, 8192, (NQ, GE))
        g_min = part(shared, 10240, (NQ,))
        g_max = part(shared, 10240 + NQ, (NQ,))
        g_base = part(shared, 10240 + 2 * NQ, (NQ,), i32)
        g_span = part(shared, 10240 + 3 * NQ, (NQ,), i32)
        g_extra = part(shared, 10240 + 4 * NQ, (NQ,), i32)
        less_dump = part(shared, 0, (NCOL,))
        dst_n, bits_hi, bits_lo = (part(shared, 2048 + n * NCOL, (NCOL,), i32) for n in range(3))
        parts0 = part(shared, 0, (2, KC, TB * T0W)).rearrange("p s k (t d) -> p s k t d", d=T0W)
        sum0 = part(shared, 2 * KC * TB * T0W, (2, TB * T0W)).rearrange("p s (t d) -> p s t d", d=T0W)
        dst_hi = part(acc, 0, (NCOL,))
        dst_lo = part(acc, NCOL, (NCOL,))
        edge_cols = part(acc, 2 * NCOL, (3, NCOL), bf16)
        at0 = 2 * NCOL + 3 * NCOL // 2
        ident_b = part(acc, at0, (P,), bf16)
        cols = part(acc, at0 + P // 2, (2, 3, KC), bf16)
        at0 += P // 2 + 3 * KC
        hot0 = part(acc, at0, (2, KC, P))
        same = part(acc, at0 + 2 * GE, (3, KC, P))
        window0 = part(acc, at0 + 5 * GE, (3, T0W))
        wrow = part(acc, at0 + 5 * GE + 3 * T0W, (2, KC, T0W))
        at0 += 5 * GE + 3 * T0W + 2 * KC * T0W
        later = part(acc, at0, (2, KC))
        keep = part(acc, at0 + 2 * KC, (KC,))
        unread = part(acc, at0 + 3 * KC, (KC, P))
        base_bc = part(acc, at0 + 3 * KC + GE, (NG,), i32)
        assert at0 + 3 * KC + GE + NG <= NPAD
        e_at = 0

        def e_part(shape):
            nonlocal e_at
            n = 1
            for m in shape:
                n *= m
            e_at += n
            return part(shared, e_at - n, shape)
        e_rows, e_y = e_part((QUAD, UT, D)), e_part((QUAD, UT, D))
        e_w1, e_w2 = e_part((QUAD, DH)), e_part((QUAD, 2, D))
        e_b2, e_bias = e_part((QUAD, D)), e_part((2, 2))
        e_rows_t, e_hid = e_part((2, UROWS)), e_part((2, 2, UROWS))
        assert e_at <= 10752
        flat = lambda a, n: small[:, a:a + n, :].rearrange("p a t -> p (a t)")
        u_one, u_n, u_incl, u_past, u_prod = (small[:, n, 0:NE] for n in (4, 5, 8, 9, 13))
        u_nt = flat(6, 2)[0:NE, 0:P]
        u_col = small[:, 14, 0:8]
        u_quads = small[:, 15, 0:1].bitcast(i32)
        unit_row = flat(10, 3)[0:1, 0:2 * P].bitcast(i32)
        quads = small[0:1, 16, 0:1].bitcast(i32)
        msg = part(work, 0, (SLOTS, KC, D))
        rows0 = part(work, 0, (3, KC, T0W))
        hot = part(work, 4656, (3, KC, WIN))
        rel_x = part(work, 6192, (KC,))
        idx_x = part(work, 6196, (KC,), i32)
        b1_rows = work[0:NE, 5376:5376 + DH]
        w_conv_t = part(work, 5376 + DH, (D,))
        gate_w = part(work, 5376 + DH + D, (NE,))
        extra_f = work[0:1, 4656:4656 + NG]
        hot_lo = part(work, 3096, (2, KC, P), bf16)
        hot_hi = part(work, 3096 + KC * P, (2, KC, NT), bf16)
        slot = part(work, 0, (7, TB, D))
        slot_w = part(work, 0, (7, BW))
        tab0 = part(work, 0, (2, TB, T0W))

        c_score = part(shared, 0, (2, TB, NE))
        c_one = part(shared, 896, (2, 2, TB * NE)).rearrange("p s k (j e) -> p s k j e", j=TB)
        c_pick = part(shared, 2688, (2, TB, NE), bf16)
        before_b = part(shared, 6144, (P,), bf16)
        ones_b = part(shared, 6144 + P // 2, (P,), bf16)
        c_prod = part(shared, 3584, (2, 2, TB * NE)).rearrange("p s k (j e) -> p s k j e", j=TB)
        c_top = part(shared, 5376, (2, TB, 8))
        c_at = part(shared, 5488, (2, TB, 8), u32)
        c_small = part(shared, 5632, (2, 10, 2 * TB))
        c_sum = part(shared, 6016, (NE,))
        w1_sb, w2_sb, wres_sb, bias_bc, bres_bc = (part(shared, 10752 + n * D, (D,)) for n in range(5))
        r_xt_sb = part(shared, 0, (2, BW))
        r_h_sb = part(shared, 2 * BW, (2, BW))
        r_z_sb = part(shared, 4 * BW, (2, BW))

        pp = [ctx.enter_context(nc.psum_tensor(f"pp{n}", [P, 1024], f32)) for n in range(4)]
        win = [pp[0][:, 0:512], pp[0][:, 512:1024], pp[1][:, 0:512]]
        hist = pp[1][:, 512:512 + NT]
        node_ps = [pp[2], pp[3]]
        chunk_at = lambda t, k: t[:, k // 2 * 512 + k % 2 * T0W:k // 2 * 512 + (k % 2 + 1) * T0W]
        by_bank = lambda t: t[:, :].rearrange("p (a n) -> p a n", a=2)[:, :, 0:2 * T0W]\
            .rearrange("p a (k d) -> p a k d", k=2)
        picked_ps, combined_ps = pp[0], pp[2]
        rel_ps = pp[1][:, 0:512]
        src_ps = [pp[3][:, 0:512], pp[3][:, 512:1024]]

        consts_made = sem("consts_made")
        pool_const = sem("pool_const")
        edges_in = sem("edges_in")
        x_in = sem("x_in")
        x_pad = sem("x_pad")
        weights_in, weights3_in = sem("weights_in"), sem("weights3_in")
        prep = sem("prep")
        rel_ready, srcf_ready = sem("rel_ready"), sem("srcf_ready")
        rel_up, src_up, w_up = sem("rel_up"), sem("src_up"), sem("w_up")
        rel_down, src_down, w_down = sem("rel_down"), sem("src_down"), sem("w_down")
        numbers_out, numbers_in = sem("numbers_out"), sem("numbers_in")
        sq_made, sq_summed = sem("sq_made"), sem("sq_summed")
        a_dve, a_act = sem("a_dve"), sem("a_act")
        row_made = sem("row_made")
        idx_ready = sem("idx_ready")
        msg_in = [sem(f"msg_in{s}") for s in range(SLOTS)]
        sums_zero, pad_zero = sem("sums_zero"), sem("pad_zero")
        cols_ready, spread, hot0_ready, route0 = sem("cols_ready"), sem("spread"), sem("hot0_ready"), sem("route0")
        window_in = [sem(f"window_in{s}") for s in range(3)]
        taken, weighted, combined, rows_ready = sem("taken"), sem("weighted"), sem("combined"), sem("rows_ready")
        scattered = [sem(f"scattered{k}") for k in range(KC)]
        sum_in = [sem("sum_in0"), sem("sum_in1")]
        z_go, z_cols, z_win, z_taken, z_weighted, z_combined = (
            sem(f"extra0_{n}") for n in ("go", "cols", "win", "taken", "weighted", "combined"))
        hot_ready, hist_ready, route_step = sem("hot_ready"), sem("hist_ready"), sem("route_step")
        summed, hist_summed = sem("summed"), sem("hist_summed")
        added = sem("added")
        layer_done = sem("layer_done")
        bits_ready = sem("bits_ready")
        degree, degree_sqrt = sem("degree"), sem("degree_sqrt")
        x_idx, x_msg, x_got, x_hot, x_sum, x_step = (sem(f"extra_{n}") for n in ("idx", "msg", "got", "hot", "sum", "step"))
        z_rows, z_sent, z_done, z_hot, z_spread, z_step = x_idx, x_msg, x_got, x_hot, x_sum, x_step
        half_staged, staged, evacuated, reduced = sem("half_staged"), sem("staged"), sem("evacuated"), sem("reduced")
        b_dve, b_act = sem("b_dve"), sem("b_act")
        y_ready, mv_ready, sd_ready, x_ready = sem("y_ready"), sem("mv_ready"), sem("sd_ready"), sem("x_ready")
        norm_ready, stat_ready = sem("norm_ready"), sem("stat_ready")
        tab_ready = sem("tab_ready")
        tab_stored = [sem("tab_stored0"), sem("tab_stored1")]
        out_stored = sem("out_stored")
        cleared = sem("cleared")
        w_dve, w_pe, w_act = sem("w_dve"), sem("w_pe"), sem("w_act")
        buffers_zero = sem("buffers_zero")
        c_staged, c_up, c_new, c_kept = sem("c_staged"), sem("c_up"), sem("c_new"), sem("c_kept")
        c_scores, c_step, c_exp = sem("c_scores"), sem("c_step"), sem("c_exp")
        c_hot, c_cum, c_route = sem("c_hot"), sem("c_cum"), sem("c_route")
        sent = [sem("sent0"), sem("sent1")]
        e_in, w_in = [sem(f"e_in{s}") for s in range(QUAD)], [sem(f"w_in{s}") for s in range(QUAD)]
        e_up, e_down, e_mm1, e_act, e_mm2, e_yup = (sem(f"e_{n}") for n in ("up", "down", "mm1", "act", "mm2", "yup"))
        e_out = [sem(f"e_out{s}") for s in range(QUAD)]
        u_pe, u_dve, units_ready = sem("u_pe"), sem("u_dve"), sem("units_ready")
        b2_in = [sem(f"b2_in{s}") for s in range(QUAD)]
        k_idx, k_half, k_sum, k_kept, k_up, k_stat = (sem(f"k_{n}") for n in ("idx", "half", "sum", "kept", "up", "stat"))
        k_in = [sem("k_in0"), sem("k_in1")]
        bn_step, bn_sd, bn_up, bn_done = sem("bn_step"), sem("bn_sd"), sem("bn_up"), sem("bn_done")
        c_late = sem("c_late")
        n_prod, n_shift = sem("n_prod"), sem("n_shift")
        d_staged, d_up, d_self = sem("d_staged"), sem("d_up"), sem("d_self")
        r_in = [sem("r_in0"), sem("r_in1")]
        r_up, r_xt, r_h, r_z, r_zt, r_y = (sem(f"r_{n}") for n in ("up", "xt", "h", "z", "zt", "y"))

        noted = sem("noted")
        e_bias_in = sem("e_bias_in")

        block = ctx.enter_context(nc.Block())

        def after(eng, s, n):
            if not isinstance(n, int) or n > 0:
                eng.wait_ge(s, n)

        def apart(eng, s, n):
            eng.wait_ge(s, n)
            eng.sem_inc(noted, 1)

        def batches(eng, *stages, lags=None):
            lags = lags or range(len(stages))
            peeled = 4 if max(lags) else 2

            def fixed(t):
                for k, stage in zip(lags, stages):
                    if 0 <= t - k < NB:
                        stage(t - k, (t - k) % 2, (t - k) // 2)

            for t in range(peeled):
                fixed(t)
            with eng.Fori(peeled // 2, NB // 2) as i:
                for half in range(2):
                    for k, stage in zip(lags, stages):
                        stage(2 * i + (half - k), (half - k) % 2, i + (half - k) // 2)
            for t in range(NB, NB + max(lags)):
                fixed(t)

        def tiles(b, n=TB):
            return ds(b * TB, n)

        def groups(eng, body, turns=TURNS, begin=None):
            if begin:
                begin(0)
            for s in range(SLOTS):
                body(s, s, 0)
            with eng.Fori(1, turns) as turn:
                if begin:
                    begin(turn)
                for s in range(SLOTS):
                    body(turn * SLOTS + s, s, turn)

        def rounds(eng, body, begin=None):
            groups(eng, body, TURNS - 1, begin)
            for turn in (TURNS - 1, TURNS):
                todo = range(SLOTS) if turn < TURNS else range(1)
                if begin:
                    begin(turn)
                for s in todo:
                    body(turn * SLOTS + s, s, turn)

        def there(g):
            return not isinstance(g, int) or g < NG

        def extra_windows(eng, body, begin=None):
            for k in range(KC):
                eng.wait_ge(scattered[k], 16 * NG)
            flag = eng.value_load(any_extra[0:1, 0:1], min_val=0, max_val=NT)
            with eng.If(flag > 0):
                with eng.Fori(0, NG) as g:
                    n = eng.value_load(extra_row[0:1, ds(g, 1)], min_val=0, max_val=NT)
                    with eng.If(n > 0):
                        if begin:
                            begin(g)
                        with eng.Fori(0, n) as j:
                            body(g, j)

        def quads_of(eng, body, last=None):
            eng.wait_ge(units_ready, 1)
            further = eng.value_load(quads, min_val=0, max_val=NE * UPE // QUAD - 2)
            for s in range(QUAD):
                body(s, s, 0)
            with eng.Fori(1, further + (1 if last else 2)) as q:
                for s in range(QUAD):
                    body(QUAD * q + s, s, q)
            if last:
                for s in range(QUAD):
                    last(QUAD * further + QUAD + s, s, further + 1)

        def take(eng, s):
            eng.wait_ge(s, 16 if s is z_win else 1)
            eng.sem_clear(s)

        LAST = NG - 1
        PREP_STEPS = 5
        B_STEPS = (7, 11)
        U_STEPS = 10
        BN_STEPS = 6
        USES = [TURNS * KC * 16 + (KLAST * 16 if s == 0 else 0) for s in range(SLOTS)]
        msg_at = lambda layer, s, turn: (layer - 1) * USES[s] + (turn + 1) * (KC * 16)
        FILL = EROWS // (EP * TURNS)
        FILLS = EROWS // (EP * FILL)
        assert FILL * FILLS * EP == EROWS and FILLS >= TURNS - 1
        STORES = NB // 2

        @block.sync
        def _(sp):
            full = (NQ - 1) * P * GE
            most = (NG - 1) * GE
            for src_ap, dst_ap, fill in ((dst, dst_i, E - (GE - EREST)), (src, src_i, 0), (edge_weight, w_g, 0)):
                sp.dma_start(dst_ap[:, 0:NQ - 1, :],
                             src_ap[0:full].rearrange("(q p j) -> p q j", p=P, j=GE)).then_inc(edges_in, 16)
                sp.dma_start(dst_ap[0:GREST - 1, NQ - 1, :],
                             src_ap[full:most].rearrange("(p j) -> p j", j=GE)).then_inc(edges_in, 16)
                sp.dma_start(dst_ap[GREST - 1:GREST, NQ - 1, 0:EREST],
                             src_ap[most:E].rearrange("(p j) -> p j", p=1)).then_inc(edges_in, 16)
                sp.dma_start(dst_ap[GREST - 1:GREST, NQ - 1, EREST:GE],
                             src_ap[fill:fill + GE - EREST].rearrange("(p j) -> p j", p=1)).then_inc(edges_in, 16)
            sp.wait_ge(x_pad, 1)
            for c in range(NB):
                m = TB if c < NB - 1 else TB - 1
                sp.dma_start(X[:, c * TB:c * TB + m, :],
                             x[c * BW:c * BW + m * P, :].rearrange("(t p) d -> p t d", p=P)).then_inc(x_in, 16)
            sp.dma_start(X[0:N - (NT - 1) * P, NT - 1, :], x[(NT - 1) * P:N, :]).then_inc(x_in, 16)
            column = lambda v: v.rearrange("(p a) -> p a", a=1)
            for to, of in ((w_gcn[:, 0:D], W_conv), (gate_w[:, :], gate_W), (b1_rows[:, :], b1e), (col[:, 0:1], column(b_conv)),
                           (col[:, 1:2], column(bn_gamma)), (col[:, 2:3], column(bn_beta)), (col[:, 3:4], column(b1)),
                           (bconv_bc[:, :], b_conv.partition_broadcast(P)),
                           (gateb_bc[:, :], gate_b.partition_broadcast(P))):
                sp.dma_start(to, of).then_inc(weights_in, 16)
            sp.wait_ge(prep, PREP_STEPS)
            for n, g in enumerate((g_base, g_extra)):
                sp.dma_start(group_numbers[n, 0:(NQ - 1) * P].rearrange("(q p) -> p q", p=P),
                             g[:, 0:NQ - 1], allow_slow_non_contiguous=True).then_inc(numbers_out, 16)
                sp.dma_start(group_numbers[n, (NQ - 1) * P:NG].rearrange("(p a) -> p a", a=1),
                             g[0:GREST, NQ - 1:NQ], allow_slow_non_contiguous=True).then_inc(numbers_out, 16)
            sp.wait_ge(numbers_out, 64)
            sp.dma_start(base_row[:, :], group_numbers[0:1, 0:NG]).then_inc(numbers_in, 16)
            sp.dma_start(extra_row[:, :], group_numbers[1:2, 0:NG]).then_inc(numbers_in, 16)
            sp.dma_start(base_bc, group_numbers[0:1, 0:NG].rearrange("a g -> (a g)").partition_broadcast(P)).then_inc(numbers_in, 16)

            def clear_sums0(b, s, turn):
                for k in range(KC // 2, KC):
                    sp.dma_start(sums0[k].rearrange("(t p) d -> p t d", p=P)[:, tiles(b), :],
                                 zeros[:, :].unsqueeze(1).to_broadcast([P, TB, T0W])).then_inc(sums_zero, 16)

            def store0(b, s, turn):
                sp.wait_ge(row_made, b + 1)
                sp.dma_start(table0.rearrange("(t p) d -> p t d", p=P)[:, tiles(b), :],
                             tab0[:, s, :, :]).then_inc(tab_stored[s], 16)
            sp.wait_ge(pool_const, 1)
            sp.dma_start(table0[NPAD:NPAD + WIN, :], zeros[:, :]).then_inc(pad_zero, 16)
            for k in range(KC // 2, KC):
                sp.dma_start(sums0[k][NPAD:NPAD + P, :], zeros[:, :]).then_inc(sums_zero, 16)
            batches(sp, store0, clear_sums0, lags=(0, 0))

            bases = {}

            def load_bases(turn):
                for s in range(SLOTS if not isinstance(turn, int) or turn < TURNS else 1):
                    bases[s] = sp.value_load(base_row[0:1, ds(turn * SLOTS + s, 1)], min_val=0, max_val=N - 1)

            def load_window(g, s, turn):
                after(sp, taken, g - 2)
                sp.dma_start(window0[:, s % 3, :], table0[ds(bases[s], WIN), :]).then_inc(window_in[s % 3], 16)

            def load_extra(g, j):
                first = sp.value_load(base_row[0:1, ds(g, 1)], min_val=0, max_val=N - 1)
                take(sp, z_go)
                at = nc.s_assert_within(first + WIN * (j + 1), WIN, N - 1,
                                        skip_runtime_bounds_check_because="no window begins beyond the group's last node")
                sp.dma_start(window0[:, 0, :], table0[ds(at, WIN), :]).then_inc(z_win, 16)

            sp.wait_ge(numbers_in, 48)
            sp.wait_ge(pad_zero, 16)
            for n in range(2):
                sp.wait_ge(tab_stored[n], 16 * STORES)
            rounds(sp, load_window, load_bases)
            extra_windows(sp, load_extra)

            def load_sums(b, s, turn):
                after(sp, staged, b - 1)
                for k in range(KC):
                    sp.dma_start(parts0[:, s, k, :, :], sums0[k].rearrange("(t p) d -> p t d", p=P)[:, tiles(b), :])\
                        .then_inc(sum_in[s], 16)
            sp.wait_ge(layer_done, 1)
            batches(sp, load_sums)

            def clear_sums(b, layer):
                sp.wait_ge(y_ready, layer * NB + b + 1)
                sp.dma_start(acc[:, ds(b * BW, BW)].rearrange("p (t d) -> p t d", d=D),
                             zeros[:, 0:D].unsqueeze(1).to_broadcast([P, TB, D])).then_inc(cleared, 16)

            def store_table(layer):
                view = tables[layer].rearrange("(t p) d -> p t d", p=P)

                def body(b, s, turn):
                    clear_sums(b, layer - 1)
                    sp.wait_ge(tab_ready, (layer - 1) * NB + b + 1)
                    sp.dma_start(view[:, tiles(b), :], slot[:, 2 + s, :, :]).then_inc(tab_stored[s], 16)
                batches(sp, body)

            store_table(1)
            for to, of in ((w1_sb, W1), (w2_sb, W2), (wres_sb, Wres), (bias_bc, b2.partition_broadcast(P)),
                           (bres_bc, bres.partition_broadcast(P))):
                sp.dma_start(to, of).then_inc(weights3_in, 16)

            def load_rows_of(u, s):
                row = sp.value_load(unit_row[0:1, ds(u + P, 1)], min_val=0, max_val=EROWS - UROWS)
                after(sp, e_up, u - (QUAD - 1))
                sp.dma_start(e_rows[0:EP, s, :, :],
                             expert_rows[ds(row, UROWS), :].rearrange("(t p) d -> p t d", p=EP)).then_inc(e_in[s], 16)

            def load_weights_of(u, s):
                e = sp.value_load(unit_row[0:1, ds(u, 1)], min_val=0, max_val=NE - 1)
                after(sp, e_mm2, u - (QUAD - 1))
                sp.dma_start(e_w1[:, s, :], W1e.rearrange("e p h -> p e h")[:, ds(e, 1), :]
                             .rearrange("p e h -> p (e h)")).then_inc(w_in[s], 16)
                sp.dma_start(e_w2[:, s, :, :], W2e.rearrange("e (h p) d -> p (e h) d", p=P)[:, ds(e * 2, 2), :])\
                    .then_inc(w_in[s], 16)

            def unit_loads(u, s, q, ahead=True):
                if ahead or s + 1 < QUAD:
                    load_rows_of(u + 1, (s + 1) % QUAD)
                load_weights_of(u, s)

            for s in range(2):
                sp.wait_ge(sent[s], 16 * 2 * TB * (NB // 2))
            sp.wait_ge(units_ready, 1)
            load_rows_of(0, 0)
            quads_of(sp, unit_loads, lambda u, s, q: unit_loads(u, s, q, False))

            store_table(2)

            def store3(b, s, turn):
                clear_sums(b, 2)
                sp.wait_ge(x_ready, 2 * NB + b + 1)
                sp.dma_start(tables[3].rearrange("(t p) d -> p t d", p=P)[:, tiles(b), :],
                             X[:, tiles(b), :]).then_inc(tab_stored[s], 16)
            batches(sp, store3)

            def load_rows(b, s):
                after(sp, r_up, b - 1)
                sp.dma_start(slot[:, s, :, :],
                             tables[3].rearrange("(t p) d -> p t d", p=P)[:, tiles(b), :]).then_inc(r_in[s], 16)

            for s in range(2):
                sp.wait_ge(tab_stored[s], 16 * 4 * STORES)
            sp.wait_ge(layer_done, 4)
            for b in range(2):
                load_rows(b, b)
            with sp.Fori(1, NB // 2) as i:
                load_rows(2 * i, 0)
                load_rows(2 * i + 1, 1)
            sp.wait_ge(out_stored, 16 * (NB + 1))

        @block.gpsimd
        def _(pool):
            pool.memset(X[:, NT - 1, :], 0.0).then_inc(x_pad, 1)
            pool.memset(zeros[:, :], 0.0).then_inc(pool_const, 1)
            pool.memset(ident[:, :], 0.0).then_inc(consts_made, 1)
            pool.memset(ones[:, :], 1.0).then_inc(consts_made, 1)
            pool.iota(iota[:, :], [[1, P]], base=0, channel_multiplier=0,
                      allow_small_or_imprecise_dtypes=True).then_inc(consts_made, 1)
            pool.iota(iota_b[:, :], [[1, P]], base=0, channel_multiplier=0,
                      allow_small_or_imprecise_dtypes=True).then_inc(consts_made, 1)
            pool.wait_ge(consts_made, 4)
            pool.affine_select(out=ident[:, :], in_=ident[:, :], compare_op=ALU.not_equal, fill=1.0,
                               base=0, pattern=[[-1, P]], channel_multiplier=1).then_inc(consts_made, 1)
            pool.affine_select(out=before[:, :], in_=ones[:, :], compare_op=ALU.is_gt, fill=0.0,
                               base=0, pattern=[[1, P]], channel_multiplier=-1).then_inc(consts_made, 1)
            pool.memset(run[:, 0, :], 0.0).then_inc(consts_made, 1)
            pool.affine_select(out=ident_b, in_=ones[:, :], compare_op=ALU.is_equal, fill=0.0,
                               base=0, pattern=[[-1, P]], channel_multiplier=1).then_inc(consts_made, 1)
            pool.iota(col[:, 5:6], [[1, 1]], base=0, channel_multiplier=1,
                      allow_small_or_imprecise_dtypes=True).then_inc(consts_made, 1)
            pool.iota(col[:, 6:7], [[1, 1]], base=NPAD, channel_multiplier=1,
                      allow_small_or_imprecise_dtypes=True).then_inc(consts_made, 1)
            pool.memset(acc[:, NPAD:ACCW], 0.0).then_inc(consts_made, 1)

            def end_dmas(s):
                pool.wait_ge(s, 16 * KC)
                pool.dma_reset(range(s.num, s.num + 1))
                pool.sem_clear(s)

            def gather(layer):
                table = tables[layer]

                def table_complete():
                    pool.wait_ge(tab_stored[0], 16 * (layer + 1) * STORES)
                    pool.wait_ge(tab_stored[1], 16 * (layer + 1) * STORES)

                def rows(s, chunks):
                    for k in range(chunks):
                        pool.indirect_dma_start(
                            out=msg[:, s, k, :], out_offset=None, in_=table,
                            in_offset=bass.IndirectOffsetOnAxis(ap=idx[:, s, k:k + 1], axis=0),
                            bounds_check=NPAD - 1, oob_is_err=False).then_inc(msg_in[s], 16)

                def body(g, s, turn):
                    apart(pool, idx_ready, (layer - 1) * NG + g + 1)
                    rows(s, KC)
                table_complete()
                groups(pool, body)
                pool.wait_ge(idx_ready, layer * NG)
                rows(0, KLAST)

                pool.wait_ge(added, layer * NG)
                flag = pool.value_load(any_extra[0:1, 0:1], min_val=0, max_val=NT)
                with pool.If(flag > 0):
                    with pool.Fori(0, NG) as g:
                        n = pool.value_load(extra_row[0:1, ds(g, 1)], min_val=0, max_val=NT)
                        with pool.If(n > 0):
                            pool.wait_ge(x_idx, 1)
                            pool.sem_clear(x_idx)
                            for k in range(KC):
                                pool.indirect_dma_start(
                                    out=msg[:, 0, k, :], out_offset=None, in_=table,
                                    in_offset=bass.IndirectOffsetOnAxis(ap=idx_x[:, k:k + 1], axis=0),
                                    bounds_check=NPAD - 1, oob_is_err=False).then_inc(x_msg, 16)
                            end_dmas(x_msg)
                            pool.sem_inc(x_got, 1)

            def scale_rows(layer, scale):
                def body(b, s, turn):
                    pool.wait_ge(x_ready, layer * NB + b + 1)
                    pool.wait_ge(tab_stored[s], 16 * ((layer + 1) * STORES + turn))
                    pool.tensor_tensor(slot[:, 2 + s, :, :], X[:, tiles(b), :],
                                       in_scale[:, scale, tiles(b)].unsqueeze(2).to_broadcast([P, TB, D]), ALU.mult).then_inc(tab_ready, 1)
                return body

            def add_rows(rows, picked, k, done):
                pool.indirect_dma_start(
                    out=sums0[k], out_offset=bass.IndirectOffsetOnAxis(ap=picked, axis=0), in_=rows, in_offset=None,
                    bounds_check=NPAD + P - 1, oob_is_err=True, compute_op=ALU.add).then_inc(done, 16)

            def scatter(g, s, turn):
                if isinstance(g, int):
                    pool.wait_ge(route0, g + 1)
                    pool.wait_ge(rows_ready, g + 1)
                else:
                    apart(pool, route0, g + 1)
                    apart(pool, rows_ready, g + 1)
                for k in range(KC):
                    if not isinstance(g, int):
                        apart(pool, scattered[k], 16 * g)
                    elif g:
                        pool.wait_ge(scattered[k], 16 * g)
                    add_rows(rows0[:, s % 3, k, :], idx[:, s, k:k + 1], k, scattered[k])

            def scatter_extra(g, j):
                take(pool, z_rows)
                for k in range(KC):
                    add_rows(rows0[:, 0, k, :], idx[:, 0, k:k + 1], k, z_sent)
                end_dmas(z_sent)
                pool.sem_inc(z_done, 1)
            pool.wait_ge(sums_zero, 16 * (KC // 2) * (NB + 2))
            rounds(pool, scatter)
            extra_windows(pool, scatter_extra)
            batches(pool, scale_rows(0, 0))
            gather(1)

            pool.wait_ge(buffers_zero, 16 * FILLS)

            def send(b, s, turn):
                apart(pool, c_route, b + 1)
                for j in range(TB):
                    for k in range(2):
                        pool.indirect_dma_start(
                            out=expert_rows, out_offset=bass.IndirectOffsetOnAxis(ap=send_row[:, s, 2 * j + k:2 * j + k + 1], axis=0),
                            in_=slot[:, 2 + s, j, :], in_offset=None,
                            bounds_check=NE * CROWS - 1, oob_is_err=False).then_inc(sent[s], 16)
            batches(pool, send)

            def unit_bias(u, s, q):
                e = pool.value_load(unit_row[0:1, ds(u, 1)], min_val=0, max_val=NE - 1)
                if not isinstance(u, int):
                    apart(pool, e_yup, u - (QUAD - 1))
                pool.dma_start(e_b2[0:EP, s, :], b2e[ds(e, 1), :].rearrange("e d -> (e d)").partition_broadcast(EP))\
                    .then_inc(b2_in[s], 16)
            for s in range(2):
                pool.wait_ge(sent[s], 16 * 2 * TB * (NB // 2))
            quads_of(pool, unit_bias)

            def fetch(b, s, turn):
                apart(pool, k_idx, b + 1)
                for j in range(TB):
                    for k in range(2):
                        pool.indirect_dma_start(
                            out=slot[:, 2 * s + k, j, :], out_offset=None, in_=expert_rows,
                            in_offset=bass.IndirectOffsetOnAxis(ap=fetch_row[:, s, 2 * j + k:2 * j + k + 1], axis=0),
                            bounds_check=NE * CROWS - 1, oob_is_err=False).then_inc(k_in[s], 16)
            further = pool.value_load(quads, min_val=0, max_val=NE * UPE // QUAD - 2)
            for s in range(QUAD):
                apart(pool, e_out[s], 16 * further + 32)
            batches(pool, fetch)

            pool.wait_ge(bn_done, 1)

            def shift(b, s, turn):
                pool.wait_ge(y_ready, NB + b - 1)
                pool.tensor_tensor(slot[:, 4 + s, :, :], X[:, tiles(b), :],
                                   bn_bc[:, 1, :].unsqueeze(1).to_broadcast([P, TB, D]), ALU.add).then_inc(n_shift, 1)

            batches(pool, shift, scale_rows(1, 1), lags=(0, 1))

            gather(2)
            pool.wait_ge(layer_done, 3)

            def own(b, s, turn):
                after(pool, y_ready, 2 * NB + b - 1)
                pool.tensor_tensor(slot[:, 4 + s, :, :], X[:, tiles(b), :],
                                   self_scale[:, tiles(b)].unsqueeze(2).to_broadcast([P, TB, D]), ALU.mult).then_inc(d_self, 1)
            batches(pool, own)
            gather(3)

            pool.wait_ge(w_dve, 4)

            pool.wait_ge(layer_done, 4)

            def residual(b, s, turn):
                pool.wait_ge(y_ready, 3 * NB + b - 1)
                pool.tensor_tensor(slot[:, 5 + s, :, :], X[:, tiles(b), :],
                                   bias_bc[:, :].unsqueeze(1).to_broadcast([P, TB, D]), ALU.add).then_inc(n_shift, 1)
            batches(pool, residual)

        @block.scalar
        def _(act):
            act.wait_ge(edges_in, 12 * 16)
            act.activation(src_f[:, 0:NQ - 1, :], src_i[:, 0:NQ - 1, :], ACT.Copy).then_inc(srcf_ready, 1)
            act.activation(src_f[0:GREST, NQ - 1, :], src_i[0:GREST, NQ - 1, :], ACT.Copy).then_inc(srcf_ready, 1)
            for q in range(NQ):
                m = P if q < NQ - 1 else GREST
                cols = slice(q * GE, q * GE + KC * m)
                act.wait_ge(src_up, q + 1)
                act.activation(src_t[:, cols].rearrange("p (g k) -> p k g", k=KC),
                               pp[3][:, 0:512].rearrange("p (k g) -> p k g", k=KC)[:, :, 0:m], ACT.Copy).then_inc(src_down, 1)
                act.wait_ge(w_up, q + 1)
                act.activation(w_t[:, cols].rearrange("p (g k) -> p k g", k=KC),
                               pp[3][:, 512:1024].rearrange("p (k g) -> p k g", k=KC)[:, :, 0:m], ACT.Copy).then_inc(w_down, 1)

            act.wait_ge(w_pe, 1)
            act.activation(w_conv_t[:, :], pp[1][:, 512:640], ACT.Copy).then_inc(w_act, 1)
            act.activation(b1_t[:, :, :], pp[1][:, 640:768].rearrange("p (h e) -> p h e", h=2), ACT.Copy).then_inc(w_act, 1)

            act.wait_ge(x_in, 16 * (NB + 1))
            act.wait_ge(x_pad, 1)
            act.wait_ge(pool_const, 1)
            for k in range(KC // 2):
                act.dma_start(sums0[k].rearrange("(t p) d -> p t d", p=P),
                              zeros[:, :].unsqueeze(1).to_broadcast([P, NT + 1, T0W])).then_inc(sums_zero, 16)

            def squares(b, s, turn):
                after(act, sq_summed, b - 1)
                act.activation(slot[:, 4 + s, :, :], X[:, tiles(b), :], ACT.Square).then_inc(sq_made, 1)
            batches(act, squares)
            act.wait_ge(sq_summed, NB)
            act.activation(small[:, 1, :], small[:, 0, :], ACT.Sqrt).then_inc(a_act, 1)
            act.wait_ge(a_dve, 1)
            act.activation(small[:, 2, :], small[:, 1, :], ACT.Tanh).then_inc(a_act, 1)

            def source_rows(g, s):
                act.copy(idx[:, s, :], src_t[:, ds(g * KC, KC)]).then_inc(idx_ready, 1)

            def weigh_rows(g, ws):
                act.copy(wrow[:, ws, :, T0W - 1].rearrange("p (a k) -> p a k", a=2), by_bank(picked_ps)[:, :, :, T0W - 1])
                for k in range(KC):
                    i = act.activation(wrow[:, ws, k, 0:T0W - 1], chunk_at(picked_ps, k)[:, 0:T0W - 1], ACT.Copy,
                                       scale=w_t[:, ds(g * KC + k, 1)])
                return i

            def keep_rows(rs):
                return act.activation(rows0[:, rs, :, :].rearrange("p (a k) d -> p a k d", a=2), by_bank(combined_ps), ACT.Copy)

            def weigh(g, s):
                act.wait_ge(taken, g + 1)
                after(act, combined, g - 1)
                weigh_rows(g, s % 2).then_inc(weighted, 1)

            def rows_by_source(g, s, turn):
                if there(g + 1):
                    weigh(g + 1, (s + 1) % SLOTS)
                for k in range(KC):
                    after(act, scattered[k], 16 * (g - 2))
                act.wait_ge(combined, g + 1)
                keep_rows(s % 3).then_inc(rows_ready, 1)

            def rows_extra(g, j):
                take(act, z_taken)
                weigh_rows(g, 0).then_inc(z_weighted, 1)
                take(act, z_combined)
                keep_rows(0).then_inc(z_rows, 1)

            def layer0_rows():
                act.wait_ge(w_down, NQ)
                weigh(0, 0)
                rounds(act, rows_by_source)
                extra_windows(act, rows_extra)

            def gather(layer):
                act.wait_ge(layer_done, layer)
                for s in range(SLOTS):
                    source_rows(s, s)

                def fill(turn):
                    rows = expert_rows[ds(turn * (FILL * EP), FILL * EP), :].rearrange("(t p) d -> p t d", p=EP)
                    act.dma_start(rows, zeros[0:EP, 0:D].unsqueeze(1).to_broadcast([EP, FILL, D])).then_inc(buffers_zero, 16)

                def body(g, s, turn):
                    act.wait_ge(summed, (layer - 1) * NG + g + 1)
                    source_rows(g + SLOTS, s)
                groups(act, body, TURNS - 1, fill if layer == 1 else None)
                if layer == 1:
                    for turn in range(TURNS - 1, FILLS):
                        fill(turn)
                act.wait_ge(summed, (layer - 1) * NG + LAST - SLOTS + 1)
                source_rows(LAST, 0)

            def deviation(layer):
                def body(b, s, turn):
                    act.wait_ge(mv_ready, layer * NB + b + 1)
                    act.activation(sd[:, s, :], mv[:, s, :, 1], ACT.Sqrt, bias=col[:, 4:5]).then_inc(sd_ready, 1)
                return body

            def normal_rows(layer, y):
                def body(b, s, turn):
                    apart(act, norm_ready, 2 * (layer * NB + b) + 2)
                    for j in range(TB):
                        i = act.activation(X[:, b * TB + j, :], slot[:, y + s, j, :], ACT.Identity,
                                           bias=off[:, s, j:j + 1], scale=sd[:, s, j:j + 1])
                    i.then_inc(x_ready, 1)
                return body

            layer0_rows()

            def down(b, s, turn):
                act.wait_ge(staged, b + 1)
                after(act, reduced, b - 1)
                act.activation(acc[:, ds(b * BW, BW)].rearrange("p (t d) -> p t d", d=D), sum0[:, s, :, 0:D], ACT.Copy)
                act.activation(slot[:, 4 + s, :, :], sum0[:, s, :, 0:D], ACT.Square).then_inc(evacuated, 1)
            batches(act, down)
            act.wait_ge(reduced, NB)
            act.activation(small[:, 1, :], small[:, 0, :], ACT.Sqrt).then_inc(b_act, 1)
            act.wait_ge(b_dve, B_STEPS[0])
            act.activation(small[:, 8, :], small[:, 7, :], ACT.Sqrt).then_inc(b_act, 1)
            act.activation(small[:, 10, :], small[:, 9, :], ACT.Sqrt).then_inc(b_act, 1)
            act.wait_ge(b_dve, B_STEPS[1])
            act.activation(small[:, 12, :], small[:, 11, :], ACT.Ln).then_inc(b_act, 1)
            batches(act, normal_rows(0, 0), deviation(0), lags=(1, 0))
            gather(1)

            act.wait_ge(degree, 1)
            act.activation(small[:, 1, :], small[:, 0, :], ACT.Sqrt).then_inc(degree_sqrt, 1)

            def keep_new(b, s, turn):
                act.wait_ge(c_new, b + 1)
                act.activation(acc[:, ds(b * BW, BW)], slot_w[:, 2 + s, :], ACT.Copy).then_inc(c_kept, 1)
                act.wait_ge(c_scores, b + 1)
                act.activation(c_small[:, s, 1, 0:TB], c_small[:, s, 0, 0:TB], ACT.Exp).then_inc(c_exp, 1)
            batches(act, keep_new)

            def hidden(u, s, q):
                e = act.value_load(unit_row[0:1, ds(u, 1)], min_val=0, max_val=NE - 1)
                half = s % 2
                after(act, e_act, 2 * (u - 1))
                act.copy(e_bias[:, half, :], b1_t[:, :, ds(e, 1)].rearrange("p h e -> p (h e)")).then_inc(e_bias_in, 1)
                after(act, e_mm2, u - 1)
                act.wait_ge(e_bias_in, u + 1)
                for h in range(2):
                    act.wait_ge(e_mm1, 2 * u + h + 1)
                    act.activation(e_hid[:, half, h, :], pp[1 + half][:, h * 512:h * 512 + UROWS], ACT.Gelu,
                                   bias=e_bias[:, half, h:h + 1]).then_inc(e_act, 1)

            def unit_store(u, s):
                row = act.value_load(unit_row[0:1, ds(u + P, 1)], min_val=0, max_val=EROWS - UROWS)
                act.wait_ge(e_yup, u + 1)
                act.dma_start(expert_rows[ds(row, UROWS), :].rearrange("(t p) d -> p t d", p=EP),
                              e_y[0:EP, s, :, :]).then_inc(e_out[s], 16)

            def unit_step(u, s, q):
                hidden(u, s, q)
                if not isinstance(u, int) or u >= 2:
                    unit_store(u - 2, (s + 2) % QUAD)

            def last_step(u, s, q):
                unit_step(u, s, q)
                if s == QUAD - 1:
                    unit_store(u - 1, s - 1)
                    unit_store(u, s)
            quads_of(act, unit_step, last_step)

            def keep_sum(b, s, turn):
                act.wait_ge(k_sum, b + 1)
                act.activation(acc[:, ds(b * BW, BW)], slot_w[:, 4 + s, :], ACT.Copy).then_inc(k_kept, 1)
            batches(act, keep_sum)
            act.wait_ge(bn_step, 1)
            act.activation(bn_mv[:, 2:3], bn_mv[:, 1:2], ACT.Sqrt, bias=col[:, 4:5]).then_inc(bn_sd, 1)
            batches(act, normal_rows(1, 0), deviation(1), lags=(1, 0))
            gather(2)

            act.wait_ge(layer_done, 3)
            batches(act, normal_rows(2, 0), deviation(2), lags=(1, 0))
            gather(3)

            def turned3(b, s, turn):
                act.wait_ge(r_up, b + 1)
                after(act, r_y, b - 1)
                act.activation(r_xt_sb[:, s, :], pp[0][:, 0:BW], ACT.Copy).then_inc(r_xt, 1)

            def hidden3(b, s, turn):
                act.wait_ge(r_z, b + 1)
                act.activation(r_z_sb[:, s, :].rearrange("p (a n) -> p a n", a=2),
                               pp[1][:, :].rearrange("p (a n) -> p a n", a=2)[:, :, 0:BW // 2], ACT.Relu,
                               bias=col[:, 3:4]).then_inc(r_zt, 1)

            def store_out(b, s, turn):
                act.wait_ge(x_ready, 3 * NB + b + 1)
                whole = BW if not isinstance(b, int) or b < NB - 1 else BW - P
                act.dma_start(out[ds(b * BW, whole), :].rearrange("(t p) d -> p t d", p=P),
                              X[:, tiles(b, whole // P), :]).then_inc(out_stored, 16)
                if whole < BW:
                    act.dma_start(out[(NT - 1) * P:N, :], X[0:N - (NT - 1) * P, NT - 1, :]).then_inc(out_stored, 16)
            batches(act, hidden3, turned3, deviation(3), normal_rows(3, 2), store_out, lags=(1, 0, 2, 3, 3))

        @block.tensor
        def _(pe):
            pe.wait_ge(consts_made, 7)
            pe.wait_ge(edges_in, 12 * 16)
            pe.wait_ge(srcf_ready, 2)
            for q in range(NQ):
                m = P if q < NQ - 1 else GREST
                pe.wait_ge(rel_ready, q + 1)
                for of, to, up, free in ((dst_f, pp[2][:, q % 2 * 512:q % 2 * 512 + 512], rel_up, (rel_down, q - 1)),
                                         (src_f, pp[3][:, 0:512], src_up, (src_down, q)),
                                         (w_g, pp[3][:, 512:1024], w_up, (w_down, q))):
                    after(pe, *free)
                    for k in range(KC):
                        i = pe.transpose(to[:, k * P:k * P + m], of[0:m, q, k * P:(k + 1) * P], ident[0:m, 0:m])
                    i.then_inc(up, 1)

            pe.wait_ge(weights_in, 9 * 16)
            pe.transpose(pp[1][:, 512:640], w_gcn[:, 0:D], ident[:, :])
            for h in range(2):
                i = pe.transpose(pp[1][:, 640 + h * NE:640 + (h + 1) * NE], b1_rows[:, h * P:(h + 1) * P], ident[0:NE, 0:NE])
            i.then_inc(w_pe, 1)
            pe.wait_ge(w_act, 2)
            pe.wait_ge(w_dve, 1)
            pe.matmul(pp[1][:, 512:512 + NE], w_conv_t[:, :], gate_w[:, :], start=True, stop=True)
            pe.matmul(pp[1][:, 512 + NE:512 + 2 * NE], bn_wide[:, 0, :], gate_w[:, :], start=True, stop=True).then_inc(w_pe, 1)

            def spread_columns(cs, ss):
                for k in range(KC):
                    to = slice(k * P, (k + 1) * P)
                    along = lambda n: cols[:, cs, n, k:k + 1].to_broadcast([P, P])
                    pe.matmul(src_ps[ss][:, to], along(0), ident_b, start=True, stop=False)
                    pe.matmul(src_ps[ss][:, to], along(1), ident_b, start=False, stop=True)
                    i = pe.matmul(rel_ps[:, to], along(2), ident_b, start=True, stop=True)
                return i

            def take_rows(ws, hs):
                for k in range(KC):
                    i = pe.matmul(chunk_at(picked_ps, k), hot0[:, hs, k, :], window0[:, ws, :], start=True, stop=True)
                return i

            def combine_rows(es, rs):
                for k in range(KC):
                    i = pe.matmul(chunk_at(combined_ps, k), same[:, es, k, :], wrow[:, rs, k, :], start=True, stop=True)
                return i

            def spread_group(g, s):
                pe.wait_ge(cols_ready, g + 1)
                after(pe, hot0_ready, g)
                spread_columns(s % 2, s % 2).then_inc(spread, 1)

            def take_group(g, s, turn):
                pe.wait_ge(hot0_ready, g + 1)
                pe.wait_ge(window_in[s % 3], 16 * (2 * turn + s // 3 + 1))
                after(pe, weighted, g)
                take_rows(s % 3, s % 2).then_inc(taken, 1)

            def count_in(g, s):
                pe.wait_ge(hist_ready, g + 1)
                for k in range(KC):
                    i = pe.matmul(hist, hot_lo[:, s % 2, k, :], hot_hi[:, s % 2, k, :],
                                  start=(isinstance(g, int) and g == k == 0),
                                  stop=(isinstance(g, int) and g == LAST and k == KC - 1))
                i.then_inc(hist_summed, 1)

            def products0(g, s, turn):
                next_of = lambda n: ((s + n) % SLOTS, turn + (s + n) // SLOTS)
                if there(g + 2):
                    spread_group(g + 2, next_of(2)[0])
                if there(g + 1):
                    take_group(g + 1, *next_of(1))
                    count_in(g + 1, next_of(1)[0])
                pe.wait_ge(weighted, g + 1)
                after(pe, rows_ready, g)
                combine_rows(s % 3, s % 2).then_inc(combined, 1)

            def products_extra(g, j):
                take(pe, z_cols)
                spread_columns(0, 0).then_inc(z_spread, 1)
                take(pe, z_hot)
                take(pe, z_win)
                take_rows(0, 0).then_inc(z_taken, 1)
                take(pe, z_weighted)
                combine_rows(0, 0).then_inc(z_combined, 1)

            pe.wait_ge(consts_made, 10)
            pe.wait_ge(w_dve, 2)
            for s, n in ((rel_down, NQ), (src_down, NQ), (w_down, NQ)):
                pe.wait_ge(s, n)
            spread_group(0, 0)
            take_group(0, 0, 0)
            count_in(0, 0)
            spread_group(1, 1)
            rounds(pe, products0)
            extra_windows(pe, products_extra)

            def sums(layer):
                def window(at, rs, hs, chunks):
                    for k in range(chunks):
                        i = pe.matmul(win[at][:, 0:WIN], msg[:, rs, k, :], hot[:, hs, k, :],
                                      start=(k == 0), stop=(k == chunks - 1))
                    return i

                def body(g, s, turn, chunks=KC):
                    pe.wait_ge(msg_in[s], msg_at(layer, s, turn) if chunks == KC else layer * USES[s])
                    after(pe, added, (layer - 1) * NG + g - 2)
                    pe.wait_ge(hot_ready, (layer - 1) * NG + g + 1)
                    window(s % 3, s, s % 3, chunks).then_inc(summed, 1)
                groups(pe, body)
                body(LAST, 0, TURNS, KLAST)

                pe.wait_ge(added, layer * NG)
                flag = pe.value_load(any_extra[0:1, 0:1], min_val=0, max_val=NT)
                with pe.If(flag > 0):
                    with pe.Fori(0, NG) as g:
                        n = pe.value_load(extra_row[0:1, ds(g, 1)], min_val=0, max_val=NT)
                        with pe.If(n > 0):
                            with pe.Fori(0, n):
                                pe.wait_ge(x_hot, 1)
                                pe.sem_clear(x_hot)
                                window(0, 0, 0, KC).then_inc(x_sum, 1)

            sums(1)

            def product1(b, s, turn):
                pe.wait_ge(c_staged, b + 1)
                after(pe, c_scores, b - 1)
                for j in range(TB):
                    pe.matmul(node_ps[s][:, j * P:(j + 1) * P], slot[:, s, j, :], w_gcn[:, 0:D], start=True, stop=True)
                for j in range(TB):
                    i = pe.matmul(pp[0][:, s * 512 + j * NE:s * 512 + (j + 1) * NE], slot[:, s, j, :], w_gcn[:, D:D + NE],
                                  start=True, stop=True)
                i.then_inc(c_up, 1)

            def counts(b, s, turn):
                pe.wait_ge(w_dve, 3)
                pe.wait_ge(c_hot, b + 1)
                after(pe, c_route, b - 1)
                for j in range(TB):
                    to = pp[1][:, s * 512 + j * NE:s * 512 + (j + 1) * NE]
                    pe.matmul(to, before_b, c_pick[:, s, j, :], start=True, stop=False)
                    for i in range(j):
                        pe.matmul(to, ones_b, c_pick[:, s, i, :], start=False, stop=False)
                    i = pe.matmul(to, ones[:, :], run[:, s, :], start=False, stop=True)
                i.then_inc(c_cum, 1)
            batches(pe, counts, product1, lags=(2, 0))

            pe.wait_ge(c_step, 7 * NB)
            pe.wait_ge(c_new, NB)
            pe.matmul(pp[2][:, 0:NE], ones[:, :], run[:, NB % 2, :], start=True, stop=True).then_inc(u_pe, 1)
            pe.wait_ge(u_dve, 2)
            pe.transpose(pp[2][0:NE, NE:NE + P], u_n, ident[:, :]).then_inc(u_pe, 1)
            pe.wait_ge(u_dve, 3)
            pe.matmul(pp[2][:, NE + P:2 * NE + P], u_nt, before[0:NE, 0:NE], start=True, stop=True).then_inc(u_pe, 1)
            pe.wait_ge(u_dve, U_STEPS)
            for n in range(2):
                i = pe.matmul(pp[2][0:1, (2 + n) * P:(3 + n) * P], u_col[:, 4 + n:5 + n], ident[:, :], start=True, stop=True)
            i.then_inc(u_pe, 1)

            def turn_rows(u, s, q):
                pe.wait_ge(e_in[s], 16 * (q + 1))
                after(pe, e_down, u - 1)
                for j in range(UT):
                    i = pe.transpose(pp[0][:, s % 2 * 512 + j * EP:s % 2 * 512 + (j + 1) * EP], e_rows[0:EP, s, j, :], ident[0:EP, 0:EP])
                i.then_inc(e_up, 1)

            def first_product(u, s, q):
                pe.wait_ge(w_in[s], 32 * (q + 1))
                pe.wait_ge(e_down, u + 1)
                after(pe, e_act, 2 * (u - 1))
                for h in range(2):
                    pe.matmul(pp[1 + s % 2][:, h * 512:h * 512 + UROWS], e_w1[:, s, h * P:(h + 1) * P], e_rows_t[:, s % 2, :],
                              start=True, stop=True).then_inc(e_mm1, 1)

            def second_product(u, s):
                pe.wait_ge(e_act, 2 * u + 2)
                after(pe, e_yup, u - 1)
                for j in range(UT):
                    for h in range(2):
                        i = pe.matmul(pp[3][0:EP, s % 2 * 512 + j * D:s % 2 * 512 + (j + 1) * D],
                                      e_hid[:, s % 2, h, j * EP:(j + 1) * EP], e_w2[:, s, h, :], start=(h == 0), stop=(h == 1))
                i.then_inc(e_mm2, 1)

            def unit_products(u, s, q, ahead=True):
                if ahead or s + 2 < QUAD:
                    turn_rows(u + 2, (s + 2) % QUAD, q + (s + 2) // QUAD)
                if ahead or s + 1 < QUAD:
                    first_product(u + 1, (s + 1) % QUAD, q + (s + 1) // QUAD)
                second_product(u, s)

            turn_rows(0, 0, 0)
            turn_rows(1, 1, 0)
            first_product(0, 0, 0)
            quads_of(pe, unit_products, lambda u, s, q: unit_products(u, s, q, False))

            def turn1(b, s, turn):
                pe.wait_ge(k_sum, b + 1)
                after(pe, k_stat, b - 1)
                for j in range(TB):
                    i = pe.transpose(node_ps[s][:, j * P:(j + 1) * P], slot[:, 4 + s, j, :], ident[:, :])
                i.then_inc(k_up, 1)
            batches(pe, turn1)
            pe.wait_ge(bn_step, BN_STEPS)
            for n in range(2):
                i = pe.matmul(pp[0][:, n * P:(n + 1) * P], bn_wide[:, n, :], ident[:, :], start=True, stop=True)
            i.then_inc(bn_up, 1)
            sums(2)

            def turn2(b, s, turn):
                pe.wait_ge(d_staged, b + 1)
                after(pe, y_ready, 2 * NB + b - 1)
                for j in range(TB):
                    i = pe.transpose(node_ps[s][:, j * P:(j + 1) * P], slot[:, 2 + s, j, :], ident[:, :])
                i.then_inc(d_up, 1)
            batches(pe, turn2)
            sums(3)

            pe.wait_ge(layer_done, 4)
            pe.wait_ge(weights3_in, 5 * 16)

            def turn3(b, s, turn):
                pe.wait_ge(r_in[s], 16 * (turn + 1))
                after(pe, r_h, b)
                after(pe, r_xt, b)
                for j in range(TB):
                    i = pe.transpose(pp[0][:, j * P:(j + 1) * P], slot[:, s, j, :], ident[:, :])
                i.then_inc(r_up, 1)

            def product3(b, s, turn):
                pe.wait_ge(r_h, b + 1)
                after(pe, r_zt, b)
                for a in range(2):
                    i = pe.matmul(pp[1][:, a * 512:a * 512 + BW // 2], w1_sb[:, :],
                                  r_h_sb[:, s, a * BW // 2:(a + 1) * BW // 2], start=True, stop=True)
                i.then_inc(r_z, 1)

            def answer3(b, s, turn):
                pe.wait_ge(r_xt, b + 1)
                pe.wait_ge(r_zt, b + 1)
                after(pe, y_ready, 3 * NB + b - 1)
                for j in range(TB):
                    to = node_ps[s][:, j * P:(j + 1) * P]
                    pe.matmul(to, r_z_sb[:, s, j * P:(j + 1) * P], w2_sb[:, :], start=True, stop=False)
                    i = pe.matmul(to, r_xt_sb[:, s, j * P:(j + 1) * P], wres_sb[:, :], start=False, stop=True)
                i.then_inc(r_y, 1)
            batches(pe, product3, turn3, answer3, lags=(1, 0, 1))

        @block.vector
        def _(dve):
            dve.memset(col[:, 4:5], LN_EPS)
            dve.wait_ge(edges_in, 12 * 16)
            dve.tensor_copy(dst_f[:, 0:NQ - 1, :], dst_i[:, 0:NQ - 1, :])
            dve.tensor_copy(dst_f[0:GREST, NQ - 1, :], dst_i[0:GREST, NQ - 1, :]).then_inc(prep, 1)
            dve.wait_ge(prep, 1)
            for m, q in ((P, slice(0, NQ - 1)), (GREST, slice(NQ - 1, NQ))):
                dve.tensor_reduce(g_min[0:m, q], dst_f[0:m, q, :], AX.X, ALU.min)
                i = dve.tensor_reduce(g_max[0:m, q], dst_f[0:m, q, :], AX.X, ALU.max)
            i.then_inc(prep, 1)
            dve.wait_ge(prep, 2)
            for q in range(NQ):
                m = P if q < NQ - 1 else GREST
                dve.tensor_scalar(dst_f[0:m, q, :], dst_f[0:m, q, :], g_min[0:m, q:q + 1], None, ALU.subtract)\
                    .then_inc(rel_ready, 1)
            for m, q in ((P, slice(0, NQ - 1)), (GREST, slice(NQ - 1, NQ))):
                dve.tensor_copy(g_base[0:m, q], g_min[0:m, q])
                i = dve.tensor_tensor(g_max[0:m, q], g_max[0:m, q], g_min[0:m, q], ALU.subtract)
            i.then_inc(prep, 1)
            dve.wait_ge(prep, 3)
            for m, q in ((P, slice(0, NQ - 1)), (GREST, slice(NQ - 1, NQ))):
                i = dve.tensor_copy(g_span[0:m, q], g_max[0:m, q])
            i.then_inc(prep, 1)
            dve.wait_ge(prep, 4)
            for m, q in ((P, slice(0, NQ - 1)), (GREST, slice(NQ - 1, NQ))):
                i = dve.tensor_scalar(g_extra[0:m, q], g_span[0:m, q], WIN.bit_length() - 1, None, ALU.arith_shift_right)
            i.then_inc(prep, 1)
            for q in range(NQ):
                m = P if q < NQ - 1 else GREST
                dve.wait_ge(rel_up, q + 1)
                dve.tensor_copy(rel_t[:, q * GE:q * GE + KC * m].rearrange("p (g k) -> p k g", k=KC),
                                pp[2][:, q % 2 * 512:q % 2 * 512 + 512].rearrange("p (k g) -> p k g", k=KC)[:, :, 0:m])\
                    .then_inc(rel_down, 1)
            dve.wait_ge(rel_down, NQ)
            dve.memset(rel_t[:, LAST * KC + KLAST:NCOL], -1.0)
            dve.memset(rel_t[EREST % P:P, LAST * KC + KLAST - 1:LAST * KC + KLAST], -1.0).then_inc(rel_down, 1)

            def square_sums(b, s, turn):
                dve.wait_ge(sq_made, b + 1)
                dve.tensor_reduce(small[:, 0, tiles(b)], slot[:, 4 + s, :, :], AX.X, ALU.add).then_inc(sq_summed, 1)
            batches(dve, square_sums)
            dve.wait_ge(a_act, 1)
            dve.tensor_scalar(small[:, 1, :], small[:, 1, :], EPS_NORM, None, ALU.max).then_inc(a_dve, 1)
            dve.wait_ge(a_dve, 1)
            dve.reciprocal(small[:, 3, :], small[:, 1, :]).then_inc(a_dve, 1)
            dve.wait_ge(a_act, 2)
            dve.wait_ge(a_dve, 2)
            dve.tensor_tensor(small[:, 4, :], small[:, 2, :], small[:, 3, :], ALU.mult).then_inc(a_dve, 1)
            dve.wait_ge(a_dve, 3)
            dve.tensor_tensor(small[:, 5, :], small[:, 4, :], small[:, 4, :], ALU.mult).then_inc(a_dve, 1)
            dve.wait_ge(a_dve, 4)
            dve.tensor_tensor(small[:, 5, :], small[:, 5, :], small[:, 0, :], ALU.mult).then_inc(a_dve, 1)
            dve.wait_ge(a_dve, 5)
            dve.tensor_scalar(small[:, 5, :], small[:, 5, :], -1.0, 1.0, ALU.mult, ALU.add).then_inc(a_dve, 1)
            dve.wait_ge(a_dve, 6)
            dve.tensor_scalar(small[:, 5, :], small[:, 5, :], EPS_NORM, None, ALU.max).then_inc(a_dve, 1)
            dve.wait_ge(a_dve, 7)
            dve.reciprocal(small[:, 6, :], small[:, 5, :]).then_inc(a_dve, 1)
            dve.wait_ge(a_dve, 8)
            dve.scalar_tensor_tensor(small[:, 7, :], small[:, 6, :], 2.0, small[:, 4, :], ALU.mult, ALU.mult)
            dve.tensor_scalar(small[:, 8, :], small[:, 6, :], 2.0, -1.0, ALU.mult, ALU.add).then_inc(a_dve, 1)
            dve.wait_ge(a_dve, 9)

            def table0_rows(b, s, turn):
                after(dve, tab_stored[s], 16 * turn)
                for j in range(TB):
                    dve.tensor_scalar(tab0[:, s, j, 0:D], X[:, b * TB + j, :], small[:, 7, ds(b * TB + j, 1)], None, ALU.mult)
                dve.memset(tab0[:, s, :, D + 1], 1.0)
                dve.tensor_copy(tab0[:, s, :, D], small[:, 8, tiles(b)]).then_inc(row_made, 1)
            batches(dve, table0_rows)

            dve.wait_ge(weights_in, 9 * 16)
            dve.tensor_copy(bn_wide[:, 0, :], col[:, 0:1].to_broadcast([P, P])).then_inc(w_dve, 1)
            dve.wait_ge(w_pe, 2)
            dve.tensor_copy(w_gcn[:, D:D + NE], pp[1][:, 512:512 + NE])
            dve.tensor_tensor(gateb_bc[:, :], gateb_bc[:, :], pp[1][:, 512 + NE:512 + 2 * NE], ALU.add).then_inc(w_dve, 1)

            dve.wait_ge(numbers_in, 48)
            dve.tensor_copy(extra_f[:, :], extra_row[:, :]).then_inc(prep, 1)
            dve.wait_ge(prep, PREP_STEPS + 1)
            dve.tensor_reduce(extra_f[:, 0:1], extra_f[:, :], AX.X, ALU.max).then_inc(prep, 1)
            dve.wait_ge(prep, PREP_STEPS + 2)
            dve.tensor_copy(any_extra[:, :], extra_f[:, 0:1]).then_inc(prep, 1)

            dve.wait_ge(consts_made, 10)
            dve.wait_ge(numbers_out, 64)
            dve.wait_ge(src_up, NQ)
            dve.wait_ge(w_up, NQ)
            dve.wait_ge(src_down, NQ)
            dve.wait_ge(rel_down, NQ + 1)
            dve.tensor_tensor(dst_n.rearrange("p (g k) -> p g k", k=KC), rel_t[:, :].rearrange("p (g k) -> p g k", k=KC),
                              base_bc.unsqueeze(2).to_broadcast([P, NG, KC]), ALU.add).then_inc(bits_ready, 1)
            dve.wait_ge(bits_ready, 1)
            shift = P.bit_length() - 1
            dve.tensor_scalar(bits_hi, dst_n, shift, None, ALU.arith_shift_right)
            dve.tensor_scalar(bits_lo, dst_n, P - 1, None, ALU.bitwise_and).then_inc(bits_ready, 1)
            dve.wait_ge(bits_ready, 2)
            dve.tensor_copy(dst_hi, bits_hi)
            dve.tensor_copy(dst_lo, bits_lo).then_inc(bits_ready, 1)
            dve.wait_ge(bits_ready, 3)
            dve.memset(dst_lo[:, LAST * KC + KLAST:NCOL], -1.0)
            dve.memset(dst_lo[EREST % P:P, LAST * KC + KLAST - 1:LAST * KC + KLAST], -1.0)
            dve.tensor_scalar(bits_lo, src_t[:, :], P - 1, None, ALU.bitwise_and)
            dve.tensor_scalar(bits_hi, src_t[:, :], -P, None, ALU.bitwise_and).then_inc(bits_ready, 1)
            dve.wait_ge(bits_ready, 4)
            dve.tensor_copy(edge_cols[:, 0, :], bits_hi)
            dve.tensor_copy(edge_cols[:, 1, :], bits_lo)
            dve.tensor_copy(edge_cols[:, 2, :], rel_t[:, :])
            dve.tensor_scalar(less_dump, src_t[:, :], col[:, 6:7], None, ALU.subtract).then_inc(bits_ready, 1)
            dve.wait_ge(bits_ready, 5)

            def by_source(g, cs, es, hs):
                dve.tensor_tensor(same[:, es, :, :], src_ps[cs].rearrange("p (k e) -> p k e", k=KC),
                                  src_t[:, ds(g * KC, KC)].unsqueeze(2).to_broadcast([P, KC, P]), ALU.is_equal)
                return dve.tensor_scalar(hot0[:, hs, :, :].rearrange("p k e -> p (k e)"), rel_ps, col[:, 5:6], None, ALU.is_equal)

            def count_later(es, ls):
                for k in range(KC):
                    i = dve.tensor_tensor_reduce(unread[:, k, :], same[:, es, k, :], before[:, :], 1.0, 0.0, ALU.mult, ALU.add,
                                                 accum_out=later[:, ls, k:k + 1])
                return i

            def route_last(g, ls):
                return dve.scalar_tensor_tensor(keep, later[:, ls, :], 0.0, less_dump[:, ds(g * KC, KC)], ALU.is_equal, ALU.mult)

            def columns(g, s):
                after(dve, spread, g - 1)
                dve.tensor_copy(cols[:, s % 2, :, :], edge_cols[:, :, ds(g * KC, KC)]).then_inc(cols_ready, 1)

            ROUTE = 2

            def compare(g, s, turn):
                if there(g + 1):
                    columns(g + 1, (s + 1) % SLOTS)
                dve.wait_ge(spread, g + 1)
                after(dve, combined, g - 2)
                after(dve, taken, g - 1)
                by_source(g, s % 2, s % 3, s % 2).then_inc(hot0_ready, 1)
                dve.wait_ge(hot0_ready, g + 1)
                count_later(s % 3, s % 2).then_inc(route_step, 1)
                after(dve, hist_summed, g - 1)
                for k in range(KC):
                    dve.tensor_scalar(hot_lo[:, s % 2, k, :], iota_b[:, :], dst_lo[:, ds(g * KC + k, 1)], None, ALU.is_equal)
                    i = dve.tensor_scalar(hot_hi[:, s % 2, k, :], iota_b[:, 0:NT], dst_hi[:, ds(g * KC + k, 1)], None, ALU.is_equal)
                i.then_inc(hist_ready, 1)
                dve.wait_ge(route_step, ROUTE * g + 1)
                route_last(g, s % 2).then_inc(route_step, 1)
                after(dve, rows_ready, g - 2)
                dve.wait_ge(route_step, ROUTE * g + 2)
                dve.tensor_scalar(idx[:, s, :], keep, col[:, 6:7], None, ALU.add).then_inc(route0, 1)

            def step(i):
                i.then_inc(z_step, 1)
                take(dve, z_step)

            def begin_extra(g):
                step(dve.tensor_copy(rel_x[:, :], rel_t[:, ds(g * KC, KC)]))

            def compare_extra(g, j):
                step(dve.tensor_scalar(rel_x[:, :], rel_x[:, :], -float(WIN), None, ALU.add))
                dve.sem_inc(z_go, 1)
                dve.tensor_copy(cols[:, 0, 0:2, :], edge_cols[:, 0:2, ds(g * KC, KC)])
                dve.tensor_copy(cols[:, 0, 2, :], rel_x[:, :]).then_inc(z_cols, 1)
                take(dve, z_spread)
                step(by_source(g, 0, 0, 0))
                step(count_later(0, 0))
                step(route_last(g, 0))
                dve.tensor_scalar(idx[:, 0, :], keep, col[:, 6:7], None, ALU.add).then_inc(z_hot, 1)
                take(dve, z_done)

            columns(0, 0)
            rounds(dve, compare)
            extra_windows(dve, compare_extra, begin_extra)
            dve.sem_inc(layer_done, 1)

            def sums(layer):
                bases = {}

                def load_bases(turn):
                    for s in range(SLOTS):
                        bases[s] = dve.value_load(base_row[0:1, ds(turn * SLOTS + s, 1)], min_val=0, max_val=N - 1)

                def make_hot(g, s):
                    after(dve, summed, (layer - 1) * NG + g - 2)
                    for k in range(KC):
                        i = dve.tensor_scalar(hot[:, s % 3, k, :], iota[:, :], rel_t[:, ds(g * KC + k, 1)], None, ALU.is_equal)
                    i.then_inc(hot_ready, 1)

                def add_window(at, base):
                    return dve.tensor_tensor(acc[:, ds(base, WIN)], acc[:, ds(base, WIN)], win[at][:, 0:WIN], ALU.add)

                def body(g, s, turn):
                    make_hot(g + 1, (s + 1) % SLOTS)
                    dve.wait_ge(summed, (layer - 1) * NG + g + 1)
                    after(dve, added, (layer - 1) * NG + g)
                    add_window(s % 3, bases[s]).then_inc(added, 1)

                dve.wait_ge(consts_made, 11)
                dve.wait_ge(cleared, 16 * layer * NB)
                for n in range(2):
                    dve.wait_ge(tab_stored[n], 16 * (layer + 1) * STORES)
                make_hot(0, 0)
                groups(dve, body, begin=load_bases)
                base = dve.value_load(base_row[0:1, LAST:NG], min_val=0, max_val=N - 1)
                dve.wait_ge(summed, layer * NG)
                dve.wait_ge(added, (layer - 1) * NG + LAST)
                add_window(LAST % 3, base).then_inc(added, 1)

                dve.wait_ge(added, layer * NG)
                flag = dve.value_load(any_extra[0:1, 0:1], min_val=0, max_val=NT)
                with dve.If(flag > 0):
                    with dve.Fori(0, NG) as g:
                        n = dve.value_load(extra_row[0:1, ds(g, 1)], min_val=0, max_val=NT)
                        with dve.If(n > 0):
                            first = dve.value_load(base_row[0:1, ds(g, 1)], min_val=0, max_val=N - 1)
                            dve.tensor_copy(idx_x[:, :], src_t[:, ds(g * KC, KC)]).then_inc(x_idx, 1)
                            dve.tensor_copy(rel_x[:, :], rel_t[:, ds(g * KC, KC)]).then_inc(x_step, 1)
                            dve.wait_ge(x_got, 1)
                            dve.sem_clear(x_got)
                            dve.wait_ge(x_step, 1)
                            dve.sem_clear(x_step)
                            with dve.Fori(0, n) as j:
                                dve.tensor_scalar(rel_x[:, :], rel_x[:, :], -float(WIN), None, ALU.add).then_inc(x_step, 1)
                                dve.wait_ge(x_step, 1)
                                dve.sem_clear(x_step)
                                for k in range(KC):
                                    i = dve.tensor_scalar(hot[:, 0, k, :], iota[:, :], rel_x[:, k:k + 1], None, ALU.is_equal)
                                i.then_inc(x_hot, 1)
                                dve.wait_ge(x_sum, 1)
                                dve.sem_clear(x_sum)
                                at = nc.s_assert_within(first + WIN * (j + 1), WIN, N - 1,
                                                        skip_runtime_bounds_check_because="no window begins beyond the group's last node")
                                add_window(0, at).then_inc(x_step, 1)
                                dve.wait_ge(x_step, 1)
                                dve.sem_clear(x_step)
                dve.sem_inc(layer_done, 1)

            def moments(layer, y):
                def body(b, s, turn):
                    dve.wait_ge(y_ready, layer * NB + b + 1)
                    for j in range(TB):
                        i = dve.bn_stats(stat[:, s, j, :], slot[:, y + s, j, :])
                    i.then_inc(stat_ready, 1)
                    apart(dve, stat_ready, layer * NB + b + 1)
                    for j in range(TB):
                        i = dve.bn_aggr(mv[:, s, j, :], stat[:, s, j, :])
                    i.then_inc(mv_ready, 1)
                return body

            def normal(layer):
                def body(b, s, turn):
                    dve.wait_ge(sd_ready, layer * NB + b + 1)
                    dve.reciprocal(sd[:, s, :], sd[:, s, :]).then_inc(norm_ready, 1)
                    dve.wait_ge(norm_ready, 2 * (layer * NB + b) + 1)
                    dve.scalar_tensor_tensor(off[:, s, :], mv[:, s, :, 0], -1.0, sd[:, s, :], ALU.mult, ALU.mult).then_inc(norm_ready, 1)
                return body

            def stage0(b, s, turn):
                dve.wait_ge(sum_in[s], 16 * KC * (turn + 1))
                dve.tensor_tensor(parts0[:, s, 0:2, :, :], parts0[:, s, 0:2, :, :], parts0[:, s, 2:4, :, :], ALU.add)\
                    .then_inc(half_staged, 1)
                dve.wait_ge(half_staged, b + 1)
                after(dve, reduced, b - 1)
                after(dve, evacuated, b - 1)
                dve.tensor_tensor(sum0[:, s, :, :], parts0[:, s, 0, :, :], parts0[:, s, 1, :, :], ALU.add).then_inc(staged, 1)

            def norms0(b, s, turn):
                dve.wait_ge(evacuated, b + 1)
                dve.tensor_reduce(small[:, 0, tiles(b)], slot[:, 4 + s, :, :], AX.X, ALU.add)
                dve.tensor_copy(deg[:, tiles(b), :], sum0[:, s, :, D:T0W]).then_inc(reduced, 1)
            batches(dve, stage0, norms0)
            dve.wait_ge(reduced, NB)
            dve.wait_ge(hist_summed, NG)
            den, count = deg[:, :, 0], hist
            dve.tensor_scalar(small[:, 2, :], den, 0.0, 2.0, ALU.is_ge, ALU.mult)
            dve.scalar_tensor_tensor(small[:, 3, :], den, -1.0, den, ALU.mult, ALU.max).then_inc(b_dve, 1)
            dve.wait_ge(b_dve, 1)
            dve.tensor_scalar(small[:, 3, :], small[:, 3, :], EPS_DEN, None, ALU.max).then_inc(b_dve, 1)
            dve.wait_ge(b_dve, 2)
            dve.reciprocal(small[:, 4, :], small[:, 3, :]).then_inc(b_dve, 1)
            dve.wait_ge(b_dve, 3)
            dve.scalar_tensor_tensor(small[:, 5, :], small[:, 2, :], -1.0, small[:, 4, :], ALU.add, ALU.mult).then_inc(b_dve, 1)
            dve.wait_ge(b_act, 1)
            dve.tensor_tensor(small[:, 6, :], small[:, 4, :], small[:, 1, :], ALU.mult).then_inc(b_dve, 1)
            dve.wait_ge(b_dve, 5)
            dve.tensor_scalar(small[:, 6, :], small[:, 6, :], EPS_NORM, None, ALU.max).then_inc(b_dve, 1)
            dve.tensor_scalar(small[:, 7, :], count, 1.0, None, ALU.max)
            dve.tensor_scalar(small[:, 9, :], count, 1.0, None, ALU.add).then_inc(b_dve, 1)
            dve.wait_ge(b_dve, 7)
            dve.tensor_scalar(small[:, 13, :], small[:, 6, :], CLIP, None, ALU.min).then_inc(b_dve, 1)
            dve.wait_ge(b_dve, 8)
            dve.tensor_scalar(small[:, 14, :], small[:, 13, :], -1.0, 1.0, ALU.mult, ALU.add).then_inc(b_dve, 1)
            dve.wait_ge(b_dve, 9)
            dve.reciprocal(small[:, 15, :], small[:, 14, :]).then_inc(b_dve, 1)
            dve.wait_ge(b_dve, 10)
            dve.scalar_tensor_tensor(small[:, 11, :], small[:, 13, :], 1.0, small[:, 15, :], ALU.add, ALU.mult).then_inc(b_dve, 1)
            dve.reciprocal(small[:, 16, :], small[:, 6, :]).then_inc(b_dve, 1)
            dve.wait_ge(b_dve, 12)
            dve.tensor_tensor(small[:, 16, :], small[:, 16, :], small[:, 5, :], ALU.mult).then_inc(b_dve, 1)
            dve.wait_ge(b_act, 4)
            dve.wait_ge(b_dve, 13)
            dve.scalar_tensor_tensor(small[:, 17, :], small[:, 12, :], 0.25, small[:, 16, :], ALU.mult, ALU.mult)
            dve.reciprocal(in_scale[:, 0, :], small[:, 8, :])
            dve.reciprocal(in_scale[:, 1, :], small[:, 10, :]).then_inc(b_dve, 1)
            dve.wait_ge(b_dve, 14)

            def residual0(b, s, turn):
                after(dve, x_ready, b - 1)
                for j in range(TB):
                    i = dve.scalar_tensor_tensor(slot[:, s, j, :], acc[:, ds((b * TB + j) * P, P)], small[:, 17, ds(b * TB + j, 1)],
                                                 X[:, b * TB + j, :], ALU.mult, ALU.add)
                i.then_inc(y_ready, 1)
                moments(0, 0)(b, s, turn)
            batches(dve, normal(0), residual0, lags=(1, 0))

            sums(1)
            dve.wait_ge(layer_done, 2)
            dve.tensor_scalar(small[:, 0, :], deg[:, :, 1], 1.0, None, ALU.add).then_inc(degree, 1)

            C_BODY, C_LATE = 7, 5

            def stage1(b, s, turn):
                after(dve, c_up, b - 1)
                dve.tensor_copy(slot_w[:, s, :], acc[:, ds(b * BW, BW)]).then_inc(c_staged, 1)

            def route(b, s, turn):
                own = lambda n: dve.wait_ge(c_step, C_BODY * b + n)
                after(dve, sent[s], 16 * 2 * TB * turn)
                after(dve, c_kept, b - 1)
                dve.wait_ge(c_up, b + 1)
                for j in range(TB):
                    i = dve.scalar_tensor_tensor(slot[:, 2 + s, j, :], node_ps[s][:, j * P:(j + 1) * P],
                                                 in_scale[:, 0, ds(b * TB + j, 1)], bconv_bc[:, :], ALU.mult, ALU.add)
                i.then_inc(c_new, 1)
                for j in range(TB):
                    i = dve.scalar_tensor_tensor(c_score[:, s, j, :], pp[0][:, s * 512 + j * NE:s * 512 + (j + 1) * NE],
                                                 in_scale[:, 0, ds(b * TB + j, 1)], gateb_bc[:, :], ALU.mult, ALU.add)
                i.then_inc(c_step, 1)
                apart(dve, c_step, C_BODY * b + 1)
                for j in range(TB):
                    i = dve.max(c_top[:, s, j, :], c_score[:, s, j, :])
                i.then_inc(c_step, 1)
                own(2)
                dve.tensor_tensor(c_small[:, s, 0, 0:TB], c_top[:, s, :, 1], c_top[:, s, :, 0], ALU.subtract).then_inc(c_scores, 1)
                for j in range(TB):
                    i = dve.max_index(c_at[:, s, j, :], c_top[:, s, j, :], c_score[:, s, j, :])
                i.then_inc(c_step, 1)
                own(3)
                dve.tensor_copy(c_small[:, s, 2, :].rearrange("p (k j) -> p k j", k=2),
                                c_at[:, s, :, 0:2].rearrange("p j k -> p k j")).then_inc(c_step, 1)
                own(4)
                for k in range(2):
                    i = dve.tensor_tensor(c_one[:, s, k, :, :], iota[:, 0:NE].unsqueeze(1).to_broadcast([P, TB, NE]),
                                          c_small[:, s, 2, k * TB:(k + 1) * TB].unsqueeze(2).to_broadcast([P, TB, NE]), ALU.is_equal)
                i.then_inc(c_step, 1)
                own(5)
                dve.tensor_tensor(c_pick[:, s, :, :], c_one[:, s, 0, :, :], c_one[:, s, 1, :, :], ALU.add).then_inc(c_hot, 1)
                dve.wait_ge(c_hot, b + 1)
                dve.tensor_reduce(c_sum, c_pick[:, s, :, :].rearrange("p j e -> p e j"), AX.X, ALU.add).then_inc(c_step, 1)
                own(6)
                after(dve, c_cum, b)
                dve.tensor_tensor(run[:, 1 - s, :], run[:, s, :], c_sum, ALU.add).then_inc(c_step, 1)

            def place(b, s, turn):
                own = lambda n: dve.wait_ge(c_late, C_LATE * b + n)
                top, pos, valid, kept, row, prob = (c_small[:, s, n, :] for n in (2, 3, 4, 5, 6, 7))
                by_node = lambda t: t.rearrange("p j k -> p k j")
                two = lambda t: t.rearrange("p (k j) -> p k j", k=2)
                dve.wait_ge(c_cum, b + 1)
                dve.wait_ge(c_hot, b + 1)
                for k in range(2):
                    i = dve.tensor_tensor(c_prod[:, s, k, :, :], pp[1][:, s * 512:s * 512 + TB * NE].rearrange("p (j e) -> p j e", j=TB),
                                          c_one[:, s, k, :, :], ALU.mult)
                i.then_inc(c_late, 1)
                own(1)
                for k in range(2):
                    i = dve.tensor_reduce(pos[:, k * TB:(k + 1) * TB], c_prod[:, s, k, :, :], AX.X, ALU.add)
                dve.wait_ge(c_exp, b + 1)
                dve.tensor_scalar(prob[:, 0:TB], c_small[:, s, 1, 0:TB], 1.0, None, ALU.add).then_inc(c_late, 1)
                own(2)
                dve.tensor_scalar(valid, pos, float(CAP), None, ALU.is_lt)
                dve.reciprocal(prob[:, 0:TB], prob[:, 0:TB])
                dve.scalar_tensor_tensor(row, top, float(CROWS), pos, ALU.mult, ALU.add).then_inc(c_late, 1)
                own(3)
                dve.tensor_tensor(prob[:, TB:2 * TB], prob[:, 0:TB], c_small[:, s, 1, 0:TB], ALU.mult)
                dve.tensor_scalar(c_small[:, s, 8, :], valid, -float(FAR), float(FAR), ALU.mult, ALU.add)
                dve.tensor_tensor(kept, pos, valid, ALU.mult).then_inc(c_late, 1)
                own(4)
                dve.tensor_tensor(by_node(gate[:, tiles(b), :]), two(prob), two(valid), ALU.mult)
                dve.scalar_tensor_tensor(by_node(pair_row[:, tiles(b), :]), two(top), float(CROWS), two(kept), ALU.mult, ALU.add)\
                    .then_inc(c_late, 1)
                dve.tensor_tensor(by_node(send_row[:, s, :].rearrange("p (j k) -> p j k", k=2)), two(row),
                                  two(c_small[:, s, 8, :]), ALU.add).then_inc(c_route, 1)
            dve.tensor_copy(before_b, before[:, :])
            dve.tensor_copy(ones_b, ones[:, :]).then_inc(w_dve, 1)
            batches(dve, stage1, place, route, lags=(0, 2, 1))
            dve.wait_ge(degree_sqrt, 1)
            dve.reciprocal(in_scale[:, 2, :], small[:, 1, :]).then_inc(degree, 1)
            dve.wait_ge(degree, 2)
            dve.tensor_tensor(self_scale[:, :], in_scale[:, 1, :], in_scale[:, 2, :], ALU.mult).then_inc(degree, 1)
            dve.wait_ge(degree, 3)
            dve.tensor_scalar(self_scale[:, :], self_scale[:, :], 1.0, None, ALU.add).then_inc(degree, 1)

            by_unit = lambda n: dve.wait_ge(u_dve, n)
            total, past_at = pp[2][:, 0:NE], pp[2][:, NE + P:2 * NE + P]
            dve.wait_ge(u_pe, 1)
            dve.tensor_scalar(u_one, total, 0.0, None, ALU.is_gt).then_inc(u_dve, 1)
            by_unit(1)
            dve.scalar_tensor_tensor(u_n, total, float(UROWS), u_one, ALU.is_gt, ALU.add).then_inc(u_dve, 1)
            dve.wait_ge(u_pe, 2)
            dve.tensor_copy(u_nt, pp[2][0:NE, NE:NE + P]).then_inc(u_dve, 1)
            dve.wait_ge(u_pe, 3)
            by_unit(2)
            dve.tensor_tensor(u_incl, past_at, u_n, ALU.add).then_inc(u_dve, 1)
            by_unit(4)
            dve.tensor_scalar(u_past, u_incl, col[:, 5:6], None, ALU.is_le).then_inc(u_dve, 1)
            by_unit(5)
            dve.tensor_tensor(u_prod, u_past, u_n, ALU.mult).then_inc(u_dve, 1)
            by_unit(6)
            expert, before_it, units, nth = (u_col[:, n:n + 1] for n in range(4))
            dve.tensor_reduce(expert, u_past, AX.X, ALU.add)
            dve.tensor_reduce(before_it, u_prod, AX.X, ALU.add)
            dve.tensor_reduce(units, u_n, AX.X, ALU.add).then_inc(u_dve, 1)
            by_unit(7)
            dve.tensor_scalar(u_col[:, 4:5], expert, float(NE - 1), None, ALU.min)
            dve.tensor_scalar(u_quads, units, float(QUAD - 1), None, ALU.add)
            dve.tensor_tensor(nth, col[:, 5:6], before_it, ALU.subtract).then_inc(u_dve, 1)
            by_unit(8)
            dve.tensor_scalar(u_quads, u_quads, QUAD.bit_length() - 1, None, ALU.arith_shift_right)
            dve.tensor_scalar(nth, nth, float(UROWS), None, ALU.mult).then_inc(u_dve, 1)
            by_unit(9)
            dve.tensor_scalar(u_quads, u_quads, -2.0, 0.0, ALU.add, ALU.max)
            dve.scalar_tensor_tensor(u_col[:, 5:6], expert, float(CROWS), nth, ALU.mult, ALU.add).then_inc(u_dve, 1)
            dve.wait_ge(u_pe, 4)
            by_unit(U_STEPS)
            dve.tensor_copy(unit_row, pp[2][0:1, 2 * P:4 * P])
            dve.tensor_copy(quads, u_quads[0:1, :]).then_inc(units_ready, 1)

            def unit_rows(u, s):
                dve.wait_ge(e_up, u + 1)
                after(dve, e_mm1, 2 * (u - 1))
                dve.tensor_copy(e_rows_t[:, s % 2, :], pp[0][:, s % 2 * 512:s % 2 * 512 + UROWS]).then_inc(e_down, 1)

            def unit_answer(u, s, q):
                dve.wait_ge(e_mm2, u + 1)
                dve.wait_ge(b2_in[s], 16 * (q + 1))
                after(dve, e_out[s], 16 * q)
                dve.tensor_tensor(e_y[0:EP, s, :, :], pp[3][0:EP, s % 2 * 512:s % 2 * 512 + UT * D].rearrange("p (t d) -> p t d", d=D),
                                  e_b2[0:EP, s, :].unsqueeze(1).to_broadcast([EP, UT, D]), ALU.add).then_inc(e_yup, 1)

            def unit_steps(u, s, q, ahead=True):
                if ahead or s + 2 < QUAD:
                    unit_rows(u + 2, (s + 2) % QUAD)
                unit_answer(u, s, q)

            dve.wait_ge(units_ready, 1)
            unit_rows(0, 0)
            unit_rows(1, 1)
            quads_of(dve, unit_steps, lambda u, s, q: unit_steps(u, s, q, False))

            def rows_of(b, s, turn):
                after(dve, k_in[s], 16 * 2 * TB * turn)
                dve.wait_ge(c_late, C_LATE * NB)
                dve.tensor_copy(fetch_row[:, s, :].rearrange("p (j k) -> p j k", k=2), pair_row[:, tiles(b), :]).then_inc(k_idx, 1)

            def combine(b, s, turn):
                dve.wait_ge(k_in[s], 16 * 2 * TB * (turn + 1))
                after(dve, k_kept, b - 1)
                after(dve, k_up, b - 1)
                for j in range(TB):
                    i = dve.scalar_tensor_tensor(slot[:, 4 + s, j, :], slot[:, 2 * s, j, :], gate[:, b * TB + j, 0:1],
                                                 acc[:, ds((b * TB + j) * P, P)], ALU.mult, ALU.add)
                i.then_inc(k_half, 1)
                dve.wait_ge(k_half, b + 1)
                for j in range(TB):
                    i = dve.scalar_tensor_tensor(slot[:, 4 + s, j, :], slot[:, 2 * s + 1, j, :], gate[:, b * TB + j, 1:2],
                                                 slot[:, 4 + s, j, :], ALU.mult, ALU.add)
                i.then_inc(k_sum, 1)
                dve.wait_ge(k_up, b + 1)
                for a in range(2):
                    n = BW // 2 if not isinstance(b, int) or b < NB - 1 or a == 0 else LASTN - BW // 2
                    i = dve.bn_stats(bn_stat[:, 2 * b + a, :], node_ps[s][:, a * BW // 2:a * BW // 2 + n])
                i.then_inc(k_stat, 1)
            dve.wait_ge(c_kept, NB)
            batches(dve, rows_of, combine)
            dve.wait_ge(k_stat, NB)
            dve.bn_aggr(bn_mv[:, 0:2], bn_stat[:, :, :]).then_inc(bn_step, 1)
            dve.wait_ge(bn_sd, 1)
            dve.reciprocal(bn_mv[:, 2:3], bn_mv[:, 2:3]).then_inc(bn_step, 1)
            dve.wait_ge(bn_step, 2)
            dve.tensor_tensor(bn_mv[:, 3:4], bn_mv[:, 2:3], col[:, 1:2], ALU.mult).then_inc(bn_step, 1)
            dve.wait_ge(bn_step, 3)
            dve.tensor_tensor(bn_mv[:, 2:3], bn_mv[:, 0:1], bn_mv[:, 3:4], ALU.mult).then_inc(bn_step, 1)
            dve.wait_ge(bn_step, 4)
            dve.tensor_tensor(bn_mv[:, 2:3], col[:, 2:3], bn_mv[:, 2:3], ALU.subtract).then_inc(bn_step, 1)
            dve.wait_ge(bn_step, 5)
            dve.tensor_copy(bn_wide[:, 0, :], bn_mv[:, 3:4].to_broadcast([P, P]))
            dve.tensor_copy(bn_wide[:, 1, :], bn_mv[:, 2:3].to_broadcast([P, P])).then_inc(bn_step, 1)
            dve.wait_ge(bn_up, 1)
            dve.tensor_copy(bn_bc[:, :, :], pp[0][:, 0:2 * P].rearrange("p (n d) -> p n d", n=2)).then_inc(bn_done, 1)
            dve.wait_ge(bn_done, 1)
            dve.wait_ge(k_kept, NB)

            def residual1(b, s, turn):
                dve.wait_ge(x_ready, NB + b - 1)
                dve.tensor_tensor(slot[:, s, :, :], acc[:, ds(b * BW, BW)].rearrange("p (t d) -> p t d", d=D),
                                  bn_bc[:, 0, :].unsqueeze(1).to_broadcast([P, TB, D]), ALU.mult).then_inc(n_prod, 1)
                dve.wait_ge(n_prod, b + 1)
                dve.wait_ge(n_shift, b + 1)
                dve.tensor_tensor(slot[:, s, :, :], slot[:, s, :, :], slot[:, 4 + s, :, :], ALU.add).then_inc(y_ready, 1)
                moments(1, 0)(b, s, turn)
            batches(dve, normal(1), residual1, lags=(1, 0))

            sums(2)
            dve.wait_ge(layer_done, 3)

            def stage2(b, s, turn):
                after(dve, d_up, b - 1)
                dve.tensor_copy(slot_w[:, 2 + s, :], acc[:, ds(b * BW, BW)]).then_inc(d_staged, 1)

            def residual2(b, s, turn):
                dve.wait_ge(x_ready, 2 * NB + b - 1)
                dve.wait_ge(d_up, b + 1)
                dve.wait_ge(d_self, b + 1)
                for j in range(TB):
                    i = dve.scalar_tensor_tensor(slot[:, s, j, :], node_ps[s][:, j * P:(j + 1) * P], in_scale[:, 2, ds(b * TB + j, 1)],
                                                 slot[:, 4 + s, j, :], ALU.mult, ALU.add)
                i.then_inc(y_ready, 1)
                moments(2, 0)(b, s, turn)
            batches(dve, stage2, normal(2), residual2, lags=(0, 2, 1))

            sums(3)
            dve.wait_ge(layer_done, 4)
            dve.wait_ge(weights3_in, 5 * 16)
            dve.tensor_tensor(bias_bc, bias_bc, bres_bc, ALU.add).then_inc(w_dve, 1)

            def stage3(b, s, turn):
                dve.wait_ge(r_xt, b + 1)
                after(dve, r_z, b - 1)
                dve.tensor_tensor(r_h_sb[:, s, :], acc[:, ds(b * BW, BW)], pp[0][:, 0:BW], ALU.add).then_inc(r_h, 1)

            def residual3(b, s, turn):
                dve.wait_ge(x_ready, 3 * NB + b - 1)
                dve.wait_ge(r_y, b + 1)
                dve.wait_ge(n_shift, NB + b + 1)
                dve.tensor_tensor(slot_w[:, 2 + s, :], node_ps[s][:, 0:BW], slot_w[:, 5 + s, :], ALU.add).then_inc(y_ready, 1)
                moments(3, 2)(b, s, turn)
            batches(dve, stage3, normal(3), residual3, lags=(0, 2, 1))


INPUTS = ["x", "src", "dst", "edge_weight", "L1_gnn_W_conv", "L1_gnn_b_conv", "L1_gnn_gate_W", "L1_gnn_gate_b",
          "L1_gnn_W1", "L1_gnn_b1", "L1_gnn_W2", "L1_gnn_b2", "L1_gnn_bn_gamma", "L1_gnn_bn_beta",
          "L3_gnn_W1", "L3_gnn_b1", "L3_gnn_W2", "L3_gnn_b2", "L3_gnn_Wres", "L3_gnn_bres"]


def kernel(**inputs):
    import numpy as np
    import concourse.bacc as bacc
    from concourse.bass_utils import run_bass_kernel_spmd

    nc = bacc.Bacc("TRN2", target_bir_lowering=False, num_devices=1)
    arrays, args = {}, []
    for name in INPUTS:
        a = np.ascontiguousarray(inputs[name])
        arrays[f"in_{name}"] = a
        args.append(nc.dram_tensor(f"in_{name}", a.shape, mybir.dt.from_np(a.dtype), kind="ExternalInput").ap())
    out = nc.dram_tensor("out", (N, D), mybir.dt.float32, kind="ExternalOutput").ap()
    program(nc, *args, out)
    result = run_bass_kernel_spmd(nc, [arrays], core_ids=[0])
    return result.results[0]["out"]
```
